# Optimizing a Trainium2 kernel written in Bass

```python
import numpy as np
import jax
import jax.numpy as jnp

def _softmax(x, axis=-1):
    return jax.nn.softmax(x, axis=axis)

def _gelu(x):
    return jax.nn.gelu(x, approximate=True)

def _silu(x):
    return jax.nn.silu(x)

def _sigmoid(x):
    return jax.nn.sigmoid(x)

def _layernorm(x, axis=-1, eps=1e-05):
    m = jnp.mean(x, axis=axis, keepdims=True)
    v = jnp.var(x, axis=axis, keepdims=True)
    return (x - m) / jnp.sqrt(v + eps)

def _scatter_add(tgt, idx, src, axis=0):
    return tgt.at[idx].add(src)

def _segment_sum(src, seg, n):
    return jax.ops.segment_sum(src, seg, n)
kernel_name = 'mk_adj_ffn_d1_adj_r2_6eced2'

def setup_inputs(seed: int=0):
    np.random.seed(seed)
    _w = jnp.asarray

    def _rec_inputs():
        import jax
        import jax.numpy as jnp
        _gk = jax.random.key(seed)
        x = 7.22e-05 + 1 * jax.random.normal(jax.random.fold_in(_gk, 1), (2048, 512), jnp.float32)
        _a = jax.random.bernoulli(jax.random.fold_in(_gk, 2), 0.00390625, (2048, 2048))
        _a = jnp.logical_or(_a, jnp.swapaxes(_a, -1, -2))
        _a = jnp.logical_or(_a, jnp.eye(2048, dtype=bool))
        _af = _a.astype(jnp.float32)
        _d = jnp.maximum(_af.sum(-1), 1.0) ** (-0.5)
        _af = _af * _d[..., :, None] * _d[..., None, :]
        adj = _af
        return (x, adj)
    x, adj = _rec_inputs()

    def _L0_gnn_setup():
        import jax, jax.numpy as jnp
        import numpy as np
        N = 4096
        D = 512

        def adjacent_mat(adj):
            adj = adj + jnp.eye(adj.shape[0], dtype=adj.dtype)
            deg = jnp.sum(adj, axis=1)
            dinv = jnp.where(deg > 0, deg ** (-0.5), 0.0).astype(adj.dtype)
            return dinv[:, None] * adj * dinv[None, :]
        key = jax.random.key(seed)
        k1, k2 = jax.random.split(key)
        x = jax.random.normal(k1, (N, D), dtype=jnp.float32)
        Coefficient2 = 1e-08 * jnp.ones((N, N), dtype=jnp.float32)
        A = jax.random.uniform(k2, (N, N), dtype=jnp.float32)
        return {'x': x, 'Coefficient2': Coefficient2, 'A': A}
    _L0_gnn_all = _L0_gnn_setup()
    _L0_gnn_in = {k: v for k, v in _L0_gnn_all.items() if k in ()}
    del _L0_gnn_all

    def _L0_ffn_setup():
        import jax, jax.numpy as jnp
        import numpy as np
        D_MODEL = 512
        EXPERT_DIM = 1024
        N_EXPERTS = 8
        LN_EPS = 1e-05

        def _bit_quant(W):
            scale = jnp.clip(jnp.mean(jnp.abs(W), axis=-1, keepdims=True), 1e-05, None)
            w_q = jnp.clip(jnp.round(W / scale), -1.0, 1.0) * scale
            return W + jax.lax.stop_gradient(w_q - W)
        key = jax.random.key(seed)
        ks = jax.random.split(key, 7)
        x = jax.random.normal(ks[0], (4, 1024, D_MODEL), dtype=jnp.float32)
        shared_w1 = jax.random.normal(ks[1], (EXPERT_DIM, D_MODEL), dtype=jnp.float32) / np.sqrt(EXPERT_DIM)
        shared_w2 = jax.random.normal(ks[2], (D_MODEL, EXPERT_DIM), dtype=jnp.float32) / np.sqrt(D_MODEL)
        expert_w1 = jax.random.normal(ks[3], (N_EXPERTS, EXPERT_DIM, D_MODEL), dtype=jnp.float32) / np.sqrt(EXPERT_DIM)
        expert_w2 = jax.random.normal(ks[4], (N_EXPERTS, D_MODEL, EXPERT_DIM), dtype=jnp.float32) / np.sqrt(D_MODEL)
        router_w = 0.02 * jax.random.normal(ks[5], (N_EXPERTS, D_MODEL), dtype=jnp.float32)
        ln_gamma = jnp.ones((D_MODEL,), dtype=jnp.float32)
        ln_beta = jnp.zeros((D_MODEL,), dtype=jnp.float32)
        return {'x': x, 'shared_w1': shared_w1, 'shared_w2': shared_w2, 'expert_w1': expert_w1, 'expert_w2': expert_w2, 'router_w': router_w, 'ln_gamma': ln_gamma, 'ln_beta': ln_beta}
    _L0_ffn_all = _L0_ffn_setup()
    _L0_ffn_in = {k: v for k, v in _L0_ffn_all.items() if k in ('shared_w1', 'shared_w2', 'expert_w1', 'expert_w2', 'router_w', 'ln_gamma', 'ln_beta')}
    del _L0_ffn_all
    return {'x': x, 'adj': adj, 'L0_ffn_shared_w1': _L0_ffn_in['shared_w1'], 'L0_ffn_shared_w2': _L0_ffn_in['shared_w2'], 'L0_ffn_expert_w1': _L0_ffn_in['expert_w1'], 'L0_ffn_expert_w2': _L0_ffn_in['expert_w2'], 'L0_ffn_router_w': _L0_ffn_in['router_w'], 'L0_ffn_ln_gamma': _L0_ffn_in['ln_gamma'], 'L0_ffn_ln_beta': _L0_ffn_in['ln_beta']}

def reference(x, adj, L0_ffn_shared_w1, L0_ffn_shared_w2, L0_ffn_expert_w1, L0_ffn_expert_w2, L0_ffn_router_w, L0_ffn_ln_gamma, L0_ffn_ln_beta):
    import jax
    import jax.numpy as jnp

    def _L0_gnn_ref(x, Coefficient2, A):
        import jax, jax.numpy as jnp
        import numpy as np
        N = 4096
        D = 512

        def adjacent_mat(adj):
            adj = adj + jnp.eye(adj.shape[0], dtype=adj.dtype)
            deg = jnp.sum(adj, axis=1)
            dinv = jnp.where(deg > 0, deg ** (-0.5), 0.0).astype(adj.dtype)
            return dinv[:, None] * adj * dinv[None, :]
        A_c = jax.lax.stop_gradient(A)
        adj = adjacent_mat((A_c + A_c.T) * 0.5)
        y = Coefficient2 @ adj
        y = y @ x
        return y

    def _L0_ffn_ref(x, shared_w1, shared_w2, expert_w1, expert_w2, router_w, ln_gamma, ln_beta):
        import jax, jax.numpy as jnp
        import numpy as np
        D_MODEL = 512
        EXPERT_DIM = 1024
        N_EXPERTS = 8
        LN_EPS = 1e-05

        def _bit_quant(W):
            scale = jnp.clip(jnp.mean(jnp.abs(W), axis=-1, keepdims=True), 1e-05, None)
            w_q = jnp.clip(jnp.round(W / scale), -1.0, 1.0) * scale
            return W + jax.lax.stop_gradient(w_q - W)
        mu = jnp.mean(x, axis=-1, keepdims=True)
        var = jnp.mean(jnp.square(x - mu), axis=-1, keepdims=True)
        h = (x - mu) / jnp.sqrt(var + LN_EPS) * ln_gamma + ln_beta
        sw1, sw2 = (_bit_quant(shared_w1), _bit_quant(shared_w2))
        shared_out = jax.nn.silu(jnp.einsum('btd,fd->btf', h, sw1)) @ sw2.T
        probs = jax.nn.softmax(h @ router_w.T, axis=-1)
        top_prob = jnp.max(probs, axis=-1)
        top_idx = jnp.argmax(probs, axis=-1)
        ew1, ew2 = (_bit_quant(expert_w1), _bit_quant(expert_w2))
        h1 = jax.nn.silu(jnp.einsum('btd,efd->ebtf', h, ew1))
        eo = jnp.einsum('ebtf,edf->ebtd', h1, ew2)
        gate = jax.nn.one_hot(top_idx, N_EXPERTS, dtype=h.dtype) * top_prob[..., None]
        routed_out = jnp.einsum('ebtd,bte->btd', eo, gate)
        return shared_out + routed_out
    x = x + _L0_gnn_ref(_layernorm(x, axis=-1), adj, adj)
    x = x + _L0_ffn_ref(_layernorm(x, axis=-1)[None], L0_ffn_shared_w1, L0_ffn_shared_w2, L0_ffn_expert_w1, L0_ffn_expert_w2, L0_ffn_router_w, L0_ffn_ln_gamma, L0_ffn_ln_beta)[0]
    return x

_drawn_inputs = setup_inputs


def setup_inputs(seed=0):
    import zlib

    import numpy as np

    out = dict(_drawn_inputs(seed))
    spreads = {'L0_ffn_ln_gamma': (1.0, 0.2), 'L0_ffn_ln_beta': (0.0, 0.284)}
    factors = {}
    for name, (base, spread) in spreads.items():
        noise = np.random.default_rng([zlib.crc32(name.encode()), seed]).standard_normal(out[name].shape)
        drawn = base * np.exp(spread * noise) if base else spread * noise
        out[name] = jnp.asarray(drawn.astype(out[name].dtype))
    for name, factor in factors.items():
        out[name] = (out[name] * factor).astype(out[name].dtype)
    return out
```

```python
from contextlib import ExitStack

import concourse.bass as bass
from concourse import mybir

ALU = mybir.AluOpType
ACT = mybir.ActivationFunctionType
F32 = mybir.dt.float32
F16 = mybir.dt.float16
BF16 = mybir.dt.bfloat16
I32 = mybir.dt.int32
AX_X = mybir.AxisListType.X
ds = bass.ds

P = 128
N = 2048
D = 512
F = 1024
E = 8
UNITS = E + 1
NT = N // P
DB = D // P
FB = F // P
EPS = 1e-5
QMIN = 1e-5

GROUPS = [(0, 6), (6, 5), (11, 5)]
G0_COLS = GROUPS[0][1] * P
REST = N - G0_COLS
A_SCALE = 256.0
U_SCALE = 16.0
CHUNK = 1024
CHUNKS = UNITS * F * D // (P * CHUNK)
MACROS = 12
STEPS = len(GROUPS) * NT // MACROS
CH = CHUNKS // MACROS
ROUTED_TILES = N // P + E - 1
TILES = NT + ROUTED_TILES
BASE_W = D + 1
PAD = N


def build(nc, x, adj, adj_t, w1, w2, router_t, gamma, beta, out):
    with ExitStack() as ctx:
        def sb(name, shape, dt):
            return ctx.enter_context(nc.sbuf_tensor(name, shape, dt))

        def sem(name):
            return ctx.enter_context(nc.semaphore(name))

        x1_dram = nc.dram_tensor("x1_scratch", [N, D], F32, kind="Internal").ap()
        h_dram = nc.dram_tensor("h_scratch", [N + P, 2 * D], F16, kind="Internal").ap()
        base_dram = nc.dram_tensor("base_scratch", [N + P, BASE_W], F32, kind="Internal").ap()
        s2_dram = nc.dram_tensor("s2_scratch", [UNITS, D], F32, kind="Internal").ap()
        list_dram = nc.dram_tensor("list_scratch", [P * ROUTED_TILES, 1], I32, kind="Internal").ap()

        region = sb("region", [P, 2 * CHUNKS * CHUNK], F16)
        w1t = region[:, 0:CHUNKS * CHUNK]
        w2t = region[:, CHUNKS * CHUNK:2 * CHUNKS * CHUNK]
        o = 0
        s_hi = region[:, o:o + NT * REST]; o += NT * REST
        s_lo = region[:, o:o + NT * REST]; o += NT * REST
        u_hi = region[:, o:o + NT * D]; o += NT * D
        u_lo = region[:, o:o + NT * D]; o += NT * D
        a_in = region[:, o:o + 2 * 2 * 2 * N].bitcast(F32).rearrange("p (b a n) -> p b a n", b=2, a=2)
        late1 = 24 * CHUNK
        xg_r = w2t[:, late1:late1 + 12 * CHUNK].bitcast(F32).rearrange("p (t d) -> p t d", d=D)
        hrow_r = w1t[:, late1:late1 + 2 * 2 * D].rearrange("p (b d) -> p b d", b=2)

        zreg = sb("zreg", [P, 2 * NT * D], F16)
        xhat = zreg[:, :].bitcast(F32).rearrange("p (t d) -> p t d", t=NT)
        z_hi = zreg[:, 0:NT * D].rearrange("p (t d) -> p t d", t=NT)
        z_lo = zreg[:, NT * D:2 * NT * D].rearrange("p (t d) -> p t d", t=NT)
        zf = zreg[:, :].bitcast(F32)
        xg_z = zf[:, 0:5 * D].rearrange("p (t d) -> p t d", d=D)
        hrow_z = zreg[:, 10 * D:14 * D].rearrange("p (b d) -> p b d", b=2)
        s2bc = zf[:, 7 * D:9 * D].rearrange("p (b d) -> p b d", b=2)
        o_t = zf[:, 9 * D:11 * D].rearrange("p (b d) -> p b d", b=2)
        base_t = zf[:, 11 * D:11 * D + 2 * BASE_W].rearrange("p (b d) -> p b d", b=2)

        work = sb("work", [P, 12288], F16)
        HL = G0_COLS
        hl = work[:, 0:4 * HL].rearrange("p (b h n) -> p b h n", b=2, h=2)
        at = work[:, 4 * HL:8 * HL].bitcast(F32).rearrange("p (b n) -> p b n", b=2)
        raw = work[:, 6144:6144 + 4096].bitcast(F32).rearrange("p (b n) -> p b n", b=2)
        tern = work[:, 10240:12288].rearrange("p (b n) -> p b n", b=2)
        pre = work[:, 0:2048].bitcast(F32)
        h1 = work[:, 2048:4096].bitcast(F32)
        h1hl = work[:, 4096:8192].rearrange("p (b h n) -> p b h n", b=2, h=2)
        ht = work[:, 8192:10240].rearrange("p (b n) -> p b n", b=2)
        hrow = work[:, 10240:12288].rearrange("p (b n) -> p b n", b=2)

        gb = sb("gb", [P, 2, D], F32)
        ident = sb("ident", [P, P], F16)
        ident2 = sb("ident2", [P, P], F16)
        tri = sb("tri", [P, P], F16)
        ones = sb("ones", [P, P], F16)
        stats = sb("stats", [P, NT, 6], F32)
        mv = sb("mv", [P, NT, 2], F32)
        tiny = sb("tiny", [P, 8, NT], F32)
        asum = sb("asum", [P, 2, 2], F32)
        rs = sb("rs", [P, 2, 2], F32)
        dv = sb("dv", [P, 2, 12], F32)
        dinvz = sb("dinvz", [P, NT], F32)
        thr = sb("thr", [P, 2, 2, 2], F32)
        s1 = sb("s1", [P, 2 * CHUNKS], F32)
        s2 = sb("s2", [P, CHUNKS], F32)
        rt = sb("rt", [P, DB, E], F32)
        rtr = sb("rtr", [P, DB, E], F32)
        r3 = sb("r3", [P, DB, 3, E], BF16)
        taken = [11 * D + 2 * BASE_W]

        def late(shape, dt=F32):
            n = 1
            for v in shape:
                n *= v
            words = n if dt != F16 else n // 2
            v = zf[:, taken[0]:taken[0] + words]
            taken[0] += words
            v = v.bitcast(dt) if dt != F32 else v
            return v.rearrange("p (a b) -> p a b", a=shape[0]) if len(shape) == 2 else v

        lg = late([NT, E])
        lg2 = late([2, E])
        mx = late([NT])
        ex = late([NT, E])
        se = late([NT])
        gate = late([NT])
        hot = late([NT, E])
        hot16 = late([NT, E], F16)
        seen = late([NT, E])
        cnt = late([NT + 1, E])
        til = late([3, E])
        tili = late([2, E], I32)
        rank = late([NT, E])
        sel = late([NT, E])
        rr = late([3, NT])
        ri = late([4, NT], I32)
        lst = late([ROUTED_TILES], I32)
        zero_row = zf[:, 0:BASE_W]
        tok = sb("tok", [P, NT], I32)
        padl = sb("padl", [P, ROUTED_TILES], I32)
        tn = sb("tn", [1, ROUTED_TILES], F32)
        tcmp = sb("tcmp", [1, ROUTED_TILES], F32)
        tacc = sb("tacc", [1, ROUTED_TILES], F32)
        idx = sb("idx", [P, 6], I32)
        unit = sb("unit", [1, TILES], I32)

        bank = [ctx.enter_context(nc.psum_tensor(f"bank{i}", [P, 512], F32)) for i in range(8)]
        acc = [bank[i][:, :] for i in range(6)]
        pst = [bank[6][:, :].bitcast(F16), bank[7][:, :].bitcast(F16)]
        ps_ht = bank[6][:, :].bitcast(F16)
        ps_h = [[bank[0], bank[1]], [bank[2], bank[3]]]
        ps_y = [bank[4], bank[5]]
        ps_r = bank[7]

        x_in = sem("x_in")
        small_in = sem("small_in")
        a_loaded = [sem("a_loaded0"), sem("a_loaded1")]
        consts = sem("consts")
        const0 = sem("const0")
        tri_ok = sem("tri_ok")
        xh_seq = sem("xh_seq")
        xh_sqrt = sem("xh_sqrt")
        xhat_ok = sem("xhat_ok")
        sum_ok = sem("sum_ok")
        shi_ok = sem("shi_ok")
        slo_ok = sem("slo_ok")
        deg_seq = sem("deg_seq")
        deg_ok = sem("deg_ok")
        deg_root = sem("deg_root")
        u_ok = sem("u_ok")
        p1_step = sem("p1_step")
        z_acc = sem("z_acc")
        zhi_ok = sem("zhi_ok")
        zlo_ok = sem("zlo_ok")
        at_loaded = [sem("at_loaded0"), sem("at_loaded1")]
        athi_ok = sem("athi_ok")
        atlo_ok = sem("atlo_ok")
        p2_step = sem("p2_step")
        raw_loaded = [sem("raw_loaded0"), sem("raw_loaded1")]
        abs_ok = sem("abs_ok")
        w_seq = sem("w_seq")
        tern_ok = sem("tern_ok")
        tr_ok = sem("tr_ok")
        wt_ok = sem("wt_ok")
        xg_in = sem("xg_in")
        x1_ok = sem("x1_ok")
        x1_stored = sem("x1_stored")
        ln_seq = sem("ln_seq")
        ln_sqrt_in = sem("ln_sqrt_in")
        ln_sqrt = sem("ln_sqrt")
        h_ok = sem("h_ok")
        hhi_ok = sem("hhi_ok")
        hlo_ok = sem("hlo_ok")
        h_stored = [sem("h_stored0"), sem("h_stored1")]
        s2_stored = sem("s2_stored")
        pads_stored = sem("pads_stored")
        hrow_in = [sem("hrow_in0"), sem("hrow_in1")]
        s2_in = [sem("s2_in0"), sem("s2_in1")]
        base_in = [sem("base_in0"), sem("base_in1")]
        hrow_got = [sem("hrow_got0"), sem("hrow_got1")]
        base_got = [sem("base_got0"), sem("base_got1")]
        out_stored = [sem("out_stored0"), sem("out_stored1")]
        tr2_ok = sem("tr2_ok")
        ht_ok = sem("ht_ok")
        m1_ok = sem("m1_ok")
        pre_ok = sem("pre_ok")
        h1_ok = sem("h1_ok")
        h1hi_ok = sem("h1hi_ok")
        h1lo_ok = sem("h1lo_ok")
        m2_ok = sem("m2_ok")
        y_seq = sem("y_seq")
        y_ok = sem("y_ok")
        y_stored = [sem("y_stored0"), sem("y_stored1")]
        r_ok = sem("r_ok")
        l_seq = sem("l_seq")
        l_ok = sem("l_ok")
        e_ok = sem("e_ok")
        r3_ok = sem("r3_ok")
        hot_ok = sem("hot_ok")
        cnt_ok = sem("cnt_ok")
        rt_seq = sem("rt_seq")
        slots_ok = sem("slots_ok")
        unit_ok = sem("unit_ok")
        scat = sem("scat")
        zero_ok = sem("zero_ok")
        pool_waits = sem("pool_waits")
        idx_ok = [sem("idx_ok_h"), sem("idx_ok_base"), sem("idx_ok_out")]
        gate_ok = sem("gate_ok")
        gate_stored = sem("gate_stored")
        list_in = sem("list_in")

        adj_j = adj.rearrange("(j p) n -> j p n", p=P)
        adjt_j = adj_t.rearrange("(j p) n -> j p n", p=P)
        x_t = x.rearrange("(t p) d -> p t d", p=P)
        x1_t = x1_dram.rearrange("(t p) d -> p t d", p=P)
        w1_c = w1.rearrange("u (c b p) d -> (u c) p b d", b=2, p=P)
        w2_c = w2.rearrange("u (c p) f -> (u c) p f", p=P)

        DEG = 9
        WOPS1, WOPS2 = 5, 3
        WOPS = CH * (WOPS1 + WOPS2)

        def slot_count(n, b):
            return (n - b) * 8

        def group_x(g):
            first, count = GROUPS[g]
            if g < 2:
                return xg_r[:, first:first + count, :]
            return xg_z[:, 0:count, :]

        def group_hrow(g):
            return hrow_r if g < 2 else hrow_z

        def ln_roots_and_h(act, g):
            t0, count = GROUPS[g]
            act.wait_ge(x1_ok, t0 + count)
            act.dma_start(x1_t[:, t0:t0 + count, :], group_x(g)).then_inc(x1_stored, 16)
            for r in range(2):
                act.wait_ge(ln_sqrt_in, 2 * g + r + 1)
                nc.scalar.activation(tiny[:, 1, 0:count], tiny[:, 0, 0:count], ACT.Sqrt).then_inc(ln_sqrt, 1)
            hr = group_hrow(g)
            act.wait_ge(h_ok, g + 1)
            for k in range(count):
                t = t0 + k
                if t >= 2:
                    act.wait_ge(h_stored[t % 2], 16 * (t // 2))
                nc.scalar.activation(hr[:, t % 2, 0:D], group_x(g)[:, k, :], ACT.Copy).then_inc(hhi_ok, 1)
                act.wait_ge(hhi_ok, t + 1)
                act.wait_ge(hlo_ok, t + 1)
                act.dma_start(h_dram[t * P:(t + 1) * P, :], hr[:, t % 2, :]).then_inc(h_stored[t % 2], 16)

        block = ctx.enter_context(nc.Block())

        @block.sync
        def _(sp):
            sp.dma_start(xhat[:, :, :], x_t).then_inc(x_in, 16)
            sp.dma_start(gb[:, 0, :], gamma.rearrange("(a d) -> a d", a=1).to_broadcast([P, D])).then_inc(small_in, 16)
            sp.dma_start(gb[:, 1, :], beta.rearrange("(a d) -> a d", a=1).to_broadcast([P, D])).then_inc(small_in, 16)
            sp.dma_start(rt[:, :, :], router_t.rearrange("(b p) e -> p b e", p=P)).then_inc(small_in, 16)

            def load_a(j, b):
                sp.dma_start(a_in[:, b, 0, :], adj_j[ds(j, 1), :, :].rearrange("a p n -> (a p) n")).then_inc(a_loaded[b], 16)
                sp.dma_start(a_in[:, b, 1, :], adjt_j[ds(j, 1), :, :].rearrange("a p n -> (a p) n")).then_inc(a_loaded[b], 16)

            for b in range(2):
                load_a(b, b)
            with sp.Fori(1, NT // 2) as i:
                for b in range(2):
                    sp.wait_ge(slo_ok, 2 * i + b - 1)
                    load_a(2 * i + b, b)

            def load_at(g, m, first):
                c0, nc_ = GROUPS[g][0] * P, GROUPS[g][1] * P
                for s in range(STEPS):
                    if not (first and g == 0 and s < 2):
                        sp.wait_ge(atlo_ok, STEPS * m + s - 1)
                    j = STEPS * (m - g * NT // STEPS) + s
                    sp.dma_start(at[:, s % 2, 0:nc_],
                                 adjt_j[ds(j, 1), :, c0:c0 + nc_].rearrange("a p n -> (a p) n")
                                 ).then_inc(at_loaded[s % 2], 16)

            for g, (t0, count) in enumerate(GROUPS):
                m0 = g * NT // STEPS
                if g == 0:
                    sp.wait_ge(z_acc, 3)
                    sp.dma_start(xg_r[:, 0:11, :], x_t[:, 0:11, :]).then_inc(xg_in, 16)
                load_at(g, m0, True)
                with sp.Fori(m0 + 1, m0 + NT // STEPS) as m:
                    load_at(g, m, False)
            sp.wait_ge(p2_step, len(GROUPS) * NT)
            t0, count = GROUPS[2]
            sp.dma_start(group_x(2), x_t[:, t0:t0 + count, :]).then_inc(xg_in, 16)

            sp.wait_ge(w_seq, MACROS * WOPS)
            sp.dma_start(s2_dram.rearrange("u (c p) -> p (u c)", p=P), s2[:, :],
                         allow_slow_non_contiguous=True).then_inc(s2_stored, 16)
            sp.wait_ge(s2_stored, 16)
            sp.wait_ge(x1_stored, 16 * 3)
            for b in range(2):
                sp.wait_ge(h_stored[b], 16 * NT // 2)

            def load_shared(n, b):
                sp.dma_start(hrow[:, b, :], h_dram[ds(n * P, P), :]).then_inc(hrow_in[b], 16)

            def load_base(n, b):
                sp.dma_start(s2bc[:, b, :], s2_dram[0:1, :].to_broadcast([P, D])).then_inc(s2_in[b], 16)
                sp.dma_start(base_t[:, b, 0:D], x1_dram[ds(n * P, P), :]).then_inc(base_in[b], 16)

            sp.wait_ge(tr_ok, 2 * CHUNKS)
            sp.wait_ge(h_ok, 3)
            for b in range(2):
                load_shared(b, b)
                load_base(b, b)
            with sp.Fori(1, NT // 2) as i:
                for b in range(2):
                    sp.wait_ge(tr2_ok, 2 * i + b - 1)
                    load_shared(2 * i + b, b)
                    sp.wait_ge(y_stored[b], 16 * i)
                    load_base(2 * i + b, b)

            sp.wait_ge(scat, 16 * NT)
            sp.dma_start(lst[:, :], list_dram.rearrange("(p n) a -> p (n a)", p=P)).then_inc(list_in, 16)

            sp.wait_ge(unit_ok, 1)
            with sp.Fori(0, ROUTED_TILES // 2) as i:
                for b in range(2):
                    u = sp.value_load(unit[0:1, ds(NT + 2 * i + b, 1)], min_val=0, max_val=UNITS - 1)
                    sp.wait_ge(y_ok, NT - 1 + 2 * i + b)
                    sp.dma_start(s2bc[:, b, :], s2_dram[ds(u, 1), :].to_broadcast([P, D])).then_inc(s2_in[b], 16)
            u = sp.value_load(unit[0:1, TILES - 1:TILES], min_val=0, max_val=UNITS - 1)
            sp.wait_ge(y_ok, TILES - 2)
            sp.dma_start(s2bc[:, 0, :], s2_dram[ds(u, 1), :].to_broadcast([P, D])).then_inc(s2_in[0], 16)

        @block.gpsimd
        def _(pool):
            def pool_wait(s, value):
                pool.wait_ge(s, value)
                pool.sem_inc(pool_waits, 1)

            nc.gpsimd.memset(ident[:], 0.0).then_inc(const0, 1)
            nc.gpsimd.memset(ident2[:], 0.0).then_inc(const0, 1)
            nc.gpsimd.memset(ones[:], 1.0).then_inc(const0, 1)
            pool.wait_ge(const0, 3)
            nc.gpsimd.affine_select(out=ident[:], in_=ident[:], compare_op=ALU.not_equal, fill=1.0, base=0,
                                    pattern=[[-1, P]], channel_multiplier=1).then_inc(consts, 1)
            nc.gpsimd.affine_select(out=ident2[:], in_=ident2[:], compare_op=ALU.not_equal, fill=2.0 * A_SCALE,
                                    base=0, pattern=[[-1, P]], channel_multiplier=1).then_inc(consts, 1)
            nc.gpsimd.affine_select(out=tri[:], in_=ones[:], compare_op=ALU.is_gt, fill=0.0, base=0,
                                    pattern=[[1, P]], channel_multiplier=-1).then_inc(consts, 1)
            nc.gpsimd.iota(tok[:, :], pattern=[[P, NT]], base=0, channel_multiplier=1).then_inc(consts, 1)
            nc.gpsimd.iota(padl[:, :], pattern=[[0, ROUTED_TILES]], base=PAD, channel_multiplier=1).then_inc(consts, 1)
            nc.gpsimd.iota(tn[:, :], pattern=[[1, ROUTED_TILES]], base=0, channel_multiplier=0,
                           allow_small_or_imprecise_dtypes=True).then_inc(consts, 1)
            nc.gpsimd.memset(unit[:, 0:NT], 0).then_inc(consts, 1)
            pool.wait_ge(consts, 7)
            pool.dma_start(list_dram.rearrange("(p n) a -> p (n a)", p=P), padl[:, :]).then_inc(pads_stored, 16)

            def load_w(m, first):
                for s in range(2 * CH):
                    b = s % 2
                    if not (first and s < 2):
                        pool_wait(tern_ok, 2 * CH * m + s - 1)
                    if s < CH:
                        pool.dma_start(raw[:, b, :].rearrange("p (a d) -> p a d", a=2),
                                       w1_c[ds(CH * m + s, 1), :, :, :].rearrange("c p b d -> (c p) b d")
                                       ).then_inc(raw_loaded[b], 16)
                    else:
                        pool.dma_start(raw[:, b, :],
                                       w2_c[ds(CH * m + s - CH, 1), :, :].rearrange("c p f -> (c p) f")
                                       ).then_inc(raw_loaded[b], 16)

            load_w(0, True)
            with pool.Fori(1, MACROS) as m:
                load_w(m, False)

            for b in range(2):
                pool.wait_ge(h_stored[b], 16 * NT // 2)
            pool.wait_ge(hlo_ok, NT)
            nc.gpsimd.memset(zero_row, 0.0).then_inc(zero_ok, 1)
            pool.wait_ge(zero_ok, 1)
            pool.dma_start(h_dram[N:N + P, :], zero_row[:, 0:D].bitcast(F16)).then_inc(pads_stored, 16)
            pool.dma_start(base_dram[N:N + P, :], zero_row).then_inc(pads_stored, 16)

            pool.wait_ge(slots_ok, 1)
            pool.wait_ge(pads_stored, 48)
            for t in range(NT):
                pool.indirect_dma_start(
                    out=list_dram, out_offset=bass.IndirectOffsetOnAxis(ap=ri[:, 3, t:t + 1], axis=0),
                    in_=tok[:, t:t + 1], in_offset=None).then_inc(scat, 16)
            pool.wait_ge(list_in, 16)
            pool.wait_ge(gate_stored, 16)
            for b in range(2):
                pool.wait_ge(y_stored[b], 16 * NT // 2)

            def tokens(n, b, use):
                at_ = idx[:, 2 * use + b:2 * use + b + 1]
                nc.gpsimd.tensor_copy(at_, lst[:, ds(n - NT, 1)]).then_inc(idx_ok[use], 1)
                pool_wait(idx_ok[use], n - NT + 1)
                return bass.IndirectOffsetOnAxis(ap=at_, axis=0)

            def gather_h(n, b):
                pool.indirect_dma_start(out=hrow[:, b, :], out_offset=None, in_=h_dram,
                                        in_offset=tokens(n, b, 0)).then_inc(hrow_got[b], 16)

            def gather_base(n, b):
                pool.indirect_dma_start(out=base_t[:, b, :], out_offset=None, in_=base_dram,
                                        in_offset=tokens(n, b, 1)).then_inc(base_got[b], 16)

            def scatter(n, b):
                pool_wait(y_ok, n + 1)
                pool.indirect_dma_start(out=out, out_offset=tokens(n, b, 2), in_=o_t[:, b, :], in_offset=None,
                                        bounds_check=N - 1, oob_is_err=False).then_inc(out_stored[b], 16)

            def turn(n, b):
                pool_wait(tr2_ok, n + 1)
                gather_h(n + 2, b)
                scatter(n, b)
                gather_base(n + 2, b)

            for b in range(2):
                gather_h(NT + b, b)
                gather_base(NT + b, b)
            with pool.Fori(0, (ROUTED_TILES - 3) // 2) as i:
                for b in range(2):
                    turn(NT + 2 * i + b, b)
            turn(TILES - 3, 0)
            scatter(TILES - 2, 1)
            scatter(TILES - 1, 0)
            for b in range(2):
                pool.wait_ge(out_stored[b], 16 * ((ROUTED_TILES + 1 - b) // 2))

        @block.scalar
        def _(act):
            act.wait_ge(xh_seq, NT * 2 + 1)
            nc.scalar.activation(tiny[:, 1, :], tiny[:, 0, :], ACT.Sqrt).then_inc(xh_sqrt, 1)

            def split_s(j, b, first):
                act.wait_ge(sum_ok, j + 1)
                if not first:
                    act.wait_ge(p1_step, j - 1)
                nc.scalar.activation(hl[:, b, 0, :], a_in[:, b, 0, 0:G0_COLS], ACT.Copy, scale=A_SCALE,
                                     accum_out=rs[:, b, 0:1]).then_inc(shi_ok, 1)
                nc.scalar.activation(s_hi[:, ds(j * REST, REST)], a_in[:, b, 0, G0_COLS:N], ACT.Copy, scale=A_SCALE,
                                     accum_out=rs[:, b, 1:2]).then_inc(shi_ok, 1)
                act.wait_ge(deg_ok, j + 1)
                nc.scalar.activation(dv[:, b, 2:3], dv[:, b, 1:2], ACT.Sqrt).then_inc(deg_root, 1)

            for b in range(2):
                split_s(b, b, True)
            with act.Fori(1, NT // 2) as i:
                for b in range(2):
                    split_s(2 * i + b, b, False)

            for g, (t0, count) in enumerate(GROUPS):
                act.wait_ge(z_acc, g + 1)
                act.wait_ge(deg_seq, NT * DEG)
                for k in range(count):
                    nc.scalar.activation(z_hi[:, t0 + k, :], acc[k], ACT.Copy,
                                         scale=dinvz[:, t0 + k:t0 + k + 1]).then_inc(zhi_ok, 1)

            def macro(g, m, first):
                nc_ = GROUPS[g][1] * P
                for s in range(2 * CH):
                    b = s % 2
                    q = 2 * CH * m + s
                    if s < STEPS:
                        J = STEPS * m + s
                        act.wait_ge(at_loaded[b], 16 * (2 * m + s // 2 + 1))
                        if not (first and g == 0 and s < 2):
                            act.wait_ge(p2_step, J - 1)
                        nc.scalar.activation(hl[:, b, 0, 0:nc_], at[:, b, 0:nc_], ACT.Copy,
                                             scale=A_SCALE).then_inc(athi_ok, 1)
                    act.wait_ge(raw_loaded[b], 16 * (CH * m + s // 2 + 1))
                    if not (first and g == 0 and s < 2):
                        act.wait_ge(tr_ok, q - 1)
                    if s < CH:
                        for a in range(2):
                            nc.scalar.activation(tern[:, b, a * D:(a + 1) * D], raw[:, b, a * D:(a + 1) * D], ACT.Abs,
                                                 accum_out=asum[:, b, a:a + 1]).then_inc(abs_ok, 1)
                    else:
                        nc.scalar.activation(tern[:, b, :], raw[:, b, :], ACT.Abs,
                                             accum_out=asum[:, b, 0:1]).then_inc(abs_ok, 2)
                    if not (first and g == 0 and s == 0):
                        store_w(m if s > 0 else m - 1, (s - 1) % (2 * CH))

            def store_w(m, s):
                act.wait_ge(tr_ok, 2 * CH * m + s + 1)
                dst = w1t if s < CH else w2t
                c = CH * m + s % CH
                nc.scalar.activation(dst[:, ds(c * CHUNK, CHUNK)], pst[s % 2], ACT.Copy).then_inc(wt_ok, 1)

            for g in range(3):
                m0 = g * NT // STEPS
                if g == 2:
                    act.wait_ge(hlo_ok, GROUPS[2][0])
                    for b in range(2):
                        act.wait_ge(h_stored[b], 16 * ((GROUPS[2][0] + 1 - b) // 2))
                macro(g, m0, True)
                with act.Fori(m0 + 1, m0 + NT // STEPS) as m:
                    macro(g, m, False)
                if g < 2:
                    ln_roots_and_h(act, g)
            store_w(MACROS - 1, 2 * CH - 1)
            ln_roots_and_h(act, 2)

            def tile(n, b, shared, lead):
                act.wait_ge(tr2_ok, n + 1)
                if lead >= 2:
                    act.wait_ge(m1_ok, n - 1)
                nc.scalar.activation(ht[:, b, :], ps_ht, ACT.Copy).then_inc(ht_ok, 1)
                for half in range(2):
                    act.wait_ge(pre_ok, 2 * n + half + 1)
                    if lead >= 1:
                        act.wait_ge(h1lo_ok, 2 * n + half - 1)
                    cols = slice(half * 512, half * 512 + 512)
                    nc.scalar.activation(h1[:, cols], pre[:, cols], ACT.Silu).then_inc(h1_ok, 1)
                    if lead >= 2:
                        act.wait_ge(m2_ok, n - 1)
                    act.wait_ge(h1_ok, 2 * n + half + 1)
                    nc.scalar.activation(h1hl[:, b, 0, cols], h1[:, cols], ACT.Copy, scale=U_SCALE).then_inc(h1hi_ok, 1)

            def shared_store(n, b):
                act.wait_ge(y_ok, n + 1)
                act.dma_start(base_dram[ds(n * P, P), 0:D], base_t[:, b, 0:D]).then_inc(y_stored[b], 16)

            tile(0, 0, True, 0)
            tile(1, 1, True, 1)
            shared_store(0, 0)
            with act.Fori(1, NT // 2) as i:
                for b in range(2):
                    tile(2 * i + b, b, True, 2)
                    shared_store(2 * i + b - 1, 1 - b)
            shared_store(NT - 1, 1)
            act.wait_ge(l_ok, NT + 1)
            nc.scalar.activation(ex[:, :, :], lg[:, :, :], ACT.Exp).then_inc(e_ok, 1)
            act.wait_ge(gate_ok, 1)
            act.dma_start(base_dram[0:N, D:D + 1].rearrange("(t p) a -> p (t a)", p=P), gate,
                          allow_slow_non_contiguous=True).then_inc(gate_stored, 16)
            with act.Fori(NT // 2, TILES // 2) as i:
                for b in range(2):
                    tile(2 * i + b, b, False, 2)
            tile(TILES - 1, (TILES - 1) % 2, False, 2)

        @block.vector
        def _(dve):
            def chained(ins, s, value):
                ins.then_inc(s, 1)
                dve.wait_ge(s, value)

            def rsqrt_finish(root, var, out_, tmp, step):
                step(nc.vector.reciprocal(out_, root))
                step(nc.vector.tensor_tensor(tmp, out_, out_, ALU.mult))
                step(nc.vector.tensor_tensor(tmp, tmp, var, ALU.mult))
                step(nc.vector.tensor_scalar(tmp, tmp, -0.5, 1.5, ALU.mult, ALU.add))
                step(nc.vector.tensor_tensor(out_, out_, tmp, ALU.mult))

            count_xh = [0]

            def xh(ins):
                count_xh[0] += 1
                chained(ins, xh_seq, count_xh[0])

            dve.wait_ge(x_in, 16)
            for t in range(NT):
                count_xh[0] += 1
                nc.vector.bn_stats(stats[:, t, :], xhat[:, t, :]).then_inc(xh_seq, 1)
            dve.wait_ge(xh_seq, NT)
            for t in range(NT):
                count_xh[0] += 1
                nc.vector.bn_aggr(mv[:, t, :], stats[:, t, :]).then_inc(xh_seq, 1)
            dve.wait_ge(xh_seq, 2 * NT)
            xh(nc.vector.tensor_scalar(tiny[:, 0, :], mv[:, :, 1], EPS, None, ALU.add))
            dve.wait_ge(xh_sqrt, 1)
            rsqrt_finish(tiny[:, 1, :], tiny[:, 0, :], tiny[:, 2, :], tiny[:, 3, :], xh)
            for t in range(NT):
                nc.vector.tensor_scalar(xhat[:, t, :], xhat[:, t, :], mv[:, t, 0:1], tiny[:, 2, t:t + 1],
                                        ALU.subtract, ALU.mult).then_inc(xhat_ok, 1)
            dve.wait_ge(xhat_ok, NT)

            dve.wait_ge(small_in, 48)
            xh(nc.vector.tensor_copy(r3[:, :, 0, :], rt[:, :, :]))
            xh(nc.vector.tensor_tensor(rtr[:, :, :], rt[:, :, :], r3[:, :, 0, :], ALU.subtract))
            xh(nc.vector.tensor_copy(r3[:, :, 1, :], rtr[:, :, :]))
            xh(nc.vector.tensor_tensor(rtr[:, :, :], rtr[:, :, :], r3[:, :, 1, :], ALU.subtract))
            nc.vector.tensor_copy(r3[:, :, 2, :], rtr[:, :, :]).then_inc(r3_ok, 1)

            def block_j(j, b, first):
                dve.wait_ge(a_loaded[b], 2 * slot_count(j, b) + 32)
                nc.vector.tensor_tensor(a_in[:, b, 0, :], a_in[:, b, 0, :], a_in[:, b, 1, :], ALU.add).then_inc(sum_ok, 1)
                dve.wait_ge(shi_ok, 2 * j + 1)
                nc.vector.scalar_tensor_tensor(out=hl[:, b, 1, :], in0=a_in[:, b, 0, 0:G0_COLS], scalar=A_SCALE,
                                               in1=hl[:, b, 0, :], op0=ALU.mult, op1=ALU.subtract)
                dve.wait_ge(shi_ok, 2 * j + 2)
                v = [dv[:, b, k:k + 1] for k in range(12)]
                n = [0]

                def step(ins):
                    n[0] += 1
                    chained(ins, deg_seq, DEG * j + n[0])

                step(nc.vector.tensor_tensor(v[3], rs[:, b, 0:1], rs[:, b, 1:2], ALU.add))
                step(nc.vector.tensor_scalar(v[0], v[3], 0.5 / A_SCALE, 1.0, ALU.mult, ALU.add))
                nc.vector.tensor_scalar(v[1], v[0], 1e-30, None, ALU.max).then_inc(deg_ok, 1)
                nc.vector.scalar_tensor_tensor(out=s_lo[:, ds(j * REST, REST)], in0=a_in[:, b, 0, G0_COLS:N],
                                               scalar=A_SCALE, in1=s_hi[:, ds(j * REST, REST)], op0=ALU.mult,
                                               op1=ALU.subtract).then_inc(slo_ok, 1)
                dve.wait_ge(deg_root, j + 1)
                dve.wait_ge(deg_ok, j + 1)
                step(nc.vector.reciprocal(v[4], v[2]))
                step(nc.vector.scalar_tensor_tensor(out=v[5], in0=v[4], scalar=v[4], in1=v[1], op0=ALU.mult, op1=ALU.mult))
                step(nc.vector.tensor_scalar(v[5], v[5], -0.5, 1.5, ALU.mult, ALU.add))
                step(nc.vector.tensor_tensor(v[6], v[4], v[5], ALU.mult))
                step(nc.vector.scalar_tensor_tensor(out=v[7], in0=v[0], scalar=0.0, in1=v[6], op0=ALU.is_gt, op1=ALU.mult))
                step(nc.vector.tensor_scalar(v[8], v[7], U_SCALE, None, ALU.mult))
                nc.vector.tensor_scalar(dinvz[:, ds(j, 1)], v[7], 0.5 / A_SCALE, None, ALU.mult).then_inc(deg_seq, 1)
                xj = xhat[:, ds(j, 1), :].rearrange("p a d -> p (a d)")
                chained(nc.vector.tensor_scalar(u_hi[:, ds(j * D, D)], xj, v[8], None, ALU.mult), u_ok, 2 * j + 1)
                nc.vector.scalar_tensor_tensor(out=u_lo[:, ds(j * D, D)], in0=xj, scalar=v[8],
                                               in1=u_hi[:, ds(j * D, D)], op0=ALU.mult,
                                               op1=ALU.subtract).then_inc(u_ok, 1)

            for b in range(2):
                block_j(b, b, True)
            with dve.Fori(1, NT // 2) as i:
                for b in range(2):
                    block_j(2 * i + b, b, False)

            for g, (t0, count) in enumerate(GROUPS):
                dve.wait_ge(z_acc, g + 1)
                dve.wait_ge(deg_seq, NT * DEG)
                for k in range(count):
                    dve.wait_ge(zhi_ok, t0 + k + 1)
                    nc.vector.scalar_tensor_tensor(out=z_lo[:, t0 + k, :], in0=acc[k], scalar=dinvz[:, t0 + k:t0 + k + 1],
                                                   in1=z_hi[:, t0 + k, :], op0=ALU.mult,
                                                   op1=ALU.subtract).then_inc(zlo_ok, 1)

            def macro(g, m, first):
                nc_ = GROUPS[g][1] * P
                n = [0]

                def step(ins):
                    n[0] += 1
                    chained(ins, w_seq, WOPS * m + n[0])

                for s in range(2 * CH):
                    b = s % 2
                    if s < STEPS:
                        dve.wait_ge(athi_ok, STEPS * m + s + 1)
                        nc.vector.scalar_tensor_tensor(out=hl[:, b, 1, 0:nc_], in0=at[:, b, 0:nc_], scalar=A_SCALE,
                                                       in1=hl[:, b, 0, 0:nc_], op0=ALU.mult,
                                                       op1=ALU.subtract).then_inc(atlo_ok, 1)
                    dve.wait_ge(abs_ok, 2 * (2 * CH * m + s + 1))
                    k, width = (2, D) if s < CH else (1, F)
                    c = CH * m + s % CH
                    scale = s1[:, ds(2 * c, 2)] if s < CH else s2[:, ds(c, 1)]
                    step(nc.vector.tensor_scalar(scale, asum[:, b, 0:k], 1.0 / width, QMIN, ALU.mult, ALU.max))
                    nc.vector.tensor_scalar(thr[:, b, 0, 0:k], scale, 0.5, None, ALU.mult)
                    step(nc.vector.tensor_scalar(thr[:, b, 1, 0:k], scale, -0.5, None, ALU.mult))
                    for a in range(k):
                        cols = slice(a * width, (a + 1) * width)
                        step(nc.vector.tensor_scalar(tern[:, b, cols], raw[:, b, cols], thr[:, b, 1, a:a + 1], None, ALU.is_lt))
                    for a in range(k):
                        cols = slice(a * width, (a + 1) * width)
                        ins = nc.vector.scalar_tensor_tensor(out=tern[:, b, cols], in0=raw[:, b, cols],
                                                             scalar=thr[:, b, 0, a:a + 1], in1=tern[:, b, cols],
                                                             op0=ALU.is_gt, op1=ALU.subtract)
                        if a == k - 1:
                            ins.then_inc(tern_ok, 1)
                        else:
                            step(ins)

            ln_n = [0]

            def ln(ins):
                ln_n[0] += 1
                chained(ins, ln_seq, ln_n[0])

            def norms(g):
                t0, count = GROUPS[g]
                xg = group_x(g)
                dve.wait_ge(xg_in, 16 if g < 2 else 32)
                dve.wait_ge(p2_step, NT * (g + 1))
                for k in range(count):
                    nc.vector.scalar_tensor_tensor(out=xg[:, k, :], in0=acc[k], scalar=1.0 / (A_SCALE * U_SCALE),
                                                   in1=xg[:, k, :], op0=ALU.mult, op1=ALU.add).then_inc(x1_ok, 1)
                dve.wait_ge(x1_ok, t0 + count)
                for r in range(2):
                    for k in range(count):
                        ln(nc.vector.bn_stats(stats[:, k, :], xg[:, k, :]))
                        ln(nc.vector.bn_aggr(mv[:, k, :], stats[:, k, :]))
                    nc.vector.tensor_scalar(tiny[:, 0, 0:count], mv[:, 0:count, 1], EPS, None, ALU.add).then_inc(ln_sqrt_in, 1)
                    dve.wait_ge(ln_sqrt, 2 * g + r + 1)
                    rsqrt_finish(tiny[:, 1, 0:count], tiny[:, 0, 0:count], tiny[:, 2, 0:count], tiny[:, 3, 0:count], ln)
                    if r == 0:
                        dve.wait_ge(x1_stored, 16 * (g + 1))
                    for k in range(count):
                        ins = nc.vector.tensor_scalar(xg[:, k, :], xg[:, k, :], mv[:, k, 0:1], tiny[:, 2, k:k + 1],
                                                      ALU.subtract, ALU.mult)
                        ln(ins)
                for k in range(count):
                    ln(nc.vector.tensor_tensor(xg[:, k, :], xg[:, k, :], gb[:, 0, :], ALU.mult))
                for k in range(count):
                    ins = nc.vector.tensor_tensor(xg[:, k, :], xg[:, k, :], gb[:, 1, :], ALU.add)
                    if k == count - 1:
                        ins.then_inc(h_ok, 1)
                    else:
                        ln(ins)
                hr = group_hrow(g)
                dve.wait_ge(h_ok, g + 1)
                for k in range(count):
                    t = t0 + k
                    dve.wait_ge(hhi_ok, t + 1)
                    nc.vector.tensor_tensor(hr[:, t % 2, D:2 * D], xg[:, k, :], hr[:, t % 2, 0:D],
                                            ALU.subtract).then_inc(hlo_ok, 1)

            for g in range(3):
                m0 = g * NT // STEPS
                macro(g, m0, True)
                with dve.Fori(m0 + 1, m0 + NT // STEPS) as m:
                    macro(g, m, False)
                norms(g)

            LO = 4

            def tile(n, b, shared, lead, u):
                for half in range(2):
                    dve.wait_ge(m1_ok, n + 1)
                    if lead >= 1:
                        dve.wait_ge(h1_ok, 2 * n + half - 1)
                    nc.vector.tensor_tensor(
                        pre[:, half * 512:(half + 1) * 512].rearrange("p (f t) -> p f t", f=4),
                        ps_h[b][half][:, :].rearrange("p (f t) -> p f t", f=4),
                        s1[:, ds(u * FB + half * 4, 4)].rearrange("p (f a) -> p f a", a=1).to_broadcast([P, 4, P]),
                        ALU.mult).then_inc(pre_ok, 1)
                if shared:
                    route(n, b)
                for half in range(2):
                    dve.wait_ge(h1hi_ok, 2 * n + half + 1)
                    cols = slice(half * 512, half * 512 + 512)
                    nc.vector.scalar_tensor_tensor(out=h1hl[:, b, 1, cols], in0=h1[:, cols], scalar=U_SCALE,
                                                   in1=h1hl[:, b, 0, cols], op0=ALU.mult,
                                                   op1=ALU.subtract).then_inc(h1lo_ok, 1)

            def route(n, b):
                k = [0]

                def step(ins):
                    k[0] += 1
                    chained(ins, l_seq, LO * n + k[0])

                row = lambda v: v[:, ds(n, 1), :].rearrange("p a e -> p (a e)")
                dve.wait_ge(r_ok, n + 1)
                step(nc.vector.tensor_copy(lg2[:, 0, :], ps_r[:, 2 * E:3 * E]))
                step(nc.vector.tensor_tensor(lg2[:, 1, :], ps_r[:, E:2 * E], lg2[:, 0, :], ALU.add))
                step(nc.vector.tensor_tensor(row(lg), ps_r[:, 0:E], lg2[:, 1, :], ALU.add))
                step(nc.vector.tensor_reduce(mx[:, ds(n, 1)], row(lg), AX_X, ALU.max))
                nc.vector.tensor_scalar(row(hot), row(lg), mx[:, ds(n, 1)], None, ALU.is_equal).then_inc(l_ok, 1)

            def output(n, b, shared, lead):
                dve.wait_ge(m2_ok, n + 1)
                dve.wait_ge(s2_in[b], slot_count(n, b) + 16)
                if shared:
                    dve.wait_ge(base_in[b], slot_count(n, b) + 16)
                else:
                    dve.wait_ge(base_got[b], slot_count(n - NT, b) + 16)
                    if lead >= 2:
                        dve.wait_ge(out_stored[b], slot_count(n - NT, b))
                chained(nc.vector.scalar_tensor_tensor(out=s2bc[:, b, :], in0=ps_y[b][:, :], scalar=1.0 / U_SCALE,
                                                       in1=s2bc[:, b, :], op0=ALU.mult, op1=ALU.mult), y_seq, n + 1)
                if shared:
                    nc.vector.tensor_tensor(base_t[:, b, 0:D], base_t[:, b, 0:D], s2bc[:, b, :],
                                            ALU.add).then_inc(y_ok, 1)
                else:
                    nc.vector.scalar_tensor_tensor(out=o_t[:, b, :], in0=s2bc[:, b, :], scalar=base_t[:, b, D:D + 1],
                                                   in1=base_t[:, b, 0:D], op0=ALU.mult, op1=ALU.add).then_inc(y_ok, 1)

            tile(0, 0, True, 0, 0)
            tile(1, 1, True, 1, 0)
            output(0, 0, True, 0)
            with dve.Fori(1, NT // 2) as i:
                tile(2 * i, 0, True, 2, 0)
                output(2 * i - 1, 1, True, 2)
                tile(2 * i + 1, 1, True, 2, 0)
                output(2 * i, 0, True, 2)

            q = [0]

            def rs_(ins):
                q[0] += 1
                chained(ins, rt_seq, q[0])

            dve.wait_ge(l_ok, NT)
            rs_(nc.vector.memset(rank[:, :, 0:1], 0.0))
            for e in range(1, E):
                rs_(nc.vector.tensor_tensor(rank[:, :, e:e + 1], rank[:, :, e - 1:e], hot[:, :, e - 1:e], ALU.max))
            rs_(nc.vector.tensor_tensor(seen[:, :, :], hot[:, :, :], rank[:, :, :], ALU.is_gt))
            nc.vector.tensor_copy(hot16[:, :, :], seen[:, :, :]).then_inc(hot_ok, 1)
            nc.vector.tensor_tensor(lg[:, :, :], lg[:, :, :],
                                    mx.rearrange("p (t a) -> p t a", a=1).to_broadcast([P, NT, E]),
                                    ALU.subtract).then_inc(l_ok, 1)
            output(NT - 1, 1, True, 2)
            dve.wait_ge(cnt_ok, 1)
            nt_e = NT * E
            rs_(nc.vector.tensor_copy(rank[:, :, :], ps_r[:, 0:nt_e].rearrange("p (t e) -> p t e", e=E)))
            rs_(nc.vector.memset(cnt[:, 0, :], 0.0))
            for t in range(NT):
                rs_(nc.vector.tensor_tensor(cnt[:, t + 1, :], ps_r[:, nt_e + t * E:nt_e + (t + 1) * E], cnt[:, t, :], ALU.add))
            rs_(nc.vector.tensor_tensor(rank[:, :, :], rank[:, :, :], cnt[:, 0:NT, :], ALU.add))
            rs_(nc.vector.tensor_scalar(til[:, 0, :], cnt[:, NT, :], float(P - 1), None, ALU.add))
            rs_(nc.vector.tensor_copy(tili[:, 0, :], til[:, 0, :]))
            rs_(nc.vector.tensor_scalar(tili[:, 1, :], tili[:, 0, :], 7, None, ALU.logical_shift_right))
            rs_(nc.vector.tensor_copy(til[:, 1, :], tili[:, 1, :]))
            rs_(nc.vector.memset(til[:, 2, 0:1], 0.0))
            for e in range(1, E):
                rs_(nc.vector.tensor_tensor(til[:, 2, e:e + 1], til[:, 2, e - 1:e], til[:, 1, e - 1:e], ALU.add))
            rs_(nc.vector.tensor_tensor(sel[:, :, :], seen[:, :, :], rank[:, :, :], ALU.mult))
            rs_(nc.vector.tensor_reduce(rr[:, 0, :], sel[:, :, :], AX_X, ALU.add))
            rs_(nc.vector.tensor_tensor(sel[:, :, :], seen[:, :, :],
                                        til[:, 2:3, :].to_broadcast([P, NT, E]), ALU.mult))
            rs_(nc.vector.tensor_reduce(rr[:, 1, :], sel[:, :, :], AX_X, ALU.add))
            rs_(nc.vector.tensor_copy(ri[:, 0, :], rr[:, 0, :]))
            rs_(nc.vector.tensor_scalar(ri[:, 1, :], ri[:, 0, :], P - 1, None, ALU.bitwise_and))
            rs_(nc.vector.tensor_scalar(ri[:, 2, :], ri[:, 0, :], 7, None, ALU.logical_shift_right))
            rs_(nc.vector.tensor_copy(rr[:, 2, :], ri[:, 1, :]))
            rs_(nc.vector.tensor_copy(rr[:, 0, :], ri[:, 2, :]))
            rs_(nc.vector.scalar_tensor_tensor(out=rr[:, 2, :], in0=rr[:, 2, :], scalar=float(ROUTED_TILES),
                                               in1=rr[:, 0, :], op0=ALU.mult, op1=ALU.add))
            rs_(nc.vector.tensor_tensor(rr[:, 2, :], rr[:, 2, :], rr[:, 1, :], ALU.add))
            nc.vector.tensor_copy(ri[:, 3, :], rr[:, 2, :]).then_inc(slots_ok, 1)
            dve.wait_ge(e_ok, 1)
            rs_(nc.vector.tensor_reduce(se, ex[:, :, :], AX_X, ALU.add))
            nc.vector.reciprocal(gate, se).then_inc(gate_ok, 1)
            dve.wait_ge(consts, 7)
            rs_(nc.vector.memset(tacc[:, :], 0.0))
            for e in range(E):
                rs_(nc.vector.scalar_tensor_tensor(out=tacc[:, :], in0=tn[:, :], scalar=til[0:1, 2, e:e + 1],
                                                   in1=tacc[:, :], op0=ALU.is_ge, op1=ALU.add))
            nc.vector.tensor_copy(unit[:, NT:TILES], tacc[:, :]).then_inc(unit_ok, 1)
            dve.wait_ge(unit_ok, 1)

            def load_unit(n):
                return dve.value_load(unit[0:1, ds(n, 1)], min_val=0, max_val=UNITS - 1)

            tile(NT, 0, False, 2, load_unit(NT))
            tile(NT + 1, 1, False, 2, load_unit(NT + 1))
            output(NT, 0, False, 0)
            tile(NT + 2, 0, False, 2, load_unit(NT + 2))
            output(NT + 1, 1, False, 1)
            with dve.Fori(NT // 2 + 1, TILES // 2 - 1) as i:
                tile(2 * i + 1, 1, False, 2, load_unit(2 * i + 1))
                output(2 * i, 0, False, 2)
                tile(2 * i + 2, 0, False, 2, load_unit(2 * i + 2))
                output(2 * i + 1, 1, False, 2)
            tile(TILES - 2, 1, False, 2, load_unit(TILES - 2))
            output(TILES - 3, 0, False, 2)
            tile(TILES - 1, 0, False, 2, load_unit(TILES - 1))
            output(TILES - 2, 1, False, 2)
            output(TILES - 1, 0, False, 2)

        @block.tensor
        def _(pe):
            def parts(dst, a_hi, a_lo, b_hi, b_lo, start):
                nc.tensor.matmul(dst, a_hi, b_hi, start=start, stop=False, skip_group_check=True)
                nc.tensor.matmul(dst, a_hi, b_lo, start=False, stop=False, skip_group_check=True)
                return nc.tensor.matmul(dst, a_lo, b_hi, start=False, stop=False, skip_group_check=True)

            def block_j(j, b, start):
                pe.wait_ge(u_ok, 2 * j + 2)
                for k in range(GROUPS[0][1]):
                    c = slice(k * P, (k + 1) * P)
                    last = parts(acc[k], hl[:, b, 0, c], hl[:, b, 1, c], u_hi[:, ds(j * D, D)], u_lo[:, ds(j * D, D)], start)
                last.then_inc(p1_step, 1)

            pe.wait_ge(consts, 7)
            block_j(0, 0, True)
            block_j(1, 1, False)
            with pe.Fori(1, NT // 2) as i:
                for b in range(2):
                    block_j(2 * i + b, b, False)

            def add_identity(t0, count, u, start):
                for k in range(count):
                    t = t0 + k
                    last = nc.tensor.matmul(acc[k], ident2[:, :], u[:, t * D:(t + 1) * D], start=start, stop=False,
                                            skip_group_check=True)
                return last

            add_identity(0, GROUPS[0][1], u_hi, False)
            add_identity(0, GROUPS[0][1], u_lo, False).then_inc(z_acc, 1)

            for g in (1, 2):
                t0, count = GROUPS[g]
                pe.wait_ge(zlo_ok, t0)
                add_identity(t0, count, u_hi, True)
                col0 = t0 * P - G0_COLS
                with pe.Fori(0, NT) as j:
                    for k in range(count):
                        a0 = j * REST + (col0 + k * P)
                        parts(acc[k], s_hi[:, ds(a0, P)], s_lo[:, ds(a0, P)], u_hi[:, ds(j * D, D)], u_lo[:, ds(j * D, D)], False)
                add_identity(t0, count, u_lo, False).then_inc(z_acc, 1)

            def macro(g, m, first):
                t0, count = GROUPS[g]
                for s in range(2 * CH):
                    b = s % 2
                    if s < STEPS:
                        J = STEPS * m + s
                        pe.wait_ge(atlo_ok, J + 1)
                        j = STEPS * (m - g * NT // STEPS) + s
                        zj_hi = z_hi[:, ds(j, 1), :].rearrange("p a d -> p (a d)")
                        zj_lo = z_lo[:, ds(j, 1), :].rearrange("p a d -> p (a d)")
                        for k in range(count):
                            c = slice(k * P, (k + 1) * P)
                            last = parts(acc[k], hl[:, b, 0, c], hl[:, b, 1, c], zj_hi, zj_lo, first and s == 0)
                        last.then_inc(p2_step, 1)
                    q = 2 * CH * m + s
                    pe.wait_ge(tern_ok, q + 1)
                    if not (first and g == 0 and s < 2):
                        pe.wait_ge(wt_ok, q - 1)
                    for k in range(8):
                        dst = (k % 4) * 2 + k // 4 if s < CH else k
                        last = nc.tensor.transpose(pst[b][:, dst * P:(dst + 1) * P], tern[:, b, k * P:(k + 1) * P], ident[:, :])
                    last.then_inc(tr_ok, 1)

            pe.wait_ge(zlo_ok, NT)
            for g in range(3):
                m0 = g * NT // STEPS
                if g:
                    pe.wait_ge(x1_ok, GROUPS[g][0])
                macro(g, m0, True)
                with pe.Fori(m0 + 1, m0 + NT // STEPS) as m:
                    macro(g, m, False)

            def rows_to_columns(n, b, shared):
                if shared:
                    pe.wait_ge(hrow_in[b], slot_count(n, b) + 16)
                else:
                    pe.wait_ge(hrow_got[b], slot_count(n - NT, b) + 16)
                if not (isinstance(n, int) and n == 0):
                    pe.wait_ge(ht_ok, n)
                for k in range(2 * DB):
                    last = nc.tensor.transpose(ps_ht[:, k * P:(k + 1) * P], hrow[:, b, k * P:(k + 1) * P], ident[:, :])
                last.then_inc(tr2_ok, 1)

            def first_product(n, b, lead, u):
                pe.wait_ge(ht_ok, n + 1)
                if lead >= 2:
                    pe.wait_ge(pre_ok, 2 * n - 2)
                for f in range(FB):
                    for d in range(DB):
                        w = w1t[:, ds(u * (4 * CHUNK) + (f // 2) * CHUNK + d * 2 * P + (f % 2) * P, P)]
                        for h in range(2):
                            c = (h * DB + d) * P
                            last = nc.tensor.matmul(ps_h[b][f // 4][:, (f % 4) * P:(f % 4 + 1) * P], w,
                                                    ht[:, b, c:c + P], start=(f % 4 == 0 and d == 0 and h == 0),
                                                    stop=False, skip_group_check=True)
                last.then_inc(m1_ok, 1)

            def logits(n, b):
                if not (isinstance(n, int) and n == 0):
                    pe.wait_ge(l_ok, n)
                for d in range(DB):
                    for h in range(2):
                        c = (h * DB + d) * P
                        last = nc.tensor.matmul(ps_r[:, 0:3 * E], ht[:, b, c:c + P],
                                                r3[:, d, :, :].rearrange("p a e -> p (a e)"),
                                                start=(d == 0 and h == 0), stop=False, skip_group_check=True)
                last.then_inc(r_ok, 1)

            def second_product(n, b, lead, u):
                pe.wait_ge(h1lo_ok, 2 * n + 2)
                if lead >= 2:
                    pe.wait_ge(y_ok, n - 1)
                for f in range(FB):
                    w = w2t[:, ds(u * (4 * CHUNK), 4 * CHUNK)].rearrange("p (d f c) -> p f d c", d=DB, f=FB)[:, f, :, :]
                    for h in range(2):
                        last = nc.tensor.matmul(ps_y[b][:, :].rearrange("p (d c) -> p d c", d=DB),
                                                h1hl[:, b, h, f * P:(f + 1) * P], w,
                                                start=(f == 0 and h == 0), stop=False, skip_group_check=True)
                last.then_inc(m2_ok, 1)

            pe.wait_ge(wt_ok, 2 * CHUNKS)
            pe.wait_ge(x1_ok, NT)
            pe.wait_ge(r3_ok, 1)
            def front(n, b, lead, u, shared=False):
                rows_to_columns(n, b, shared)
                first_product(n, b, lead, u)

            def shared_front(n, b, lead):
                front(n, b, lead, 0, True)
                logits(n, b)

            shared_front(0, 0, 0)
            shared_front(1, 1, 1)
            second_product(0, 0, 0, 0)
            shared_front(2, 0, 2)
            second_product(1, 1, 1, 0)
            with pe.Fori(1, NT // 2 - 1) as i:
                shared_front(2 * i + 1, 1, 2)
                second_product(2 * i, 0, 2, 0)
                shared_front(2 * i + 2, 0, 2)
                second_product(2 * i + 1, 1, 2, 0)
            shared_front(NT - 1, 1, 2)
            second_product(NT - 2, 0, 2, 0)
            second_product(NT - 1, 1, 2, 0)

            pe.wait_ge(hot_ok, 1)
            hot_all = hot16[:, :, :].rearrange("p t e -> p (t e)")
            nc.tensor.matmul(ps_r[:, 0:NT * E], tri[:, :], hot_all, start=True, stop=True, skip_group_check=True)
            nc.tensor.matmul(ps_r[:, NT * E:2 * NT * E], ones[:, :], hot_all, start=False, stop=True,
                             skip_group_check=True).then_inc(cnt_ok, 1)

            pe.wait_ge(unit_ok, 1)

            def load_unit(n):
                return pe.value_load(unit[0:1, ds(n, 1)], min_val=0, max_val=UNITS - 1)

            front(NT, 0, 2, load_unit(NT))
            with pe.Fori(NT // 2, TILES // 2 - 1) as i:
                front(2 * i + 1, 1, 2, load_unit(2 * i + 1))
                second_product(2 * i, 0, 2, load_unit(2 * i))
                front(2 * i + 2, 0, 2, load_unit(2 * i + 2))
                second_product(2 * i + 1, 1, 2, load_unit(2 * i + 1))
            front(TILES - 2, 1, 2, load_unit(TILES - 2))
            second_product(TILES - 3, 0, 2, load_unit(TILES - 3))
            front(TILES - 1, 0, 2, load_unit(TILES - 1))
            second_product(TILES - 2, 1, 2, load_unit(TILES - 2))
            second_product(TILES - 1, 0, 2, load_unit(TILES - 1))


def kernel(x, adj, L0_ffn_shared_w1, L0_ffn_shared_w2, L0_ffn_expert_w1, L0_ffn_expert_w2, L0_ffn_router_w,
           L0_ffn_ln_gamma, L0_ffn_ln_beta):
    import numpy as np
    import concourse.bacc as bacc
    from concourse.bass_utils import run_bass_kernel_spmd

    arrays = {
        "x": np.ascontiguousarray(x),
        "adj": np.ascontiguousarray(adj),
        "adj_t": np.ascontiguousarray(np.asarray(adj).T),
        "w1": np.concatenate([np.asarray(L0_ffn_shared_w1)[None], np.asarray(L0_ffn_expert_w1)]),
        "w2": np.concatenate([np.asarray(L0_ffn_shared_w2)[None], np.asarray(L0_ffn_expert_w2)]),
        "router_t": np.ascontiguousarray(np.asarray(L0_ffn_router_w).T),
        "gamma": np.ascontiguousarray(L0_ffn_ln_gamma),
        "beta": np.ascontiguousarray(L0_ffn_ln_beta),
    }
    nc = bacc.Bacc("TRN2", target_bir_lowering=False, num_devices=1)
    args = [nc.dram_tensor(f"in_{k}", v.shape, mybir.dt.from_np(v.dtype), kind="ExternalInput").ap()
            for k, v in arrays.items()]
    out = nc.dram_tensor("out", (N, D), F32, kind="ExternalOutput").ap()
    build(nc, *args, out)
    r = run_bass_kernel_spmd(nc, [{f"in_{k}": v for k, v in arrays.items()}], core_ids=[0])
    return r.results[0]["out"]
```

```python
from contextlib import ExitStack

import concourse.bass as bass
from concourse import mybir

ALU = mybir.AluOpType
ACT = mybir.ActivationFunctionType
F32 = mybir.dt.float32
F16 = mybir.dt.float16
BF16 = mybir.dt.bfloat16
I32 = mybir.dt.int32
AX_X = mybir.AxisListType.X
ds = bass.ds

P = 128
N = 2048
D = 512
F = 1024
E = 8
UNITS = E + 1
NT = N // P
DB = D // P
FB = F // P
EPS = 1e-5
QMIN = 1e-5

Z_GROUPS = [(0, 8, (0, 1, 2, 3, 4, 5, 6, 7)), (8, 4, (0, 1, 2, 3)), (12, 4, (0, 1, 4, 5))]
Y_GROUPS = [(0, 6), (6, 6), (12, 4)]
G0_COLS = Z_GROUPS[0][1] * P
REST = N - G0_COLS
UNROLL = 4
A_SCALE = 256.0
U_SCALE = 16.0
CHUNK = 1024
CHUNKS = UNITS * F * D // (P * CHUNK)
ROUNDS = 4
ROUND_STEPS = 2 * NT // ROUNDS
EARLY = 6
EARLY0 = CHUNKS - ROUNDS * EARLY
MACROS = 12
STEPS = len(Y_GROUPS) * NT // MACROS
CH = CHUNKS // MACROS
KINDS = CH + 1
ROUTED_TILES = N // P + E - 1
TILES = NT + ROUTED_TILES
BASE_W = D + 1
PAD = N


def build(nc, x, adj, adj_t, w1, w2, router_t, gamma, beta, out):
    with ExitStack() as ctx:
        def sb(name, shape, dt):
            return ctx.enter_context(nc.sbuf_tensor(name, shape, dt))

        def sem(name):
            return ctx.enter_context(nc.semaphore(name))

        x1_dram = nc.dram_tensor("x1_scratch", [N, D], F32, kind="Internal").ap()
        h_dram = nc.dram_tensor("h_scratch", [N + P, 2 * D], F16, kind="Internal").ap()
        base_dram = nc.dram_tensor("base_scratch", [N + P, BASE_W], F32, kind="Internal").ap()
        s2_dram = nc.dram_tensor("s2_scratch", [UNITS, D], F32, kind="Internal").ap()
        list_dram = nc.dram_tensor("list_scratch", [P * ROUTED_TILES, 1], I32, kind="Internal").ap()

        region = sb("region", [P, 2 * CHUNKS * CHUNK], F16)
        w1t = region[:, 0:CHUNKS * CHUNK]
        w2t = region[:, CHUNKS * CHUNK:2 * CHUNKS * CHUNK]
        o = 0
        s_hi = region[:, o:o + NT * REST]; o += NT * REST
        s_lo = region[:, o:o + NT * REST]; o += NT * REST
        u_hi = region[:, o:o + NT * D]; o += NT * D
        u_lo = region[:, o:o + NT * D]; o += NT * D
        a_in = region[:, o:o + 4 * 2 * N].bitcast(F32).rearrange("p (b n) -> p b n", b=4); o += 8 * N
        t_in = region[:, o:o + 2 * 2 * N].bitcast(F32).rearrange("p (b n) -> p b n", b=2)
        late1 = 24 * CHUNK
        xg_r = w1t[:, late1:late1 + 12 * CHUNK].bitcast(F32).rearrange("p (t d) -> p t d", d=D)

        zreg = sb("zreg", [P, 2 * NT * D], F16)
        xhat = zreg[:, :].bitcast(F32).rearrange("p (t d) -> p t d", t=NT)
        z_hi = zreg[:, 0:NT * D].rearrange("p (t d) -> p t d", t=NT)
        z_lo = zreg[:, NT * D:2 * NT * D].rearrange("p (t d) -> p t d", t=NT)
        zf = zreg[:, :].bitcast(F32)
        xg_z = zf[:, 0:4 * D].rearrange("p (t d) -> p t d", d=D)
        s2bc = zf[:, 7 * D:9 * D].rearrange("p (b d) -> p b d", b=2)
        o_t = zf[:, 9 * D:11 * D].rearrange("p (b d) -> p b d", b=2)
        base_t = zf[:, 11 * D:11 * D + 2 * BASE_W].rearrange("p (b d) -> p b d", b=2)

        work = sb("work", [P, 12288], F16)
        HL = Y_GROUPS[0][1] * P
        hl_z = work[:, 0:4 * G0_COLS].rearrange("p (b h n) -> p b h n", b=2, h=2)
        hl = work[:, 0:4 * HL].rearrange("p (b h n) -> p b h n", b=2, h=2)
        at = work[:, 4 * HL:8 * HL].bitcast(F32).rearrange("p (b n) -> p b n", b=2)
        raw = work[:, 6144:6144 + 4096].bitcast(F32).rearrange("p (b n) -> p b n", b=2)
        tern = work[:, 10240:12288].rearrange("p (b n) -> p b n", b=2)
        pre = work[:, 0:2048].bitcast(F32)
        h1 = work[:, 2048:4096].bitcast(F32)
        h1hl = work[:, 4096:8192].rearrange("p (b h n) -> p b h n", b=2, h=2)
        ht = work[:, 8192:10240].rearrange("p (b n) -> p b n", b=2)
        hrow = work[:, 10240:12288].rearrange("p (b n) -> p b n", b=2)

        gb = sb("gb", [P, 2, D], F32)
        xb = sb("xb", [P, 2, D], F32)
        hb = sb("hb", [P, 2, 2 * D], F16)
        ident = sb("ident", [P, P], F16)
        ident2 = sb("ident2", [P, P], F16)
        tri = sb("tri", [P, P], F16)
        ones = sb("ones", [P, P], F16)
        st4 = sb("st4", [P, UNROLL, 6], F32)
        mv4 = sb("mv4", [P, UNROLL, 2], F32)
        r4 = sb("r4", [P, 3, UNROLL], F32)
        stb = sb("stb", [P, 2, 6], F32)
        mvb = sb("mvb", [P, 2, 2], F32)
        rb = sb("rb", [P, 2, 2], F32)
        power = sb("power", [P, UNROLL], F32)
        junk = sb("junk", [P, D], F16)
        asum = sb("asum", [P, 2, 2], F32)
        rs = sb("rs", [P, 2, 2], F32)
        dv = sb("dv", [P, 2, 4], F32)
        dinv = sb("dinv", [P, NT], F32)
        dinvz = sb("dinvz", [P, NT], F32)
        thr = sb("thr", [P, 2, 2, 2], F32)
        s1 = sb("s1", [P, 2 * CHUNKS], F32)
        s2 = sb("s2", [P, CHUNKS], F32)
        rt = sb("rt", [P, DB, E], F32)
        r3 = sb("r3", [P, DB, 3, E], BF16)
        taken = [11 * D + 2 * BASE_W]

        def late(shape, dt=F32):
            n = 1
            for v in shape:
                n *= v
            words = n if dt != F16 else n // 2
            v = zf[:, taken[0]:taken[0] + words]
            taken[0] += words
            v = v.bitcast(dt) if dt != F32 else v
            return v.rearrange("p (a b) -> p a b", a=shape[0]) if len(shape) == 2 else v

        lg = late([NT, E])
        lg2 = late([2, E])
        mx = late([NT])
        ex = late([NT, E])
        se = late([NT])
        gate = late([NT])
        hot = late([NT, E])
        hot16 = late([NT, E], F16)
        seen = late([NT, E])
        cnt = late([NT + 1, E])
        til = late([3, E])
        tili = late([2, E], I32)
        rank = late([NT, E])
        sel = late([NT, E])
        rr = late([3, NT])
        ri = late([4, NT], I32)
        lst = late([ROUTED_TILES], I32)
        tacc = late([ROUTED_TILES])[0:1, :]
        rtr = late([DB, E])
        zero_row = zf[:, 0:BASE_W]
        tok = sb("tok", [P, NT], I32)
        padl = sb("padl", [P, ROUTED_TILES], I32)
        tn = sb("tn", [1, ROUTED_TILES], F32)
        idx = sb("idx", [P, 6], I32)
        unit = sb("unit", [1, TILES], I32)

        bank = [ctx.enter_context(nc.psum_tensor(f"bank{i}", [P, 512], F32)) for i in range(8)]
        acc = [bank[i][:, :] for i in range(8)]
        pst = [bank[6][:, :].bitcast(F16), bank[7][:, :].bitcast(F16)]
        ps_ht = bank[6][:, :].bitcast(F16)
        ps_h = [[bank[0], bank[1]], [bank[2], bank[3]]]
        ps_y = [bank[4], bank[5]]
        ps_r = bank[7]

        x_in = [sem("x_in0"), sem("x_in1")]
        small_in = sem("small_in")
        a_loaded = [sem(f"a_loaded{i}") for i in range(4)]
        t_loaded = [sem(f"t_loaded{i}") for i in range(2)]
        consts = sem("consts")
        const0 = sem("const0")
        tri_ok = sem("tri_ok")
        xh_seq = sem("xh_seq")
        xv_ok = sem("xv_ok")
        xr_ok = sem("xr_ok")
        sum_ok = sem("sum_ok")
        rest_ok = sem("rest_ok")
        shi_ok = sem("shi_ok")
        slo_ok = sem("slo_ok")
        deg_seq = sem("deg_seq")
        deg_ok = sem("deg_ok")
        deg_root = sem("deg_root")
        u_ok = sem("u_ok")
        p1_step = sem("p1_step")
        z_acc = sem("z_acc")
        zhi_ok = sem("zhi_ok")
        zlo_ok = sem("zlo_ok")
        at_loaded = [sem("at_loaded0"), sem("at_loaded1")]
        athi_ok = sem("athi_ok")
        atlo_ok = sem("atlo_ok")
        p2_step = sem("p2_step")
        raw_loaded = [sem("raw_loaded0"), sem("raw_loaded1")]
        abs_ok = sem("abs_ok")
        w_seq = sem("w_seq")
        tern_ok = sem("tern_ok")
        tr_ok = sem("tr_ok")
        wt_ok = sem("wt_ok")
        xg_in = [sem("xg_in0"), sem("xg_in1")]
        x1_ok = sem("x1_ok")
        x1_stored = sem("x1_stored")
        ln_seq = sem("ln_seq")
        ln_var = sem("ln_var")
        ln_root = sem("ln_root")
        ln_normed = sem("ln_normed")
        h_seq = sem("h_seq")
        h_ok = sem("h_ok")
        hhi_ok = sem("hhi_ok")
        hlo_ok = sem("hlo_ok")
        h_stored = [sem("h_stored0"), sem("h_stored1")]
        dinvz_ok = sem("dinvz_ok")
        s2_stored = sem("s2_stored")
        pads_stored = sem("pads_stored")
        hrow_in = [sem("hrow_in0"), sem("hrow_in1")]
        s2_in = [sem("s2_in0"), sem("s2_in1")]
        base_in = [sem("base_in0"), sem("base_in1")]
        hrow_got = [sem("hrow_got0"), sem("hrow_got1")]
        base_got = [sem("base_got0"), sem("base_got1")]
        out_stored = [sem("out_stored0"), sem("out_stored1")]
        tr2_ok = sem("tr2_ok")
        ht_ok = sem("ht_ok")
        m1_ok = sem("m1_ok")
        pre_ok = sem("pre_ok")
        h1_ok = sem("h1_ok")
        h1hi_ok = sem("h1hi_ok")
        h1lo_ok = sem("h1lo_ok")
        m2_ok = sem("m2_ok")
        y_seq = sem("y_seq")
        y_ok = sem("y_ok")
        y_stored = [sem("y_stored0"), sem("y_stored1")]
        r_ok = sem("r_ok")
        l_seq = sem("l_seq")
        l_ok = sem("l_ok")
        e_ok = sem("e_ok")
        r3_ok = sem("r3_ok")
        r_seq = sem("r_seq")
        hot_ok = sem("hot_ok")
        cnt_ok = sem("cnt_ok")
        rt_seq = sem("rt_seq")
        slots_ok = sem("slots_ok")
        unit_ok = sem("unit_ok")
        scat = sem("scat")
        zero_ok = sem("zero_ok")
        pool_waits = sem("pool_waits")
        dve_waits = sem("dve_waits")
        idx_ok = [sem("idx_ok_h"), sem("idx_ok_base"), sem("idx_ok_out")]
        gate_ok = sem("gate_ok")
        gate_stored = sem("gate_stored")
        list_in = sem("list_in")

        adj_j = adj.rearrange("(j p) n -> j p n", p=P)
        adjt_j = adj_t.rearrange("(j p) n -> j p n", p=P)
        x_t = x.rearrange("(t p) d -> p t d", p=P)
        x1_t = x1_dram.rearrange("(t p) d -> p t d", p=P)
        w1_c = w1.rearrange("u (c b p) d -> (u c) p b d", b=2, p=P)
        w2_c = w2.rearrange("u (c p) f -> (u c) p f", p=P)

        DEG = 3
        XOPS = 3 * UNROLL + 1
        LN_OPS = 3
        WOPS1, WOPS2 = 5, 4
        WOPS = CH * WOPS1 + WOPS2
        EARLY_OPS = EARLY * WOPS2
        EARLY_CHUNKS = ROUNDS * EARLY

        def slot_count(n, b):
            return (n - b) * 8

        def early(rnd, s):
            return EARLY * rnd + s, 2, EARLY0 + EARLY * rnd + s

        def later(m, s):
            return (EARLY_CHUNKS + KINDS * m + s,) + ((1, CH * m + s) if s < CH else (2, m))

        block = ctx.enter_context(nc.Block())

        @block.sync
        def _(sp):
            sp.dma_start(xhat[:, 0:UNROLL, :], x_t[:, 0:UNROLL, :]).then_inc(x_in[0], 16)

            def load_a(j, s, first):
                if not first:
                    sp.wait_ge(slo_ok, j - 3)
                sp.dma_start(a_in[:, s, :], adj_j[ds(j, 1), :, :].rearrange("a p n -> (a p) n")).then_inc(a_loaded[s], 16)
                if not (first and s < 2):
                    sp.wait_ge(sum_ok, j - 1)
                    sp.wait_ge(rest_ok, j - 1)
                sp.dma_start(t_in[:, s % 2, :], adjt_j[ds(j, 1), :, :].rearrange("a p n -> (a p) n")
                             ).then_inc(t_loaded[s % 2], 16)

            load_a(0, 0, True)
            def load_x(batch):
                sp.dma_start(xhat[:, ds(UNROLL * batch, UNROLL), :], x_t[:, ds(UNROLL * batch, UNROLL), :]
                             ).then_inc(x_in[1], 16)

            load_a(1, 1, True)
            load_x(1)
            for s in range(2, UNROLL):
                load_a(s, s, True)
            with sp.Fori(1, NT // UNROLL - 1) as i:
                for s in range(UNROLL):
                    load_a(UNROLL * i + s, s, False)
                    if s == 1:
                        load_x(i + 1)
            for s in range(UNROLL):
                load_a(NT - UNROLL + s, s, False)
            sp.dma_start(gb[:, 0, :], gamma.rearrange("(a d) -> a d", a=1).to_broadcast([P, D])).then_inc(small_in, 16)
            sp.dma_start(gb[:, 1, :], beta.rearrange("(a d) -> a d", a=1).to_broadcast([P, D])).then_inc(small_in, 16)
            sp.dma_start(rt[:, :, :], router_t.rearrange("(b p) e -> p b e", p=P)).then_inc(small_in, 16)

            def load_w(chunk, b, first):
                q, kind, c = chunk
                if not first:
                    sp.wait_ge(tern_ok, q - 1)
                if kind == 1:
                    sp.dma_start(raw[:, b, :].rearrange("p (a d) -> p a d", a=2),
                                 w1_c[ds(c, 1), :, :, :].rearrange("c p b d -> (c p) b d")).then_inc(raw_loaded[b], 16)
                else:
                    sp.dma_start(raw[:, b, :], w2_c[ds(c, 1), :, :].rearrange("c p f -> (c p) f")
                                 ).then_inc(raw_loaded[b], 16)

            for s in range(EARLY):
                load_w(early(0, s), s % 2, s < 2)
            with sp.Fori(1, ROUNDS) as rnd:
                for s in range(EARLY):
                    load_w(early(rnd, s), s % 2, False)

            def macro(g, m, first):
                c0, nc_ = Y_GROUPS[g][0] * P, Y_GROUPS[g][1] * P
                for s in range(STEPS):
                    if not (first and s < 2):
                        sp.wait_ge(atlo_ok, STEPS * m + s - 1)
                    j = STEPS * (m - g * NT // STEPS) + s
                    sp.dma_start(at[:, s % 2, 0:nc_],
                                 adjt_j[ds(j, 1), :, c0:c0 + nc_].rearrange("a p n -> (a p) n")
                                 ).then_inc(at_loaded[s % 2], 16)
                    load_w(later(m, s), s % 2, False)

            sp.wait_ge(z_acc, 1)
            for g in range(3):
                m0 = g * NT // STEPS
                macro(g, m0, g == 0)
                if g == 0:
                    sp.wait_ge(z_acc, 3)
                    sp.dma_start(xg_r[:, :, :], x_t[:, 0:12, :]).then_inc(xg_in[0], 16)
                with sp.Fori(m0 + 1, m0 + NT // STEPS) as m:
                    macro(g, m, False)
            sp.wait_ge(tern_ok, 2 * CHUNKS)
            sp.dma_start(raw[:, :, :].rearrange("p b (t d) -> p (b t) d", d=D), x_t[:, 12:16, :]).then_inc(xg_in[1], 16)
            sp.dma_start(s2_dram.rearrange("u (c p) -> p (u c)", p=P), s2[:, :],
                         allow_slow_non_contiguous=True).then_inc(s2_stored, 16)

            def load_shared(n, b):
                sp.wait_ge(h_stored[b], slot_count(n, b) + 16)
                sp.dma_start(hrow[:, b, :], h_dram[ds(n * P, P), :]).then_inc(hrow_in[b], 16)

            def load_base(n, b):
                sp.dma_start(s2bc[:, b, :], s2_dram[0:1, :].to_broadcast([P, D])).then_inc(s2_in[b], 16)
                sp.dma_start(base_t[:, b, 0:D], x1_dram[ds(n * P, P), :]).then_inc(base_in[b], 16)

            sp.wait_ge(tr_ok, 2 * CHUNKS)
            for b in range(2):
                load_shared(b, b)
            sp.wait_ge(s2_stored, 16)
            sp.wait_ge(x1_stored, 16 * 3)
            for b in range(2):
                load_base(b, b)
            sp.wait_ge(tr2_ok, 1)
            load_shared(2, 0)

            def shared_loads(i, last=False):
                for b in range(2):
                    if not (last and b):
                        sp.wait_ge(tr2_ok, 2 * i + b)
                        load_shared(2 * i + b + 1, 1 - b)
                    sp.wait_ge(y_stored[b], 16 * i)
                    load_base(2 * i + b, b)

            with sp.Fori(1, NT // 2 - 1) as i:
                shared_loads(i)
            shared_loads(NT // 2 - 1, True)

            sp.wait_ge(scat, 16 * NT)
            sp.dma_start(lst[:, :], list_dram.rearrange("(p n) a -> p (n a)", p=P)).then_inc(list_in, 16)

            sp.wait_ge(unit_ok, 1)
            with sp.Fori(0, ROUTED_TILES // 2) as i:
                for b in range(2):
                    u = sp.value_load(unit[0:1, ds(NT + 2 * i + b, 1)], min_val=0, max_val=UNITS - 1)
                    sp.wait_ge(y_ok, NT - 1 + 2 * i + b)
                    sp.dma_start(s2bc[:, b, :], s2_dram[ds(u, 1), :].to_broadcast([P, D])).then_inc(s2_in[b], 16)
            u = sp.value_load(unit[0:1, TILES - 1:TILES], min_val=0, max_val=UNITS - 1)
            sp.wait_ge(y_ok, TILES - 2)
            sp.dma_start(s2bc[:, 0, :], s2_dram[ds(u, 1), :].to_broadcast([P, D])).then_inc(s2_in[0], 16)

        @block.gpsimd
        def _(pool):
            def pool_wait(s, value):
                pool.wait_ge(s, value)
                pool.sem_inc(pool_waits, 1)

            nc.gpsimd.memset(ident[:], 0.0).then_inc(const0, 1)
            nc.gpsimd.memset(ident2[:], 0.0).then_inc(const0, 1)
            nc.gpsimd.memset(ones[:], 1.0).then_inc(const0, 1)
            pool.wait_ge(const0, 3)
            nc.gpsimd.affine_select(out=ident[:], in_=ident[:], compare_op=ALU.not_equal, fill=1.0, base=0,
                                    pattern=[[-1, P]], channel_multiplier=1).then_inc(consts, 1)
            nc.gpsimd.affine_select(out=ident2[:], in_=ident2[:], compare_op=ALU.not_equal, fill=2.0 * A_SCALE,
                                    base=0, pattern=[[-1, P]], channel_multiplier=1).then_inc(consts, 1)
            nc.gpsimd.affine_select(out=tri[:], in_=ones[:], compare_op=ALU.is_gt, fill=0.0, base=0,
                                    pattern=[[1, P]], channel_multiplier=-1).then_inc(consts, 1)
            nc.gpsimd.iota(tok[:, :], pattern=[[P, NT]], base=0, channel_multiplier=1).then_inc(consts, 1)
            nc.gpsimd.iota(padl[:, :], pattern=[[0, ROUTED_TILES]], base=PAD, channel_multiplier=1).then_inc(consts, 1)
            nc.gpsimd.iota(tn[:, :], pattern=[[1, ROUTED_TILES]], base=0, channel_multiplier=0,
                           allow_small_or_imprecise_dtypes=True).then_inc(consts, 1)
            nc.gpsimd.memset(unit[:, 0:NT], 0).then_inc(consts, 1)
            nc.gpsimd.memset(power[:, :], -0.5).then_inc(consts, 1)
            pool.wait_ge(consts, 8)

            def x_root(batch):
                pool.wait_ge(xv_ok, batch + 1)
                nc.gpsimd.tensor_tensor(r4[:, 1, :], r4[:, 0, :], power[:, :], ALU.pow).then_inc(xr_ok, 1)

            def sum_rest(i, s):
                pool.wait_ge(a_loaded[s], 16 * i + 16)
                pool.wait_ge(t_loaded[s % 2], 32 * i + 16 * (s // 2) + 16)
                nc.gpsimd.tensor_tensor(a_in[:, s, G0_COLS:N], a_in[:, s, G0_COLS:N], t_in[:, s % 2, G0_COLS:N],
                                        ALU.add).then_inc(rest_ok, 1)

            def round_roots(i, last):
                for s in range(UNROLL):
                    if s < UNROLL - 1:
                        sum_rest(i, s + 1)
                    elif not last:
                        sum_rest(i + 1, 0)
                    pool.wait_ge(deg_ok, UNROLL * i + s + 1)
                    nc.gpsimd.tensor_tensor(dv[:, s % 2, 3:4], dv[:, s % 2, 2:3], power[:, 0:1],
                                            ALU.pow).then_inc(deg_root, 1)
                if not last:
                    x_root(i + 1)

            x_root(0)
            sum_rest(0, 0)
            with pool.Fori(0, NT // UNROLL - 1) as i:
                round_roots(i, False)
            round_roots(NT // UNROLL - 1, True)
            pool.dma_start(list_dram.rearrange("(p n) a -> p (n a)", p=P), padl[:, :]).then_inc(pads_stored, 16)

            def norm_pair(t):
                for r in range(2):
                    for b in range(2):
                        pool.wait_ge(ln_var, 2 * t + 2 * r + b + 1)
                        nc.gpsimd.tensor_tensor(rb[:, b, 1:2], rb[:, b, 0:1], power[:, 0:1], ALU.pow).then_inc(ln_root, 1)
                for b in range(2):
                    pool.wait_ge(ln_normed, t + b + 1)
                    nc.gpsimd.tensor_tensor(xb[:, b, :], xb[:, b, :], gb[:, 0, :], ALU.mult).then_inc(h_seq, 1)
                    pool.wait_ge(h_seq, t + b + 1)
                    nc.gpsimd.tensor_tensor(xb[:, b, :], xb[:, b, :], gb[:, 1, :], ALU.add).then_inc(h_ok, 1)
                for b in range(2):
                    pool.wait_ge(hhi_ok, t + b + 1)
                    nc.gpsimd.tensor_tensor(hb[:, b, D:2 * D], xb[:, b, :], hb[:, b, 0:D],
                                            ALU.subtract).then_inc(hlo_ok, 1)
                for b in range(2):
                    pool_wait(hlo_ok, t + b + 1)
                    pool.dma_start(h_dram[ds((t + b) * P, P), :], hb[:, b, :]).then_inc(h_stored[b], 16)

            pool.wait_ge(small_in, 48)
            with pool.Fori(0, NT // 2) as i:
                norm_pair(2 * i)

            for b in range(2):
                pool.wait_ge(h_stored[b], 16 * NT // 2)
            pool.wait_ge(hlo_ok, NT)
            nc.gpsimd.memset(zero_row, 0.0).then_inc(zero_ok, 1)
            pool.wait_ge(zero_ok, 1)
            pool.dma_start(h_dram[N:N + P, :], zero_row[:, 0:D].bitcast(F16)).then_inc(pads_stored, 16)
            pool.dma_start(base_dram[N:N + P, :], zero_row).then_inc(pads_stored, 16)

            pool.wait_ge(slots_ok, 1)
            pool.wait_ge(pads_stored, 48)
            for t in range(NT):
                pool.indirect_dma_start(
                    out=list_dram, out_offset=bass.IndirectOffsetOnAxis(ap=ri[:, 3, t:t + 1], axis=0),
                    in_=tok[:, t:t + 1], in_offset=None).then_inc(scat, 16)
            pool.wait_ge(list_in, 16)
            pool.wait_ge(gate_stored, 16)
            for b in range(2):
                pool.wait_ge(y_stored[b], 16 * NT // 2)

            def tokens(n, b, use):
                at_ = idx[:, 2 * use + b:2 * use + b + 1]
                nc.gpsimd.tensor_copy(at_, lst[:, ds(n - NT, 1)]).then_inc(idx_ok[use], 1)
                pool_wait(idx_ok[use], n - NT + 1)
                return bass.IndirectOffsetOnAxis(ap=at_, axis=0)

            def gather_h(n, b):
                pool.indirect_dma_start(out=hrow[:, b, :], out_offset=None, in_=h_dram,
                                        in_offset=tokens(n, b, 0)).then_inc(hrow_got[b], 16)

            def gather_base(n, b):
                pool.indirect_dma_start(out=base_t[:, b, :], out_offset=None, in_=base_dram,
                                        in_offset=tokens(n, b, 1)).then_inc(base_got[b], 16)

            def scatter(n, b):
                pool_wait(y_ok, n + 1)
                pool.indirect_dma_start(out=out, out_offset=tokens(n, b, 2), in_=o_t[:, b, :], in_offset=None,
                                        bounds_check=N - 1, oob_is_err=False).then_inc(out_stored[b], 16)

            def turn(n, b):
                pool_wait(tr2_ok, n + 2)
                gather_h(n + 3, 1 - b)
                scatter(n, b)
                gather_base(n + 2, b)

            for b in range(2):
                gather_h(NT + b, b)
                gather_base(NT + b, b)
            pool_wait(tr2_ok, NT + 1)
            gather_h(NT + 2, 0)
            with pool.Fori(0, (ROUTED_TILES - 3) // 2) as i:
                for b in range(2):
                    turn(NT + 2 * i + b, b)
            scatter(TILES - 3, 0)
            gather_base(TILES - 1, 0)
            scatter(TILES - 2, 1)
            scatter(TILES - 1, 0)
            for b in range(2):
                pool.wait_ge(out_stored[b], 16 * ((ROUTED_TILES + 1 - b) // 2))

        @block.scalar
        def _(act):
            def split_s(j, b, first):
                act.wait_ge(sum_ok, j + 1)
                if not (first and j < 2):
                    act.wait_ge(p1_step, j - 1)
                    act.wait_ge(deg_ok, j - 1)
                nc.scalar.activation(hl_z[:, b % 2, 0, :], a_in[:, b, 0:G0_COLS], ACT.Copy, scale=A_SCALE,
                                     accum_out=rs[:, b % 2, 0:1]).then_inc(shi_ok, 1)
                act.wait_ge(rest_ok, j + 1)
                nc.scalar.activation(s_hi[:, ds(j * REST, REST)], a_in[:, b, G0_COLS:N], ACT.Copy, scale=A_SCALE,
                                     accum_out=rs[:, b % 2, 1:2]).then_inc(shi_ok, 1)

            for s in range(UNROLL):
                split_s(s, s, True)
            with act.Fori(1, NT // UNROLL) as i:
                for s in range(UNROLL):
                    split_s(UNROLL * i + s, s, False)

            def z_high(g):
                t0, count, banks = Z_GROUPS[g]
                act.wait_ge(z_acc, g + 1)
                for k in range(count):
                    nc.scalar.activation(z_hi[:, t0 + k, :], acc[banks[k]], ACT.Copy,
                                         scale=dinvz[:, t0 + k:t0 + k + 1]).then_inc(zhi_ok, 1)

            def sums(chunk, b):
                q, kind, c = chunk
                act.wait_ge(raw_loaded[b], 8 * (q - b) + 16)
                for a in range(2):
                    if not (isinstance(q, int) and q == 0 and a == 0):
                        act.wait_ge(abs_ok, 2 * q + a)
                    nc.scalar.activation(junk[:, :], raw[:, b, a * D:(a + 1) * D], ACT.Abs,
                                         accum_out=asum[:, b, a:a + 1]).then_inc(abs_ok, 1)

            def store_w(chunk, b):
                q, kind, c = chunk
                act.wait_ge(tr_ok, q + 1)
                dst = w1t if kind == 1 else w2t
                nc.scalar.activation(dst[:, ds(c * CHUNK, CHUNK)], pst[b], ACT.Copy).then_inc(wt_ok, 1)

            act.wait_ge(dinvz_ok, 1)
            z_high(0)

            LAG = 3

            def early_round(rnd, first):
                for s in range(EARLY):
                    if not (first and s < LAG):
                        store_w(early(rnd, s - LAG) if s >= LAG else early(rnd - 1, s - LAG + EARLY), (s - LAG) % 2)
                    sums(early(rnd, s), s % 2)

            early_round(0, True)
            early_round(1, False)
            z_high(1)
            early_round(2, False)
            early_round(3, False)
            z_high(2)

            def high(g, J, b, first=False):
                nc_ = Y_GROUPS[g][1] * P
                act.wait_ge(at_loaded[b], 8 * (J - b) + 16)
                if not first:
                    act.wait_ge(p2_step, J - 1)
                nc.scalar.activation(hl[:, b, 0, 0:nc_], at[:, b, 0:nc_], ACT.Copy, scale=A_SCALE).then_inc(athi_ok, 1)

            def macro(g, m, first, norm_t=None, x1_from=None):
                for s in range(STEPS):
                    b = s % 2
                    if s != 1 or x1_from is None:
                        high(g, STEPS * m + s, b, first and s < 2)
                    if isinstance(m, int) and m == 8 and s == LAG:
                        act.wait_ge(x1_stored, 32)
                    if s >= LAG:
                        store_w(later(m, s - LAG), (s - LAG) % 2)
                    elif first:
                        store_w(early(ROUNDS - 1, s - LAG + EARLY), (s - LAG) % 2)
                    else:
                        store_w(later(m - 1, s - LAG + KINDS), (s - LAG) % 2)
                    sums(later(m, s), b)
                    if s == 0 and norm_t is not None:
                        for e in range(2):
                            h_high(norm_t + e, e)
                    if s == 0 and x1_from is not None:
                        high(g, STEPS * m + 1, 1)
                        store_x1(g - 1, x1_from)
            def h_high(t, b):
                act.wait_ge(h_ok, t + 1)
                if not (isinstance(t, int) and t < 2):
                    act.wait_ge(h_stored[b], slot_count(t, b))
                nc.scalar.activation(hb[:, b, 0:D], xb[:, b, :], ACT.Copy).then_inc(hhi_ok, 1)

            def store_x1(g, xg):
                t0, count = Y_GROUPS[g]
                act.wait_ge(x1_ok, t0 + count)
                act.dma_start(x1_t[:, t0:t0 + count, :], xg).then_inc(x1_stored, 16)

            macro(0, 0, True)
            with act.Fori(1, 4) as m:
                macro(0, m, False)
            macro(1, 4, False, x1_from=xg_r[:, 0:6, :])
            macro(1, 5, False)
            with act.Fori(6, 8) as m:
                macro(1, m, False, 2 * m - 12)
            macro(2, 8, False, 4, x1_from=xg_r[:, 6:12, :])
            macro(2, 9, False)
            with act.Fori(10, MACROS) as m:
                macro(2, m, False, 2 * m - 14)
            act.wait_ge(ln_var, 24)
            for s in range(KINDS - LAG, KINDS):
                store_w(later(MACROS - 1, s), s % 2)
            for b in range(2):
                h_high(10 + b, b)
            store_x1(2, xg_z)

            def columns(n, b, lead):
                act.wait_ge(tr2_ok, n + 1)
                if lead >= 2:
                    act.wait_ge(m1_ok, n - 1)
                nc.scalar.activation(ht[:, b, :], ps_ht, ACT.Copy).then_inc(ht_ok, 1)

            def tile(n, b, lead):
                for half in range(2):
                    act.wait_ge(pre_ok, 2 * n + half + 1)
                    if lead >= 1:
                        act.wait_ge(h1lo_ok, 2 * n + half - 1)
                    cols = slice(half * 512, half * 512 + 512)
                    nc.scalar.activation(h1[:, cols], pre[:, cols], ACT.Silu).then_inc(h1_ok, 1)
                    if lead >= 2:
                        act.wait_ge(m2_ok, n - 1)
                    act.wait_ge(h1_ok, 2 * n + half + 1)
                    nc.scalar.activation(h1hl[:, b, 0, cols], h1[:, cols], ACT.Copy, scale=U_SCALE).then_inc(h1hi_ok, 1)

            def shared_store(n, b):
                act.wait_ge(y_ok, n + 1)
                act.dma_start(base_dram[ds(n * P, P), 0:D], base_t[:, b, 0:D]).then_inc(y_stored[b], 16)

            columns(0, 0, 0)
            columns(1, 1, 1)
            tile(0, 0, 0)
            columns(2, 0, 2)
            tile(1, 1, 1)
            shared_store(0, 0)
            for b in range(2):
                h_high(12 + b, b)
            for n in range(2, 6):
                columns(n + 1, (n + 1) % 2, 2)
                tile(n, n % 2, 2)
                shared_store(n - 1, (n - 1) % 2)
                if n == 4:
                    for b in range(2):
                        h_high(14 + b, b)
            with act.Fori(3, NT // 2 - 1) as i:
                for b in range(2):
                    columns(2 * i + b + 1, 1 - b, 2)
                    tile(2 * i + b, b, 2)
                    shared_store(2 * i + b - 1, 1 - b)
            columns(NT - 1, 1, 2)
            tile(NT - 2, 0, 2)
            shared_store(NT - 3, 1)
            tile(NT - 1, 1, 2)
            shared_store(NT - 2, 0)
            shared_store(NT - 1, 1)
            act.wait_ge(l_ok, NT + 1)
            nc.scalar.activation(ex[:, :, :], lg[:, :, :], ACT.Exp).then_inc(e_ok, 1)
            act.wait_ge(gate_ok, 1)
            act.dma_start(base_dram[0:N, D:D + 1].rearrange("(t p) a -> p (t a)", p=P), gate,
                          allow_slow_non_contiguous=True).then_inc(gate_stored, 16)
            columns(NT, 0, 2)
            with act.Fori(NT // 2, TILES // 2) as i:
                for b in range(2):
                    columns(2 * i + b + 1, 1 - b, 2)
                    tile(2 * i + b, b, 2)
            tile(TILES - 1, 0, 2)

        @block.vector
        def _(dve):
            def chained(ins, s, value):
                ins.then_inc(s, 1)
                dve.wait_ge(s, value)

            dve.wait_ge(consts, 8)

            def x_stats(batch, s):
                t = UNROLL * batch + s
                chained(nc.vector.bn_stats(st4[:, s, :], xhat[:, ds(t, 1), :].rearrange("p a d -> p (a d)")),
                        xh_seq, XOPS * batch + 2 * s + 1)
                dve.sem_inc(dve_waits, 1)
                nc.vector.bn_aggr(mv4[:, s, :], st4[:, s, :]).then_inc(xh_seq, 1)

            def x_normed(batch):
                dve.wait_ge(xh_seq, XOPS * batch + 2 * UNROLL)
                nc.vector.tensor_scalar(r4[:, 0, :], mv4[:, :, 1], EPS, None, ALU.add).then_inc(xv_ok, 1)
                dve.wait_ge(xr_ok, batch + 1)
                chained(nc.vector.tensor_scalar(r4[:, 2, :], r4[:, 1, :], U_SCALE, None, ALU.mult),
                        xh_seq, XOPS * batch + 2 * UNROLL + 1)
                for s in range(UNROLL):
                    xs = xhat[:, ds(UNROLL * batch + s, 1), :].rearrange("p a d -> p (a d)")
                    nc.vector.tensor_scalar(xs, xs, mv4[:, s, 0:1], r4[:, 2, s:s + 1],
                                            ALU.subtract, ALU.mult).then_inc(xh_seq, 1)

            def sum_s(i, s):
                j = UNROLL * i + s
                dve.wait_ge(a_loaded[s], 16 * i + 16)
                dve.wait_ge(t_loaded[s % 2], 32 * i + 16 * (s // 2) + 16)
                nc.vector.tensor_tensor(a_in[:, s, 0:G0_COLS], a_in[:, s, 0:G0_COLS], t_in[:, s % 2, 0:G0_COLS],
                                        ALU.add).then_inc(sum_ok, 1)

            def finish(i, s):
                j = UNROLL * i + s
                b = s % 2
                raw_deg, deg, safe, root = [dv[:, b, k:k + 1] for k in range(4)]
                n = [0]

                def step(ins):
                    n[0] += 1
                    chained(ins, deg_seq, DEG * j + n[0])

                dve.wait_ge(shi_ok, 2 * j + 2)
                step(nc.vector.tensor_tensor(raw_deg, rs[:, b, 0:1], rs[:, b, 1:2], ALU.add))
                step(nc.vector.tensor_scalar(deg, raw_deg, 0.5 / A_SCALE, 1.0, ALU.mult, ALU.add))
                nc.vector.tensor_scalar(safe, deg, 1e-30, None, ALU.max).then_inc(deg_ok, 1)
                nc.vector.scalar_tensor_tensor(out=hl_z[:, b, 1, :], in0=a_in[:, s, 0:G0_COLS], scalar=A_SCALE,
                                               in1=hl_z[:, b, 0, :], op0=ALU.mult, op1=ALU.subtract)
                nc.vector.scalar_tensor_tensor(out=s_lo[:, ds(j * REST, REST)], in0=a_in[:, s, G0_COLS:N],
                                               scalar=A_SCALE, in1=s_hi[:, ds(j * REST, REST)], op0=ALU.mult,
                                               op1=ALU.subtract).then_inc(slo_ok, 1)
                dve.wait_ge(deg_root, j + 1)
                step(nc.vector.scalar_tensor_tensor(out=dinv[:, ds(j, 1)], in0=deg, scalar=0.0, in1=root,
                                                    op0=ALU.is_gt, op1=ALU.mult))
                dve.wait_ge(xh_seq, XOPS * i + XOPS)
                xj = xhat[:, ds(j, 1), :].rearrange("p a d -> p (a d)")
                chained(nc.vector.tensor_scalar(u_hi[:, ds(j * D, D)], xj, dinv[:, ds(j, 1)], None, ALU.mult), u_ok, 2 * j + 1)
                nc.vector.scalar_tensor_tensor(out=u_lo[:, ds(j * D, D)], in0=xj, scalar=dinv[:, ds(j, 1)],
                                               in1=u_hi[:, ds(j * D, D)], op0=ALU.mult,
                                               op1=ALU.subtract).then_inc(u_ok, 1)

            def stream_round(i, first, last):
                for s in range(UNROLL):
                    if first and s == 0:
                        finish(i, s)
                    if s < UNROLL - 1:
                        sum_s(i, s + 1)
                    elif not last:
                        sum_s(i + 1, 0)
                    if not (first and s == 0):
                        finish(i, s)
                    if not last:
                        if s == 0:
                            dve.wait_ge(x_in[1], 16 * i + 16)
                        x_stats(i + 1, s)
                if not last:
                    x_normed(i + 1)

            dve.wait_ge(x_in[0], 16)
            for s in range(UNROLL):
                x_stats(0, s)
            x_normed(0)
            sum_s(0, 0)
            stream_round(0, True, False)
            with dve.Fori(1, NT // UNROLL - 1) as i:
                stream_round(i, False, False)
            stream_round(NT // UNROLL - 1, False, True)
            nc.vector.tensor_scalar(dinvz[:, :], dinv[:, :], 0.5 / A_SCALE, None, ALU.mult).then_inc(dinvz_ok, 1)

            def z_low(g):
                t0, count, banks = Z_GROUPS[g]
                dve.wait_ge(z_acc, g + 1)
                for k in range(count):
                    dve.wait_ge(zhi_ok, t0 + k + 1)
                    nc.vector.scalar_tensor_tensor(out=z_lo[:, t0 + k, :], in0=acc[banks[k]],
                                                   scalar=dinvz[:, t0 + k:t0 + k + 1], in1=z_hi[:, t0 + k, :],
                                                   op0=ALU.mult, op1=ALU.subtract).then_inc(zlo_ok, 1)

            def ternary(chunk, b, base, done, first=False):
                q, kind, c = chunk
                n = [done]

                def step(ins):
                    n[0] += 1
                    chained(ins, w_seq, base + n[0])

                dve.wait_ge(abs_ok, 2 * q + 2)
                if kind == 1:
                    k, width, scale = 2, D, s1[:, ds(2 * c, 2)]
                    step(nc.vector.tensor_scalar(scale, asum[:, b, 0:2], 1.0 / width, QMIN, ALU.mult, ALU.max))
                else:
                    k, width, scale = 1, F, s2[:, ds(c, 1)]
                    step(nc.vector.tensor_scalar(thr[:, b, 0, 1:2], asum[:, b, 0:1], asum[:, b, 1:2], None, ALU.add))
                    step(nc.vector.tensor_scalar(scale, thr[:, b, 0, 1:2], 1.0 / width, QMIN, ALU.mult, ALU.max))
                nc.vector.tensor_scalar(thr[:, b, 0, 0:k], scale, 0.5, None, ALU.mult)
                step(nc.vector.tensor_scalar(thr[:, b, 1, 0:k], scale, -0.5, None, ALU.mult))
                if not first:
                    dve.wait_ge(tr_ok, q - 1)
                for a in range(k):
                    cols = slice(a * width, (a + 1) * width)
                    step(nc.vector.tensor_scalar(tern[:, b, cols], raw[:, b, cols], thr[:, b, 1, a:a + 1], None, ALU.is_lt))
                for a in range(k):
                    cols = slice(a * width, (a + 1) * width)
                    ins = nc.vector.scalar_tensor_tensor(out=tern[:, b, cols], in0=raw[:, b, cols],
                                                         scalar=thr[:, b, 0, a:a + 1], in1=tern[:, b, cols],
                                                         op0=ALU.is_gt, op1=ALU.subtract)
                    if a == k - 1:
                        ins.then_inc(tern_ok, 1)
                    else:
                        step(ins)
                return n[0]

            def early_round(rnd):
                done = 0
                for s in range(EARLY):
                    done = ternary(early(rnd, s), s % 2, EARLY_OPS * rnd, done, rnd == 0 and s < 2)

            z_low(0)
            early_round(0)
            early_round(1)
            z_low(1)
            early_round(2)
            early_round(3)
            z_low(2)

            def norm_part(part, t, b):
                if isinstance(t, int) and t >= 12:
                    x1 = xg_z[:, t - 12, :]
                else:
                    x1 = xg_r[:, ds(t, 1), :].rearrange("p a d -> p (a d)")
                x1b, base = xb[:, b, :], 5 * (t - b)
                mean, var = mvb[:, b, 0:1], mvb[:, b, 1:2]
                if part == 0:
                    src = x1
                    base = base + 2 * b
                else:
                    dve.wait_ge(ln_root, 2 * (t - b) + 2 * (part - 1) + b + 1)
                    src = x1b
                    ins = nc.vector.tensor_scalar(x1b, x1 if part == 1 else x1b, mean, rb[:, b, 1:2],
                                                  ALU.subtract, ALU.mult)
                    if part == 2:
                        ins.then_inc(ln_normed, 1)
                        return
                    base = base + 4 + 3 * b + 1
                    chained(ins, ln_seq, base)
                chained(nc.vector.bn_stats(stb[:, b, :], src), ln_seq, base + 1)
                dve.sem_inc(dve_waits, 1)
                chained(nc.vector.bn_aggr(mvb[:, b, :], stb[:, b, :]), ln_seq, base + 2)
                nc.vector.tensor_scalar(rb[:, b, 0:1], var, EPS, None, ALU.add).then_inc(ln_var, 1)

            def norm_parts(part, t):
                for b in range(2):
                    norm_part(part, t + b, b)

            def low(g, J, b):
                nc_ = Y_GROUPS[g][1] * P
                dve.wait_ge(athi_ok, J + 1)
                nc.vector.scalar_tensor_tensor(out=hl[:, b, 1, 0:nc_], in0=at[:, b, 0:nc_], scalar=A_SCALE,
                                               in1=hl[:, b, 0, 0:nc_], op0=ALU.mult, op1=ALU.subtract).then_inc(atlo_ok, 1)

            def macro(g, m, norm_t=None, x1_from=None):
                done = 0
                for s in range(STEPS):
                    b = s % 2
                    if s != 1 or x1_from is None:
                        low(g, STEPS * m + s, b)
                    if s == 0 and x1_from is not None:
                        x1_of_group(g - 1, x1_from)
                        low(g, STEPS * m + 1, 1)
                    done = ternary(later(m, s), b, ROUNDS * EARLY_OPS + WOPS * m, done)
                    if norm_t is not None and s < 3:
                        norm_parts(s, norm_t)

            def x1_of_group(g, xg):
                t0, count = Y_GROUPS[g]
                x_rows = xg if g < 2 else raw[:, :, :].rearrange("p b (t d) -> p (b t) d", d=D)
                dve.wait_ge(xg_in[g // 2], 16)
                dve.wait_ge(p2_step, NT * (g + 1))
                for k in range(count):
                    nc.vector.scalar_tensor_tensor(out=xg[:, k, :], in0=acc[k], scalar=1.0 / (A_SCALE * U_SCALE),
                                                   in1=x_rows[:, k, :], op0=ALU.mult, op1=ALU.add).then_inc(x1_ok, 1)

            macro(0, 0)
            with dve.Fori(1, 4) as m:
                macro(0, m)
            macro(1, 4, x1_from=xg_r[:, 0:6, :])
            with dve.Fori(5, 8) as m:
                macro(1, m, 2 * m - 10)
            macro(2, 8, x1_from=xg_r[:, 6:12, :])
            with dve.Fori(9, 12) as m:
                macro(2, m, 2 * m - 12)
            x1_of_group(2, xg_z)

            r_n = [0]

            def rstep(ins):
                r_n[0] += 1
                chained(ins, r_seq, r_n[0])

            dve.wait_ge(small_in, 48)
            rstep(nc.vector.tensor_copy(r3[:, :, 0, :], rt[:, :, :]))
            rstep(nc.vector.tensor_tensor(rtr[:, :, :], rt[:, :, :], r3[:, :, 0, :], ALU.subtract))
            rstep(nc.vector.tensor_copy(r3[:, :, 1, :], rtr[:, :, :]))
            rstep(nc.vector.tensor_tensor(rtr[:, :, :], rtr[:, :, :], r3[:, :, 1, :], ALU.subtract))
            nc.vector.tensor_copy(r3[:, :, 2, :], rtr[:, :, :]).then_inc(r3_ok, 1)

            LO = 4

            def tile(n, b, shared, lead, u):
                for half in range(2):
                    dve.wait_ge(m1_ok, n + 1)
                    if lead >= 1:
                        dve.wait_ge(h1_ok, 2 * n + half - 1)
                    nc.vector.tensor_tensor(
                        pre[:, half * 512:(half + 1) * 512].rearrange("p (f t) -> p f t", f=4),
                        ps_h[b][half][:, :].rearrange("p (f t) -> p f t", f=4),
                        s1[:, ds(u * FB + half * 4, 4)].rearrange("p (f a) -> p f a", a=1).to_broadcast([P, 4, P]),
                        ALU.mult).then_inc(pre_ok, 1)
                if shared:
                    route(n, b)
                for half in range(2):
                    dve.wait_ge(h1hi_ok, 2 * n + half + 1)
                    cols = slice(half * 512, half * 512 + 512)
                    nc.vector.scalar_tensor_tensor(out=h1hl[:, b, 1, cols], in0=h1[:, cols], scalar=U_SCALE,
                                                   in1=h1hl[:, b, 0, cols], op0=ALU.mult,
                                                   op1=ALU.subtract).then_inc(h1lo_ok, 1)

            def route(n, b):
                k = [0]

                def step(ins):
                    k[0] += 1
                    chained(ins, l_seq, LO * n + k[0])

                row = lambda v: v[:, ds(n, 1), :].rearrange("p a e -> p (a e)")
                dve.wait_ge(r_ok, n + 1)
                step(nc.vector.tensor_copy(lg2[:, 0, :], ps_r[:, 2 * E:3 * E]))
                step(nc.vector.tensor_tensor(lg2[:, 1, :], ps_r[:, E:2 * E], lg2[:, 0, :], ALU.add))
                step(nc.vector.tensor_tensor(row(lg), ps_r[:, 0:E], lg2[:, 1, :], ALU.add))
                step(nc.vector.tensor_reduce(mx[:, ds(n, 1)], row(lg), AX_X, ALU.max))
                nc.vector.tensor_scalar(row(hot), row(lg), mx[:, ds(n, 1)], None, ALU.is_equal).then_inc(l_ok, 1)

            def output(n, b, shared, lead):
                dve.wait_ge(m2_ok, n + 1)
                dve.wait_ge(s2_in[b], slot_count(n, b) + 16)
                if shared:
                    dve.wait_ge(base_in[b], slot_count(n, b) + 16)
                else:
                    dve.wait_ge(base_got[b], slot_count(n - NT, b) + 16)
                    if lead >= 2:
                        dve.wait_ge(out_stored[b], slot_count(n - NT, b))
                chained(nc.vector.scalar_tensor_tensor(out=s2bc[:, b, :], in0=ps_y[b][:, :], scalar=1.0 / U_SCALE,
                                                       in1=s2bc[:, b, :], op0=ALU.mult, op1=ALU.mult), y_seq, n + 1)
                if shared:
                    nc.vector.tensor_tensor(base_t[:, b, 0:D], base_t[:, b, 0:D], s2bc[:, b, :],
                                            ALU.add).then_inc(y_ok, 1)
                else:
                    nc.vector.scalar_tensor_tensor(out=o_t[:, b, :], in0=s2bc[:, b, :], scalar=base_t[:, b, D:D + 1],
                                                   in1=base_t[:, b, 0:D], op0=ALU.mult, op1=ALU.add).then_inc(y_ok, 1)

            tile(0, 0, True, 0, 0)
            norm_parts(0, 12)
            tile(1, 1, True, 1, 0)
            norm_parts(1, 12)
            output(0, 0, True, 0)
            norm_parts(2, 12)
            tile(2, 0, True, 2, 0)
            output(1, 1, True, 1)
            tile(3, 1, True, 2, 0)
            norm_parts(0, 14)
            output(2, 0, True, 2)
            norm_parts(1, 14)
            tile(4, 0, True, 2, 0)
            norm_parts(2, 14)
            output(3, 1, True, 2)
            tile(5, 1, True, 2, 0)
            output(4, 0, True, 2)
            with dve.Fori(3, NT // 2) as i:
                tile(2 * i, 0, True, 2, 0)
                output(2 * i - 1, 1, True, 2)
                tile(2 * i + 1, 1, True, 2, 0)
                output(2 * i, 0, True, 2)

            q = [0]

            def rs_(ins):
                q[0] += 1
                chained(ins, rt_seq, q[0])

            dve.wait_ge(l_ok, NT)
            rs_(nc.vector.memset(rank[:, :, 0:1], 0.0))
            for e in range(1, E):
                rs_(nc.vector.tensor_tensor(rank[:, :, e:e + 1], rank[:, :, e - 1:e], hot[:, :, e - 1:e], ALU.max))
            rs_(nc.vector.tensor_tensor(seen[:, :, :], hot[:, :, :], rank[:, :, :], ALU.is_gt))
            nc.vector.tensor_copy(hot16[:, :, :], seen[:, :, :]).then_inc(hot_ok, 1)
            nc.vector.tensor_tensor(lg[:, :, :], lg[:, :, :],
                                    mx.rearrange("p (t a) -> p t a", a=1).to_broadcast([P, NT, E]),
                                    ALU.subtract).then_inc(l_ok, 1)
            output(NT - 1, 1, True, 2)
            dve.wait_ge(cnt_ok, 1)
            nt_e = NT * E
            rs_(nc.vector.tensor_copy(rank[:, :, :], ps_r[:, 0:nt_e].rearrange("p (t e) -> p t e", e=E)))
            rs_(nc.vector.memset(cnt[:, 0, :], 0.0))
            for t in range(NT):
                rs_(nc.vector.tensor_tensor(cnt[:, t + 1, :], ps_r[:, nt_e + t * E:nt_e + (t + 1) * E], cnt[:, t, :], ALU.add))
            rs_(nc.vector.tensor_tensor(rank[:, :, :], rank[:, :, :], cnt[:, 0:NT, :], ALU.add))
            rs_(nc.vector.tensor_scalar(til[:, 0, :], cnt[:, NT, :], float(P - 1), None, ALU.add))
            rs_(nc.vector.tensor_copy(tili[:, 0, :], til[:, 0, :]))
            rs_(nc.vector.tensor_scalar(tili[:, 1, :], tili[:, 0, :], 7, None, ALU.logical_shift_right))
            rs_(nc.vector.tensor_copy(til[:, 1, :], tili[:, 1, :]))
            rs_(nc.vector.memset(til[:, 2, 0:1], 0.0))
            for e in range(1, E):
                rs_(nc.vector.tensor_tensor(til[:, 2, e:e + 1], til[:, 2, e - 1:e], til[:, 1, e - 1:e], ALU.add))
            rs_(nc.vector.tensor_tensor(sel[:, :, :], seen[:, :, :], rank[:, :, :], ALU.mult))
            rs_(nc.vector.tensor_reduce(rr[:, 0, :], sel[:, :, :], AX_X, ALU.add))
            rs_(nc.vector.tensor_tensor(sel[:, :, :], seen[:, :, :],
                                        til[:, 2:3, :].to_broadcast([P, NT, E]), ALU.mult))
            rs_(nc.vector.tensor_reduce(rr[:, 1, :], sel[:, :, :], AX_X, ALU.add))
            rs_(nc.vector.tensor_copy(ri[:, 0, :], rr[:, 0, :]))
            rs_(nc.vector.tensor_scalar(ri[:, 1, :], ri[:, 0, :], P - 1, None, ALU.bitwise_and))
            rs_(nc.vector.tensor_scalar(ri[:, 2, :], ri[:, 0, :], 7, None, ALU.logical_shift_right))
            rs_(nc.vector.tensor_copy(rr[:, 2, :], ri[:, 1, :]))
            rs_(nc.vector.tensor_copy(rr[:, 0, :], ri[:, 2, :]))
            rs_(nc.vector.scalar_tensor_tensor(out=rr[:, 2, :], in0=rr[:, 2, :], scalar=float(ROUTED_TILES),
                                               in1=rr[:, 0, :], op0=ALU.mult, op1=ALU.add))
            rs_(nc.vector.tensor_tensor(rr[:, 2, :], rr[:, 2, :], rr[:, 1, :], ALU.add))
            nc.vector.tensor_copy(ri[:, 3, :], rr[:, 2, :]).then_inc(slots_ok, 1)
            dve.wait_ge(e_ok, 1)
            rs_(nc.vector.tensor_reduce(se, ex[:, :, :], AX_X, ALU.add))
            nc.vector.reciprocal(gate, se).then_inc(gate_ok, 1)
            dve.wait_ge(consts, 8)
            rs_(nc.vector.memset(tacc[:, :], 0.0))
            for e in range(E):
                rs_(nc.vector.scalar_tensor_tensor(out=tacc[:, :], in0=tn[:, :], scalar=til[0:1, 2, e:e + 1],
                                                   in1=tacc[:, :], op0=ALU.is_ge, op1=ALU.add))
            nc.vector.tensor_copy(unit[:, NT:TILES], tacc[:, :]).then_inc(unit_ok, 1)
            dve.wait_ge(unit_ok, 1)

            def load_unit(n):
                return dve.value_load(unit[0:1, ds(n, 1)], min_val=0, max_val=UNITS - 1)

            tile(NT, 0, False, 2, load_unit(NT))
            tile(NT + 1, 1, False, 2, load_unit(NT + 1))
            output(NT, 0, False, 0)
            tile(NT + 2, 0, False, 2, load_unit(NT + 2))
            output(NT + 1, 1, False, 1)
            with dve.Fori(NT // 2 + 1, TILES // 2 - 1) as i:
                tile(2 * i + 1, 1, False, 2, load_unit(2 * i + 1))
                output(2 * i, 0, False, 2)
                tile(2 * i + 2, 0, False, 2, load_unit(2 * i + 2))
                output(2 * i + 1, 1, False, 2)
            tile(TILES - 2, 1, False, 2, load_unit(TILES - 2))
            output(TILES - 3, 0, False, 2)
            tile(TILES - 1, 0, False, 2, load_unit(TILES - 1))
            output(TILES - 2, 1, False, 2)
            output(TILES - 1, 0, False, 2)

        @block.tensor
        def _(pe):
            def parts(dst, a_hi, a_lo, b_hi, b_lo, start):
                nc.tensor.matmul(dst, a_hi, b_hi, start=start, stop=False, skip_group_check=True)
                nc.tensor.matmul(dst, a_hi, b_lo, start=False, stop=False, skip_group_check=True)
                return nc.tensor.matmul(dst, a_lo, b_hi, start=False, stop=False, skip_group_check=True)

            def block_j(j, s, start):
                pe.wait_ge(u_ok, 2 * j + 2)
                for k in range(Z_GROUPS[0][1]):
                    c = slice(k * P, (k + 1) * P)
                    last = parts(acc[k], hl_z[:, s % 2, 0, c], hl_z[:, s % 2, 1, c], u_hi[:, ds(j * D, D)],
                                 u_lo[:, ds(j * D, D)], start)
                last.then_inc(p1_step, 1)

            pe.wait_ge(consts, 8)
            def add_identity(g, u, start, tiles=None, left=()):
                t0, count, banks = Z_GROUPS[g]
                for k in tiles or range(count):
                    t = t0 + k
                    if k < len(left):
                        pe.wait_ge(zlo_ok, left[k])
                    last = nc.tensor.matmul(acc[banks[k]], ident2[:, :], u[:, t * D:(t + 1) * D], start=start,
                                            stop=False, skip_group_check=True)
                return last

            def turn_w(chunk, b, first):
                q, kind, c = chunk
                pe.wait_ge(tern_ok, q + 1)
                if not first:
                    pe.wait_ge(wt_ok, q - 1)
                for k in range(8):
                    dst = (k % 4) * 2 + k // 4 if kind == 1 else k
                    last = nc.tensor.transpose(pst[b][:, dst * P:(dst + 1) * P], tern[:, b, k * P:(k + 1) * P], ident[:, :])
                last.then_inc(tr_ok, 1)

            assert Z_GROUPS[0][1] <= 2 * UNROLL
            for j in range(2 * UNROLL):
                block_j(j, j % UNROLL, j == 0)
            add_identity(0, u_hi, False)
            add_identity(0, u_lo, False, range(Z_GROUPS[0][1] - 1))
            with pe.Fori(2, NT // UNROLL) as i:
                for s in range(UNROLL):
                    block_j(UNROLL * i + s, s, False)
            add_identity(0, u_lo, False, (Z_GROUPS[0][1] - 1,)).then_inc(z_acc, 1)

            def early_round(g, rnd, first):
                t0, count, banks = Z_GROUPS[g]
                for k8 in range(ROUND_STEPS):
                    j = ROUND_STEPS * (rnd - 2 * (g - 1)) + k8
                    for k in range(count):
                        a0 = j * REST + ((t0 + k) * P - G0_COLS)
                        parts(acc[banks[k]], s_hi[:, ds(a0, P)], s_lo[:, ds(a0, P)], u_hi[:, ds(j * D, D)],
                              u_lo[:, ds(j * D, D)], False)
                    if k8 < EARLY and not (first and k8 == 0):
                        turn_w(early(rnd, k8 - 1) if k8 else early(rnd - 1, EARLY - 1), (k8 - 1) % 2, first and k8 <= 2)

            add_identity(1, u_hi, True, left=(1, 2, 3, 4))
            early_round(1, 0, True)
            early_round(1, 1, False)
            add_identity(1, u_lo, False).then_inc(z_acc, 1)
            add_identity(2, u_hi, True, left=(9, 10))
            with pe.Fori(2, 4) as rnd:
                early_round(2, rnd, False)
            add_identity(2, u_lo, False).then_inc(z_acc, 1)

            def macro(g, m, first):
                t0, count = Y_GROUPS[g]
                for s in range(STEPS):
                    b = s % 2
                    late_turn = first and g and s == 1
                    if s:
                        if not late_turn:
                            turn_w(later(m, s - 1), (s - 1) % 2, False)
                    elif isinstance(m, int) and m == 0:
                        turn_w(early(ROUNDS - 1, EARLY - 1), 1, False)
                    else:
                        turn_w(later(m - 1, KINDS - 1), 1, False)
                    pe.wait_ge(atlo_ok, STEPS * m + s + 1)
                    j = STEPS * (m - g * NT // STEPS) + s
                    zj_hi = z_hi[:, ds(j, 1), :].rearrange("p a d -> p (a d)")
                    zj_lo = z_lo[:, ds(j, 1), :].rearrange("p a d -> p (a d)")
                    for k in range(count):
                        if first and s == 0 and g == 0 and k in Z_GROUPS[2][2]:
                            pe.wait_ge(zlo_ok, 13 + Z_GROUPS[2][2].index(k))
                        if first and s == 0 and g:
                            pe.wait_ge(x1_ok, Y_GROUPS[g - 1][0] + k + 1)
                        c = slice(k * P, (k + 1) * P)
                        last = parts(acc[k], hl[:, b, 0, c], hl[:, b, 1, c], zj_hi, zj_lo, first and s == 0)
                    last.then_inc(p2_step, 1)
                    if late_turn:
                        turn_w(later(m, 0), 0, False)

            for g in range(3):
                m0 = g * NT // STEPS
                macro(g, m0, True)
                with pe.Fori(m0 + 1, m0 + NT // STEPS) as m:
                    macro(g, m, False)
            turn_w(later(MACROS - 1, KINDS - 1), 1, False)

            def rows_to_columns(n, b, shared):
                if shared:
                    pe.wait_ge(hrow_in[b], slot_count(n, b) + 16)
                else:
                    pe.wait_ge(hrow_got[b], slot_count(n - NT, b) + 16)
                if not (isinstance(n, int) and n == 0):
                    pe.wait_ge(ht_ok, n)
                for k in range(2 * DB):
                    last = nc.tensor.transpose(ps_ht[:, k * P:(k + 1) * P], hrow[:, b, k * P:(k + 1) * P], ident[:, :])
                last.then_inc(tr2_ok, 1)

            def first_product(n, b, lead, u):
                pe.wait_ge(ht_ok, n + 1)
                if lead >= 2:
                    pe.wait_ge(pre_ok, 2 * n - 2)
                for f in range(FB):
                    for d in range(DB):
                        w = w1t[:, ds(u * (4 * CHUNK) + (f // 2) * CHUNK + d * 2 * P + (f % 2) * P, P)]
                        for h in range(2):
                            c = (h * DB + d) * P
                            last = nc.tensor.matmul(ps_h[b][f // 4][:, (f % 4) * P:(f % 4 + 1) * P], w,
                                                    ht[:, b, c:c + P], start=(f % 4 == 0 and d == 0 and h == 0),
                                                    stop=False, skip_group_check=True)
                last.then_inc(m1_ok, 1)

            def logits(n, b):
                if not (isinstance(n, int) and n == 0):
                    pe.wait_ge(l_ok, n)
                for d in range(DB):
                    for h in range(2):
                        c = (h * DB + d) * P
                        last = nc.tensor.matmul(ps_r[:, 0:3 * E], ht[:, b, c:c + P],
                                                r3[:, d, :, :].rearrange("p a e -> p (a e)"),
                                                start=(d == 0 and h == 0), stop=False, skip_group_check=True)
                last.then_inc(r_ok, 1)

            def second_product(n, b, lead, u):
                pe.wait_ge(h1lo_ok, 2 * n + 2)
                if lead >= 2:
                    pe.wait_ge(y_ok, n - 1)
                for f in range(FB):
                    w = w2t[:, ds(u * (4 * CHUNK), 4 * CHUNK)].rearrange("p (d f c) -> p f d c", d=DB, f=FB)[:, f, :, :]
                    for h in range(2):
                        last = nc.tensor.matmul(ps_y[b][:, :].rearrange("p (d c) -> p d c", d=DB),
                                                h1hl[:, b, h, f * P:(f + 1) * P], w,
                                                start=(f == 0 and h == 0), stop=False, skip_group_check=True)
                last.then_inc(m2_ok, 1)

            pe.wait_ge(wt_ok, 2 * CHUNKS)
            def shared_turn(n, b, lead, second=True):
                first_product(n, b, lead, 0)
                rows_to_columns(n + 1, 1 - b, True)
                logits(n, b)
                if second:
                    second_product(n - 1, 1 - b, 0 if lead < 2 or lead == 3 else 2, 0)

            rows_to_columns(0, 0, True)
            pe.wait_ge(x1_ok, NT)
            pe.wait_ge(r3_ok, 1)
            shared_turn(0, 0, 0, False)
            shared_turn(1, 1, 1)
            shared_turn(2, 0, 3)
            shared_turn(3, 1, 2)
            with pe.Fori(2, NT // 2 - 1) as i:
                for b in range(2):
                    shared_turn(2 * i + b, b, 2)
            shared_turn(NT - 2, 0, 2)
            first_product(NT - 1, 1, 2, 0)
            logits(NT - 1, 1)
            second_product(NT - 2, 0, 2, 0)
            second_product(NT - 1, 1, 2, 0)

            pe.wait_ge(hot_ok, 1)
            hot_all = hot16[:, :, :].rearrange("p t e -> p (t e)")
            nc.tensor.matmul(ps_r[:, 0:NT * E], tri[:, :], hot_all, start=True, stop=True, skip_group_check=True)
            nc.tensor.matmul(ps_r[:, NT * E:2 * NT * E], ones[:, :], hot_all, start=False, stop=True,
                             skip_group_check=True).then_inc(cnt_ok, 1)

            pe.wait_ge(unit_ok, 1)

            def load_unit(n):
                return pe.value_load(unit[0:1, ds(n, 1)], min_val=0, max_val=UNITS - 1)

            def routed_turn(n, b):
                first_product(n, b, 2, load_unit(n))
                rows_to_columns(n + 1, 1 - b, False)
                second_product(n - 1, 1 - b, 2, load_unit(n - 1))

            rows_to_columns(NT, 0, False)
            first_product(NT, 0, 2, load_unit(NT))
            rows_to_columns(NT + 1, 1, False)
            routed_turn(NT + 1, 1)
            with pe.Fori(NT // 2 + 1, TILES // 2) as i:
                for b in range(2):
                    routed_turn(2 * i + b, b)
            first_product(TILES - 1, 0, 2, load_unit(TILES - 1))
            second_product(TILES - 2, 1, 2, load_unit(TILES - 2))
            second_product(TILES - 1, 0, 2, load_unit(TILES - 1))


def kernel(x, adj, L0_ffn_shared_w1, L0_ffn_shared_w2, L0_ffn_expert_w1, L0_ffn_expert_w2, L0_ffn_router_w,
           L0_ffn_ln_gamma, L0_ffn_ln_beta):
    import numpy as np
    import concourse.bacc as bacc
    from concourse.bass_utils import run_bass_kernel_spmd

    arrays = {
        "x": np.ascontiguousarray(x),
        "adj": np.ascontiguousarray(adj),
        "adj_t": np.ascontiguousarray(np.asarray(adj).T),
        "w1": np.concatenate([np.asarray(L0_ffn_shared_w1)[None], np.asarray(L0_ffn_expert_w1)]),
        "w2": np.concatenate([np.asarray(L0_ffn_shared_w2)[None], np.asarray(L0_ffn_expert_w2)]),
        "router_t": np.ascontiguousarray(np.asarray(L0_ffn_router_w).T),
        "gamma": np.ascontiguousarray(L0_ffn_ln_gamma),
        "beta": np.ascontiguousarray(L0_ffn_ln_beta),
    }
    nc = bacc.Bacc("TRN2", target_bir_lowering=False, num_devices=1, dynamic_dma_scratch_size=8192)
    args = [nc.dram_tensor(f"in_{k}", v.shape, mybir.dt.from_np(v.dtype), kind="ExternalInput").ap()
            for k, v in arrays.items()]
    out = nc.dram_tensor("out", (N, D), F32, kind="ExternalOutput").ap()
    build(nc, *args, out)
    r = run_bass_kernel_spmd(nc, [{f"in_{k}": v for k, v in arrays.items()}], core_ids=[0])
    return r.results[0]["out"]
```

```python
from contextlib import ExitStack

import concourse.bass as bass
from concourse import mybir

ALU = mybir.AluOpType
ACT = mybir.ActivationFunctionType
F32 = mybir.dt.float32
F16 = mybir.dt.float16
BF16 = mybir.dt.bfloat16
I32 = mybir.dt.int32
AX_X = mybir.AxisListType.X
ds = bass.ds

P = 128
N = 2048
D = 512
F = 1024
E = 8
UNITS = E + 1
NT = N // P
DB = D // P
FB = F // P
EPS = 1e-5
QMIN = 1e-5

Z_GROUPS = [(0, 8, (0, 1, 2, 3, 4, 5, 6, 7)), (8, 4, (0, 1, 2, 3)), (12, 4, (0, 1, 4, 5))]
Y_GROUPS = [(0, 6), (6, 6), (12, 4)]
G0_COLS = Z_GROUPS[0][1] * P
REST = N - G0_COLS
UNROLL = 4
A_SCALE = 256.0
U_SCALE = 16.0
CHUNK = 1024
CHUNKS = UNITS * F * D // (P * CHUNK)
ROUNDS = 4
ROUND_STEPS = 2 * NT // ROUNDS
EARLY = 6
EARLY_W1 = 2
EARLY0 = CHUNKS - ROUNDS * EARLY
MACROS = 12
STEPS = len(Y_GROUPS) * NT // MACROS
IDLE = 8
MIXED = 4
ROUTED_TILES = N // P + E - 1
TILES = NT + ROUTED_TILES
BASE_W = D + 1
RING = 4
AHEAD = RING - 1
PAD = N


def build(nc, x, adj, adj_t, w1, w2, router_t, gamma, beta, out):
    with ExitStack() as ctx:
        def sb(name, shape, dt):
            return ctx.enter_context(nc.sbuf_tensor(name, shape, dt))

        def sem(name):
            return ctx.enter_context(nc.semaphore(name))

        x1_dram = nc.dram_tensor("x1_scratch", [N, D], F32, kind="Internal").ap()
        h_dram = nc.dram_tensor("h_scratch", [N + P, 2 * D], F16, kind="Internal").ap()
        base_dram = nc.dram_tensor("base_scratch", [N + P, BASE_W], F32, kind="Internal").ap()
        s2_dram = nc.dram_tensor("s2_scratch", [UNITS, D], F32, kind="Internal").ap()

        region = sb("region", [P, 2 * CHUNKS * CHUNK], F16)
        w1t = region[:, 0:CHUNKS * CHUNK]
        w2t = region[:, CHUNKS * CHUNK:2 * CHUNKS * CHUNK]
        o = 0
        HALF = REST // 2
        kept = region[:, o:o + 2 * NT * REST].rearrange("p (g h j n) -> p g h j n", g=2, h=2, j=NT); o += 2 * NT * REST
        u_hi = region[:, o:o + NT * D]; o += NT * D
        u_lo = region[:, o:o + NT * D]; o += NT * D
        a_in = region[:, o:o + 4 * 2 * N].bitcast(F32).rearrange("p (b n) -> p b n", b=4); o += 8 * N
        t_in = region[:, o:o + 2 * 2 * N].bitcast(F32).rearrange("p (b n) -> p b n", b=2)
        late1 = 24 * CHUNK
        xg_r = w1t[:, late1:late1 + 12 * CHUNK].bitcast(F32).rearrange("p (t d) -> p t d", d=D)

        zreg = sb("zreg", [P, 2 * NT * D], F16)
        xhat = zreg[:, :].bitcast(F32).rearrange("p (t d) -> p t d", t=NT)
        z_hi = zreg[:, 0:NT * D].rearrange("p (t d) -> p t d", t=NT)
        z_lo = zreg[:, NT * D:2 * NT * D].rearrange("p (t d) -> p t d", t=NT)
        zf = zreg[:, :].bitcast(F32)
        xg_z = zf[:, 0:4 * D].rearrange("p (t d) -> p t d", d=D)
        s2bc = zf[:, 7 * D:9 * D].rearrange("p (b d) -> p b d", b=2)
        o_t = zf[:, 9 * D:11 * D].rearrange("p (b d) -> p b d", b=2)
        base_t = zf[:, 11 * D:11 * D + 2 * BASE_W].rearrange("p (b d) -> p b d", b=2)

        work = sb("work", [P, 12288], F16)
        HL = Y_GROUPS[0][1] * P
        hl_z = work[:, 0:4 * G0_COLS].rearrange("p (b h n) -> p b h n", b=2, h=2)
        hl = work[:, 0:4 * HL].rearrange("p (b h n) -> p b h n", b=2, h=2)
        at = work[:, 4 * HL:8 * HL].bitcast(F32).rearrange("p (b n) -> p b n", b=2)
        raw = work[:, 6144:6144 + 4096].bitcast(F32).rearrange("p (b n) -> p b n", b=2)
        tern = work[:, 10240:12288].rearrange("p (b n) -> p b n", b=2)
        pre = work[:, 0:2048].bitcast(F32)
        h1 = work[:, 2048:4096].bitcast(F32)
        h1hl = work[:, 4096:8192].rearrange("p (b h n) -> p b h n", b=2, h=2)
        ht = [work[:, 8192:9216], work[:, 9216:10240], zf[:, 4 * D:5 * D].bitcast(F16), zf[:, 5 * D:6 * D].bitcast(F16)]
        hrow = work[:, 10240:12288].rearrange("p (b n) -> p b n", b=2)

        gb = sb("gb", [P, 2, D], F32)
        xb = sb("xb", [P, 2, D], F32)
        raw_early = [xb[:, :, :].rearrange("p b d -> p (b d)"), raw[:, 0, :], raw[:, 1, :]]
        hb = sb("hb", [P, 2, 2 * D], F16)
        ident = sb("ident", [P, P], F16)
        ident2 = sb("ident2", [P, P], F16)
        tri = sb("tri", [P, P], F16)
        ones = sb("ones", [P, P], F16)
        st4 = sb("st4", [P, UNROLL, 6], F32)
        mv4 = sb("mv4", [P, UNROLL, 2], F32)
        r4 = sb("r4", [P, 3, UNROLL], F32)
        stb = sb("stb", [P, 2, 6], F32)
        mvb = sb("mvb", [P, 2, 2], F32)
        rb = sb("rb", [P, 2, 2], F32)
        power = sb("power", [P, UNROLL], F32)
        junk = sb("junk", [P, D], F16)
        asum = sb("asum", [P, 2, 2], F32)
        rs = sb("rs", [P, 2, 2], F32)
        dv = sb("dv", [P, 2, 4], F32)
        dinv = sb("dinv", [P, NT], F32)
        dinvz = sb("dinvz", [P, NT], F32)
        thr = sb("thr", [P, 2, 2, 2], F32)
        s1 = sb("s1", [P, 2 * CHUNKS], F32)
        s2 = sb("s2", [P, CHUNKS], F32)
        rt = sb("rt", [P, DB, E], F32)
        r3 = sb("r3", [P, DB, 3, E], BF16)
        taken = [11 * D + 2 * BASE_W]

        def late(shape, dt=F32):
            n = 1
            for v in shape:
                n *= v
            words = n if dt != F16 else n // 2
            v = zf[:, taken[0]:taken[0] + words]
            taken[0] += words
            v = v.bitcast(dt) if dt != F32 else v
            return v.rearrange("p (a b) -> p a b", a=shape[0]) if len(shape) == 2 else v

        lg = late([NT, E])
        lg2 = late([2, E])
        mx = late([NT])
        ex = late([NT, E])
        se = late([NT])
        gate = late([NT])
        hot = late([NT, E])
        hot16 = late([NT + 1, E], F16)
        seen = late([NT, E])
        til = late([3, E])
        tili = late([2, E], I32)
        rank = late([NT, E])
        sel = late([NT, E])
        rr = late([3, NT])
        ri = late([3, NT], I32)
        lst = late([ROUTED_TILES], I32)
        tacc = late([ROUTED_TILES])[0:1, :]
        rtr = late([DB, E])
        zero_row = zf[:, 0:BASE_W]
        lane_hot = zf[:, 2 * D:4 * D].bitcast(F16).rearrange("p (t l) -> p t l", t=NT)
        taken[0] = 6 * D
        tile_tok = late([NT, ROUTED_TILES], F16)
        lane_no = late([P])
        tile_no = late([ROUTED_TILES])
        tok_pad = late([NT])
        assert taken[0] <= 7 * D
        idx = sb("idx", [P, 6], I32)
        unit = sb("unit", [1, TILES], I32)

        bank = [ctx.enter_context(nc.psum_tensor(f"bank{i}", [P, 512], F32)) for i in range(8)]
        acc = [bank[i][:, :] for i in range(8)]
        pst = [bank[6][:, :].bitcast(F16), bank[7][:, :].bitcast(F16)]
        ps_ht = bank[6][:, :].bitcast(F16)
        ps_h = [[bank[0], bank[1]], [bank[2], bank[3]]]
        ps_y = [bank[4], bank[5]]
        ps_r = bank[7]
        CNT0, LIST0 = 64, 256
        ps_cnt = bank[7][:, CNT0:CNT0 + (NT + 1) * E].rearrange("p (t e) -> p t e", e=E)
        ps_list = bank[7][:, LIST0:LIST0 + ROUTED_TILES]

        x_in = [sem("x_in0"), sem("x_in1")]
        small_in = sem("small_in")
        a_loaded = [sem(f"a_loaded{i}") for i in range(4)]
        t_loaded = [sem(f"t_loaded{i}") for i in range(2)]
        consts = sem("consts")
        const0 = sem("const0")
        tri_ok = sem("tri_ok")
        xh_seq = sem("xh_seq")
        xv_ok = sem("xv_ok")
        xr_ok = sem("xr_ok")
        sum_ok = sem("sum_ok")
        rest_ok = sem("rest_ok")
        shi_ok = sem("shi_ok")
        slo_ok = sem("slo_ok")
        deg_seq = sem("deg_seq")
        deg_ok = sem("deg_ok")
        deg_root = sem("deg_root")
        u_ok = sem("u_ok")
        p1_step = sem("p1_step")
        z_acc = sem("z_acc")
        zhi_ok = sem("zhi_ok")
        zlo_ok = sem("zlo_ok")
        at_loaded = [sem("at_loaded0"), sem("at_loaded1")]
        athi_ok = sem("athi_ok")
        atlo_ok = sem("atlo_ok")
        p2_step = sem("p2_step")
        raw_loaded = [sem("raw_loaded0"), sem("raw_loaded1")]
        early_loaded = [sem(f"early_loaded{i}") for i in range(3)]
        abs_ok = sem("abs_ok")
        w_seq = sem("w_seq")
        tern_ok = sem("tern_ok")
        tr_ok = sem("tr_ok")
        wt_ok = sem("wt_ok")
        xg_in = sem("xg_in")
        xz_in = [sem("xz_in0"), sem("xz_in1")]
        x1_ok = sem("x1_ok")
        x1_stored = sem("x1_stored")
        ln_seq = sem("ln_seq")
        ln_var = sem("ln_var")
        ln_root = sem("ln_root")
        ln_normed = sem("ln_normed")
        h_seq = sem("h_seq")
        h_ok = sem("h_ok")
        hhi_ok = sem("hhi_ok")
        hlo_ok = sem("hlo_ok")
        h_stored = [sem("h_stored0"), sem("h_stored1")]
        dinvz_ok = sem("dinvz_ok")
        s2_stored = sem("s2_stored")
        pads_stored = sem("pads_stored")
        hrow_in = [sem("hrow_in0"), sem("hrow_in1")]
        s2_in = [sem("s2_in0"), sem("s2_in1")]
        base_in = [sem("base_in0"), sem("base_in1")]
        hrow_got = [sem("hrow_got0"), sem("hrow_got1")]
        base_got = [sem("base_got0"), sem("base_got1")]
        out_stored = [sem("out_stored0"), sem("out_stored1")]
        tr2_ok = sem("tr2_ok")
        ht_ok = sem("ht_ok")
        m1_ok = sem("m1_ok")
        pre_ok = sem("pre_ok")
        h1_ok = sem("h1_ok")
        h1hi_ok = sem("h1hi_ok")
        h1lo_ok = sem("h1lo_ok")
        m2_ok = sem("m2_ok")
        y_seq = sem("y_seq")
        y_ok = sem("y_ok")
        y_stored = [sem("y_stored0"), sem("y_stored1")]
        r_ok = sem("r_ok")
        l_seq = sem("l_seq")
        l_ok = sem("l_ok")
        e_ok = sem("e_ok")
        r3_ok = sem("r3_ok")
        r_seq = sem("r_seq")
        hot_ok = sem("hot_ok")
        cnt_ok = sem("cnt_ok")
        rt_seq = sem("rt_seq")
        slots_ok = sem("slots_ok")
        unit_ok = sem("unit_ok")
        zero_ok = sem("zero_ok")
        pool_waits = sem("pool_waits")
        dve_waits = sem("dve_waits")
        idx_ok = [sem("idx_ok_h"), sem("idx_ok_base"), sem("idx_ok_out")]
        gate_ok = sem("gate_ok")
        gate_stored = sem("gate_stored")
        route_consts = sem("route_consts")
        list_ok = sem("list_ok")
        lst_ok = sem("lst_ok")

        adj_j = adj.rearrange("(j p) n -> j p n", p=P)
        adjt_j = adj_t.rearrange("(j p) n -> j p n", p=P)
        x_t = x.rearrange("(t p) d -> p t d", p=P)
        x1_t = x1_dram.rearrange("(t p) d -> p t d", p=P)
        w1_c = w1.rearrange("u (c b p) d -> (u c) p b d", b=2, p=P)
        w2_c = w2.rearrange("u (c p) f -> (u c) p f", p=P)

        DEG = 3
        XOPS = 3 * UNROLL + 1
        LN_OPS = 3
        WOPS = 3
        EARLY_CHUNKS = ROUNDS * EARLY + 2 * EARLY_W1

        def slot_count(n, b):
            return (n - b) * 8

        def early_count(rnd):
            return EARLY if rnd < 2 else EARLY + EARLY_W1

        def early(rnd, s):
            if isinstance(rnd, int) and rnd < 2:
                return EARLY * rnd + s, 2, EARLY0 + EARLY * rnd + s
            q = 2 * EARLY + (EARLY + EARLY_W1) * (rnd - 2) + s
            return (q, 1, EARLY_W1 * (rnd - 2) + s) if s < EARLY_W1 else (q, 2, EARLY0 + EARLY * rnd + s - EARLY_W1)

        def later(g, m, s):
            q = EARLY_CHUNKS + STEPS * m + s
            if s == STEPS - 1:
                return q, 2, m
            if isinstance(m, int) and m == MIXED and s == STEPS - 2:
                return q, 2, EARLY0 - 1
            before = m <= MIXED if isinstance(m, int) else g == 0
            return q, 1, (2 * EARLY_W1 if before else 2 * EARLY_W1 - 1) + (STEPS - 1) * m + s

        block = ctx.enter_context(nc.Block())

        @block.sync
        def _(sp):
            sp.dma_start(xhat[:, 0:UNROLL, :], x_t[:, 0:UNROLL, :]).then_inc(x_in[0], 16)

            def load_a(j, s, first):
                if not first:
                    sp.wait_ge(slo_ok, j - 3)
                sp.dma_start(a_in[:, s, :], adj_j[ds(j, 1), :, :].rearrange("a p n -> (a p) n")).then_inc(a_loaded[s], 16)
                if not (first and s < 2):
                    sp.wait_ge(sum_ok, j - 1)
                    sp.wait_ge(rest_ok, j - 1)
                sp.dma_start(t_in[:, s % 2, :], adjt_j[ds(j, 1), :, :].rearrange("a p n -> (a p) n")
                             ).then_inc(t_loaded[s % 2], 16)

            load_a(0, 0, True)
            def load_x(batch):
                sp.dma_start(xhat[:, ds(UNROLL * batch, UNROLL), :], x_t[:, ds(UNROLL * batch, UNROLL), :]
                             ).then_inc(x_in[1], 16)

            load_a(1, 1, True)
            load_x(1)
            for s in range(2, UNROLL):
                load_a(s, s, True)
            with sp.Fori(1, NT // UNROLL - 1) as i:
                for s in range(UNROLL):
                    load_a(UNROLL * i + s, s, False)
                    if s == 1:
                        load_x(i + 1)
            for s in range(UNROLL):
                load_a(NT - UNROLL + s, s, False)
            sp.dma_start(gb[:, 0, :], gamma.rearrange("(a d) -> a d", a=1).to_broadcast([P, D])).then_inc(small_in, 16)
            sp.dma_start(gb[:, 1, :], beta.rearrange("(a d) -> a d", a=1).to_broadcast([P, D])).then_inc(small_in, 16)
            sp.dma_start(rt[:, :, :], router_t.rearrange("(b p) e -> p b e", p=P)).then_inc(small_in, 16)

            def load_early(rnd, s):
                q, kind, c = early(rnd, s)
                if q >= 3:
                    sp.wait_ge(tern_ok, q - 2)
                if kind == 1:
                    sp.dma_start(raw_early[q % 3].rearrange("p (a d) -> p a d", a=2),
                                 w1_c[c, :, :, :]).then_inc(early_loaded[q % 3], 16)
                else:
                    sp.dma_start(raw_early[q % 3], w2_c[c, :, :]).then_inc(early_loaded[q % 3], 16)

            def load_w(chunk, b):
                q, kind, c = chunk
                sp.wait_ge(tern_ok, q - 1)
                if kind == 1:
                    sp.dma_start(raw[:, b, :].rearrange("p (a d) -> p a d", a=2),
                                 w1_c[ds(c, 1), :, :, :].rearrange("c p b d -> (c p) b d")).then_inc(raw_loaded[b], 16)
                else:
                    sp.dma_start(raw[:, b, :], w2_c[ds(c, 1), :, :].rearrange("c p f -> (c p) f")
                                 ).then_inc(raw_loaded[b], 16)

            for rnd in range(ROUNDS):
                for s in range(early_count(rnd)):
                    load_early(rnd, s)

            def macro(g, m, first):
                c0, nc_ = Y_GROUPS[g][0] * P, Y_GROUPS[g][1] * P
                for s in range(STEPS):
                    if not (first and s < 2):
                        sp.wait_ge(atlo_ok, STEPS * m + s - 1)
                    j = STEPS * (m - g * NT // STEPS) + s
                    sp.dma_start(at[:, s % 2, 0:nc_],
                                 adjt_j[ds(j, 1), :, c0:c0 + nc_].rearrange("a p n -> (a p) n")
                                 ).then_inc(at_loaded[s % 2], 16)
                    if not (isinstance(m, int) and m == IDLE):
                        load_w(later(g, m - (g == 2), s), s % 2)
                if g == 0:
                    if first:
                        sp.wait_ge(z_acc, 3)
                    sp.dma_start(xg_r[:, ds(3 * m, 3), :], x_t[:, ds(3 * m, 3), :]).then_inc(xg_in, 16)

            sp.wait_ge(z_acc, 1)
            for g in range(3):
                m0 = g * NT // STEPS
                macro(g, m0, g == 0)
                with sp.Fori(m0 + 1, m0 + NT // STEPS) as m:
                    macro(g, m, False)
            for b in range(2):
                sp.wait_ge(tern_ok, 2 * CHUNKS - 1 + b)
                sp.dma_start(raw[:, b, :].rearrange("p (t d) -> p t d", d=D), x_t[:, 12 + 2 * b:14 + 2 * b, :]
                             ).then_inc(xz_in[b], 16)

            def load_shared(n, b):
                sp.wait_ge(h_stored[b], slot_count(n, b) + 16)
                sp.dma_start(hrow[:, b, :], h_dram[ds(n * P, P), :]).then_inc(hrow_in[b], 16)

            def load_base(n, b):
                sp.dma_start(s2bc[:, b, :], s2_dram[0:1, :].to_broadcast([P, D])).then_inc(s2_in[b], 16)
                sp.dma_start(base_t[:, b, 0:D], x1_dram[ds(n * P, P), :]).then_inc(base_in[b], 16)

            sp.wait_ge(tr_ok, 2 * CHUNKS)
            for b in range(2):
                load_shared(b, b)
            sp.dma_start(s2_dram.rearrange("u (c p) -> p (u c)", p=P), s2[:, :],
                         allow_slow_non_contiguous=True).then_inc(s2_stored, 16)
            sp.wait_ge(s2_stored, 16)
            sp.wait_ge(x1_stored, 16 * NT // 2)
            for b in range(2):
                load_base(b, b)
            def next_shared(n, b):
                sp.wait_ge(tr2_ok, n - 1)
                load_shared(n, b)

            def next_base(n, b, i):
                sp.wait_ge(y_stored[b], 16 * i)
                load_base(n, b)

            for n in range(2, AHEAD + 3):
                next_shared(n, n % 2)
            with sp.Fori(1, (NT - AHEAD - 1) // 2) as i:
                for b in range(2):
                    next_shared(2 * i + b + AHEAD + 1, b)
                    next_base(2 * i + b, b, i)
            for n in range(NT - AHEAD - 1, NT):
                next_base(n, n % 2, n // 2)

            sp.wait_ge(unit_ok, 1)
            with sp.Fori(0, ROUTED_TILES // 2) as i:
                for b in range(2):
                    u = sp.value_load(unit[0:1, ds(NT + 2 * i + b, 1)], min_val=0, max_val=UNITS - 1)
                    sp.wait_ge(y_ok, NT - 1 + 2 * i + b)
                    sp.dma_start(s2bc[:, b, :], s2_dram[ds(u, 1), :].to_broadcast([P, D])).then_inc(s2_in[b], 16)
            u = sp.value_load(unit[0:1, TILES - 1:TILES], min_val=0, max_val=UNITS - 1)
            sp.wait_ge(y_ok, TILES - 2)
            sp.dma_start(s2bc[:, 0, :], s2_dram[ds(u, 1), :].to_broadcast([P, D])).then_inc(s2_in[0], 16)

        @block.gpsimd
        def _(pool):
            def pool_wait(s, value):
                pool.wait_ge(s, value)
                pool.sem_inc(pool_waits, 1)

            nc.gpsimd.memset(ident[:], 0.0).then_inc(const0, 1)
            nc.gpsimd.memset(ident2[:], 0.0).then_inc(const0, 1)
            nc.gpsimd.memset(ones[:], 1.0).then_inc(const0, 1)
            pool.wait_ge(const0, 3)
            nc.gpsimd.affine_select(out=ident[:], in_=ident[:], compare_op=ALU.not_equal, fill=1.0, base=0,
                                    pattern=[[-1, P]], channel_multiplier=1).then_inc(consts, 1)
            nc.gpsimd.affine_select(out=ident2[:], in_=ident2[:], compare_op=ALU.not_equal, fill=2.0 * A_SCALE,
                                    base=0, pattern=[[-1, P]], channel_multiplier=1).then_inc(consts, 1)
            nc.gpsimd.affine_select(out=tri[:], in_=ones[:], compare_op=ALU.is_gt, fill=0.0, base=0,
                                    pattern=[[1, P]], channel_multiplier=-1).then_inc(consts, 1)
            nc.gpsimd.memset(unit[:, 0:NT], 0).then_inc(consts, 1)
            nc.gpsimd.memset(power[:, :], -0.5).then_inc(consts, 1)
            pool.wait_ge(consts, 5)

            def x_root(batch):
                pool.wait_ge(xv_ok, batch + 1)
                nc.gpsimd.tensor_tensor(r4[:, 1, :], r4[:, 0, :], power[:, :], ALU.pow).then_inc(xr_ok, 1)

            def sum_rest(i, s):
                pool.wait_ge(a_loaded[s], 16 * i + 16)
                pool.wait_ge(t_loaded[s % 2], 32 * i + 16 * (s // 2) + 16)
                nc.gpsimd.tensor_tensor(a_in[:, s, G0_COLS:N], a_in[:, s, G0_COLS:N], t_in[:, s % 2, G0_COLS:N],
                                        ALU.add).then_inc(rest_ok, 1)

            def round_roots(i, last):
                for s in range(UNROLL):
                    if s < UNROLL - 1:
                        sum_rest(i, s + 1)
                    elif not last:
                        sum_rest(i + 1, 0)
                    pool.wait_ge(deg_ok, UNROLL * i + s + 1)
                    nc.gpsimd.tensor_tensor(dv[:, s % 2, 3:4], dv[:, s % 2, 2:3], power[:, 0:1],
                                            ALU.pow).then_inc(deg_root, 1)
                if not last:
                    x_root(i + 1)

            x_root(0)
            sum_rest(0, 0)
            with pool.Fori(0, NT // UNROLL - 1) as i:
                round_roots(i, False)
            round_roots(NT // UNROLL - 1, True)
            def norm_pair(t, alone=False):
                for r in range(2):
                    pool.wait_ge(ln_var, t + r + 1)
                    nc.gpsimd.tensor_tensor(rb[:, :, 1], rb[:, :, 0], power[:, 0:2], ALU.pow).then_inc(ln_root, 1)
                for b in range(2):
                    pool.wait_ge(ln_normed, t + b + 1)
                    nc.gpsimd.tensor_tensor(xb[:, b, :], xb[:, b, :], gb[:, 0, :], ALU.mult).then_inc(h_seq, 1)
                    pool.wait_ge(h_seq, t + b + 1)
                    nc.gpsimd.tensor_tensor(xb[:, b, :], xb[:, b, :], gb[:, 1, :], ALU.add).then_inc(h_ok, 1)
                for b in range(2):
                    if alone:
                        pool.wait_ge(h_ok, t + b + 1)
                        pool.wait_ge(h_stored[b], slot_count(t + b, b))
                        nc.gpsimd.tensor_copy(hb[:, b, 0:D], xb[:, b, :]).then_inc(hhi_ok, 1)
                    pool.wait_ge(hhi_ok, t + b + 1)
                    nc.gpsimd.tensor_tensor(hb[:, b, D:2 * D], xb[:, b, :], hb[:, b, 0:D],
                                            ALU.subtract).then_inc(hlo_ok, 1)
                for b in range(2):
                    pool_wait(hlo_ok, t + b + 1)
                    pool.dma_start(h_dram[ds((t + b) * P, P), :], hb[:, b, :]).then_inc(h_stored[b], 16)

            pool.wait_ge(small_in, 48)
            with pool.Fori(0, Y_GROUPS[2][0] // 2) as i:
                norm_pair(2 * i)
            norm_pair(12, True)
            norm_pair(14, True)

            pool.wait_ge(hlo_ok, NT)
            nc.gpsimd.iota(lane_no, pattern=[[1, P]], base=0, channel_multiplier=0,
                           allow_small_or_imprecise_dtypes=True).then_inc(route_consts, 1)
            nc.gpsimd.iota(tile_no, pattern=[[1, ROUTED_TILES]], base=0, channel_multiplier=0,
                           allow_small_or_imprecise_dtypes=True).then_inc(route_consts, 1)
            nc.gpsimd.iota(tok_pad, pattern=[[P, NT]], base=-PAD, channel_multiplier=1,
                           allow_small_or_imprecise_dtypes=True).then_inc(route_consts, 1)

            for b in range(2):
                pool.wait_ge(h_stored[b], 16 * NT // 2)
            pool.wait_ge(x1_stored, 16 * NT // 2)
            nc.gpsimd.memset(zero_row, 0.0).then_inc(zero_ok, 1)
            pool.wait_ge(zero_ok, 1)
            pool.dma_start(h_dram[N:N + P, :], zero_row[:, 0:D].bitcast(F16)).then_inc(pads_stored, 16)
            pool.dma_start(base_dram[N:N + P, :], zero_row).then_inc(pads_stored, 16)
            pool.wait_ge(pads_stored, 32)
            pool.wait_ge(lst_ok, 1)
            pool.wait_ge(tr2_ok, NT)

            def tokens(n, b, use):
                at_ = idx[:, 2 * use + b:2 * use + b + 1]
                nc.gpsimd.tensor_copy(at_, lst[:, ds(n - NT, 1)]).then_inc(idx_ok[use], 1)
                pool_wait(idx_ok[use], n - NT + 1)
                return bass.IndirectOffsetOnAxis(ap=at_, axis=0)

            def gather_h(n, b):
                pool.indirect_dma_start(out=hrow[:, b, :], out_offset=None, in_=h_dram,
                                        in_offset=tokens(n, b, 0)).then_inc(hrow_got[b], 16)

            def gather_base(n, b):
                pool.indirect_dma_start(out=base_t[:, b, :], out_offset=None, in_=base_dram,
                                        in_offset=tokens(n, b, 1)).then_inc(base_got[b], 16)

            def scatter(n, b):
                pool_wait(y_ok, n + 1)
                pool.indirect_dma_start(out=out, out_offset=tokens(n, b, 2), in_=o_t[:, b, :], in_offset=None,
                                        bounds_check=N - 1, oob_is_err=False).then_inc(out_stored[b], 16)

            def turn(n, b):
                pool_wait(tr2_ok, n + 2)
                gather_h(n + 3, 1 - b)
                scatter(n, b)
                gather_base(n + 2, b)

            for b in range(2):
                gather_h(NT + b, b)
            pool.wait_ge(gate_stored, 16)
            for b in range(2):
                pool_wait(y_stored[b], 16 * NT // 2)
            for b in range(2):
                gather_base(NT + b, b)
            pool_wait(tr2_ok, NT + 1)
            gather_h(NT + 2, 0)
            with pool.Fori(0, (ROUTED_TILES - 3) // 2) as i:
                for b in range(2):
                    turn(NT + 2 * i + b, b)
            scatter(TILES - 3, 0)
            gather_base(TILES - 1, 0)
            scatter(TILES - 2, 1)
            scatter(TILES - 1, 0)
            for b in range(2):
                pool.wait_ge(out_stored[b], 16 * ((ROUTED_TILES + 1 - b) // 2))

        @block.scalar
        def _(act):
            def split_s(j, b, first):
                act.wait_ge(sum_ok, j + 1)
                if not (first and j < 2):
                    act.wait_ge(p1_step, j - 1)
                    act.wait_ge(deg_ok, j - 1)
                nc.scalar.activation(hl_z[:, b % 2, 0, :], a_in[:, b, 0:G0_COLS], ACT.Copy, scale=A_SCALE,
                                     accum_out=rs[:, b % 2, 0:1]).then_inc(shi_ok, 1)
                act.wait_ge(rest_ok, j + 1)
                nc.scalar.activation(kept[:, :, 0, ds(j, 1), :].rearrange("p g j n -> p g (j n)"),
                                     a_in[:, b, G0_COLS:N].rearrange("p (g n) -> p g n", g=2), ACT.Copy, scale=A_SCALE,
                                     accum_out=rs[:, b % 2, 1:2]).then_inc(shi_ok, 1)

            for s in range(UNROLL):
                split_s(s, s, True)
            with act.Fori(1, NT // UNROLL) as i:
                for s in range(UNROLL):
                    split_s(UNROLL * i + s, s, False)

            def z_high(g):
                t0, count, banks = Z_GROUPS[g]
                act.wait_ge(z_acc, g + 1)
                for k in range(count):
                    nc.scalar.activation(z_hi[:, t0 + k, :], acc[banks[k]], ACT.Copy,
                                         scale=dinvz[:, t0 + k:t0 + k + 1]).then_inc(zhi_ok, 1)

            def sums(chunk, b, src, first=False):
                q, kind, c = chunk
                if not first:
                    act.wait_ge(tern_ok, q - 1)
                for a in range(2):
                    if not (isinstance(q, int) and q == 0 and a == 0):
                        act.wait_ge(abs_ok, 2 * q + a)
                    nc.scalar.activation(junk[:, :], src[:, a * D:(a + 1) * D], ACT.Abs,
                                         accum_out=asum[:, b, a:a + 1]).then_inc(abs_ok, 1)

            def store_w(chunk, b):
                q, kind, c = chunk
                act.wait_ge(tr_ok, q + 1)
                dst = w1t if kind == 1 else w2t
                nc.scalar.activation(dst[:, ds(c * CHUNK, CHUNK)], pst[b], ACT.Copy).then_inc(wt_ok, 1)

            act.wait_ge(dinvz_ok, 1)
            z_high(0)

            LAG = 3

            def early_round(rnd):
                for s in range(early_count(rnd)):
                    q = early(rnd, s)[0]
                    if q >= LAG:
                        store_w(early(rnd, s - LAG) if s >= LAG else early(rnd - 1, s - LAG + early_count(rnd - 1)),
                                (q - LAG) % 2)
                    act.wait_ge(early_loaded[q % 3], 16 * (q // 3) + 16)
                    sums(early(rnd, s), q % 2, raw_early[q % 3], q < 2)

            early_round(0)
            early_round(1)
            z_high(1)
            early_round(2)
            early_round(3)

            def high(g, J, b, first=False):
                nc_ = Y_GROUPS[g][1] * P
                act.wait_ge(at_loaded[b], 8 * (J - b) + 16)
                if not first:
                    act.wait_ge(p2_step, J - 1)
                nc.scalar.activation(hl[:, b, 0, 0:nc_], at[:, b, 0:nc_], ACT.Copy, scale=A_SCALE).then_inc(athi_ok, 1)

            def macro(g, m, first, norm_t=None, x1_from=None):
                high_step = 0 if g < 2 or x1_from is not None else 1
                for s in range(STEPS):
                    b = s % 2
                    if not (first and s < 2) and (s != 1 or x1_from is None):
                        high(g, STEPS * m + s, b)
                    past = g == 2 and not (isinstance(m, int) and m == IDLE)
                    mm = m - past
                    if s >= LAG:
                        if not (isinstance(m, int) and m == IDLE):
                            store_w(later(g, mm, s - LAG), (s - LAG) % 2)
                    elif first and s:
                        store_w(early(ROUNDS - 1, s - LAG + early_count(ROUNDS - 1)), (s - LAG) % 2)
                    elif not (first or isinstance(m, int) and m == IDLE + 1):
                        store_w(later(g, mm - 1, s - LAG + STEPS), (s - LAG) % 2)
                    if not (isinstance(m, int) and m == IDLE):
                        act.wait_ge(raw_loaded[b], 32 * mm + 16 * (s // 2) + 16)
                        sums(later(g, mm, s), b, raw[:, b, :])
                    if norm_t is not None and s == high_step:
                        for e in range(2):
                            h_high(norm_t + e, e)
                    if s == 0 and x1_from is not None:
                        high(g, STEPS * m + 1, 1)
                        store_x1(g - 1, x1_from)
            def h_high(t, b):
                act.wait_ge(h_ok, t + 1)
                if not (isinstance(t, int) and t < 2):
                    act.wait_ge(h_stored[b], slot_count(t, b))
                nc.scalar.activation(hb[:, b, 0:D], xb[:, b, :], ACT.Copy).then_inc(hhi_ok, 1)

            def store_x1(g, xg):
                t0, count = Y_GROUPS[g]
                for k in range(0, count, 2):
                    act.wait_ge(x1_ok, t0 + k + 2)
                    act.dma_start(x1_t[:, t0 + k:t0 + k + 2, :], xg[:, k:k + 2, :]).then_inc(x1_stored, 16)

            store_w(early(ROUNDS - 1, early_count(ROUNDS - 1) - LAG), (EARLY_CHUNKS - LAG) % 2)
            high(0, 0, 0, True)
            z_high(2)
            high(0, 1, 1, True)
            macro(0, 0, True)
            with act.Fori(1, 4) as m:
                macro(0, m, False)
            macro(1, 4, False, x1_from=xg_r[:, 0:6, :])
            act.wait_ge(x1_stored, 48)
            macro(1, 5, False)
            with act.Fori(6, 8) as m:
                macro(1, m, False, 2 * m - 12)
            macro(2, 8, False, 4, x1_from=xg_r[:, 6:12, :])
            act.wait_ge(x1_stored, 96)
            macro(2, 9, False, 6)
            with act.Fori(10, MACROS) as m:
                macro(2, m, False, 2 * m - 12)
            for s in range(STEPS - LAG, STEPS):
                store_w(later(2, MACROS - 2, s), s % 2)
            store_x1(2, xg_z)

            def columns(n, r, used):
                act.wait_ge(tr2_ok, n + 1)
                if used is not None:
                    act.wait_ge(m1_ok, used)
                nc.scalar.activation(ht[r], ps_ht, ACT.Copy).then_inc(ht_ok, 1)

            def tile(n, b, lead):
                for half in range(2):
                    act.wait_ge(pre_ok, 2 * n + half + 1)
                    if lead >= 1:
                        act.wait_ge(h1lo_ok, 2 * n + half - 1)
                    cols = slice(half * 512, half * 512 + 512)
                    nc.scalar.activation(h1[:, cols], pre[:, cols], ACT.Silu).then_inc(h1_ok, 1)
                    if lead >= 2:
                        act.wait_ge(m2_ok, n - 1)
                    act.wait_ge(h1_ok, 2 * n + half + 1)
                    nc.scalar.activation(h1hl[:, b, 0, cols], h1[:, cols], ACT.Copy, scale=U_SCALE).then_inc(h1hi_ok, 1)

            def shared_store(n, b):
                act.wait_ge(y_ok, n + 1)
                act.dma_start(base_dram[ds(n * P, P), 0:D], base_t[:, b, 0:D]).then_inc(y_stored[b], 16)

            def shared_tile(n, r, cols=()):
                for c in cols[:1]:
                    columns(*c)
                tile(n, r % 2, min(n, 2) if isinstance(n, int) else 2)
                if not (isinstance(n, int) and n == 0):
                    shared_store(n - 1, (r + 1) % 2)
                for c in cols[1:]:
                    columns(*c)

            columns(0, 0, None)
            shared_tile(0, 0, [(1, 1, None)])
            shared_tile(1, 1, [(2, 2, None), (3, 3, None)])
            shared_tile(2, 2, [(4, 0, 1), (5, 1, 2)])
            shared_tile(3, 3, [(6, 2, 3)])
            with act.Fori(1, NT // RING - 1) as i:
                for r in range(RING):
                    n = RING * i + r
                    shared_tile(n, r, [(n + AHEAD, (r + AHEAD) % RING, n + AHEAD - RING + 1)])
            shared_tile(NT - 4, 0, [(NT - 1, 3, NT - 4)])
            shared_tile(NT - 3, 1)
            act.wait_ge(l_ok, NT + 1)
            nc.scalar.activation(ex[:, :, :], lg[:, :, :], ACT.Exp).then_inc(e_ok, 1)
            shared_tile(NT - 2, 2)
            shared_tile(NT - 1, 3)
            columns(NT, 0, NT - 1)
            act.wait_ge(gate_ok, 1)
            act.dma_start(base_dram[0:N, D:D + 1].rearrange("(t p) a -> p (t a)", p=P), gate,
                          allow_slow_non_contiguous=True).then_inc(gate_stored, 16)
            shared_store(NT - 1, 1)
            with act.Fori(NT // 2, TILES // 2) as i:
                for b in range(2):
                    columns(2 * i + b + 1, 1 - b, 2 * i + b)
                    tile(2 * i + b, b, 2)
            tile(TILES - 1, 0, 2)

        @block.vector
        def _(dve):
            def chained(ins, s, value):
                ins.then_inc(s, 1)
                dve.wait_ge(s, value)

            dve.wait_ge(consts, 5)

            def x_stats(batch, s):
                t = UNROLL * batch + s
                chained(nc.vector.bn_stats(st4[:, s, :], xhat[:, ds(t, 1), :].rearrange("p a d -> p (a d)")),
                        xh_seq, XOPS * batch + 2 * s + 1)
                dve.sem_inc(dve_waits, 1)
                nc.vector.bn_aggr(mv4[:, s, :], st4[:, s, :]).then_inc(xh_seq, 1)

            def x_normed(batch):
                dve.wait_ge(xh_seq, XOPS * batch + 2 * UNROLL)
                nc.vector.tensor_scalar(r4[:, 0, :], mv4[:, :, 1], EPS, None, ALU.add).then_inc(xv_ok, 1)
                dve.wait_ge(xr_ok, batch + 1)
                chained(nc.vector.tensor_scalar(r4[:, 2, :], r4[:, 1, :], U_SCALE, None, ALU.mult),
                        xh_seq, XOPS * batch + 2 * UNROLL + 1)
                for s in range(UNROLL):
                    xs = xhat[:, ds(UNROLL * batch + s, 1), :].rearrange("p a d -> p (a d)")
                    nc.vector.tensor_scalar(xs, xs, mv4[:, s, 0:1], r4[:, 2, s:s + 1],
                                            ALU.subtract, ALU.mult).then_inc(xh_seq, 1)

            def sum_s(i, s):
                j = UNROLL * i + s
                dve.wait_ge(a_loaded[s], 16 * i + 16)
                dve.wait_ge(t_loaded[s % 2], 32 * i + 16 * (s // 2) + 16)
                nc.vector.tensor_tensor(a_in[:, s, 0:G0_COLS], a_in[:, s, 0:G0_COLS], t_in[:, s % 2, 0:G0_COLS],
                                        ALU.add).then_inc(sum_ok, 1)

            def finish(i, s):
                j = UNROLL * i + s
                b = s % 2
                raw_deg, deg, safe, root = [dv[:, b, k:k + 1] for k in range(4)]
                n = [0]

                def step(ins):
                    n[0] += 1
                    chained(ins, deg_seq, DEG * j + n[0])

                dve.wait_ge(shi_ok, 2 * j + 2)
                step(nc.vector.tensor_tensor(raw_deg, rs[:, b, 0:1], rs[:, b, 1:2], ALU.add))
                step(nc.vector.tensor_scalar(deg, raw_deg, 0.5 / A_SCALE, 1.0, ALU.mult, ALU.add))
                nc.vector.tensor_scalar(safe, deg, 1e-30, None, ALU.max).then_inc(deg_ok, 1)
                nc.vector.scalar_tensor_tensor(out=hl_z[:, b, 1, :], in0=a_in[:, s, 0:G0_COLS], scalar=A_SCALE,
                                               in1=hl_z[:, b, 0, :], op0=ALU.mult, op1=ALU.subtract)
                kept_j = [kept[:, :, h, ds(j, 1), :].rearrange("p g j n -> p g (j n)") for h in range(2)]
                nc.vector.scalar_tensor_tensor(out=kept_j[1], in0=a_in[:, s, G0_COLS:N].rearrange("p (g n) -> p g n", g=2),
                                               scalar=A_SCALE, in1=kept_j[0], op0=ALU.mult,
                                               op1=ALU.subtract).then_inc(slo_ok, 1)
                dve.wait_ge(deg_root, j + 1)
                step(nc.vector.scalar_tensor_tensor(out=dinv[:, ds(j, 1)], in0=deg, scalar=0.0, in1=root,
                                                    op0=ALU.is_gt, op1=ALU.mult))
                dve.wait_ge(xh_seq, XOPS * i + XOPS)
                xj = xhat[:, ds(j, 1), :].rearrange("p a d -> p (a d)")
                chained(nc.vector.tensor_scalar(u_hi[:, ds(j * D, D)], xj, dinv[:, ds(j, 1)], None, ALU.mult), u_ok, 2 * j + 1)
                nc.vector.scalar_tensor_tensor(out=u_lo[:, ds(j * D, D)], in0=xj, scalar=dinv[:, ds(j, 1)],
                                               in1=u_hi[:, ds(j * D, D)], op0=ALU.mult,
                                               op1=ALU.subtract).then_inc(u_ok, 1)

            def stream_round(i, first, last):
                for s in range(UNROLL):
                    if first and s == 0:
                        finish(i, s)
                    if s < UNROLL - 1:
                        sum_s(i, s + 1)
                    elif not last:
                        sum_s(i + 1, 0)
                    if not (first and s == 0):
                        finish(i, s)
                    if not last:
                        if s == 0:
                            dve.wait_ge(x_in[1], 16 * i + 16)
                        x_stats(i + 1, s)
                if not last:
                    x_normed(i + 1)

            dve.wait_ge(x_in[0], 16)
            for s in range(UNROLL):
                x_stats(0, s)
            x_normed(0)
            sum_s(0, 0)
            stream_round(0, True, False)
            with dve.Fori(1, NT // UNROLL - 1) as i:
                stream_round(i, False, False)
            stream_round(NT // UNROLL - 1, False, True)
            nc.vector.tensor_scalar(dinvz[:, :], dinv[:, :], 0.5 / A_SCALE, None, ALU.mult).then_inc(dinvz_ok, 1)

            def z_low(g):
                t0, count, banks = Z_GROUPS[g]
                dve.wait_ge(z_acc, g + 1)
                for k in range(count):
                    dve.wait_ge(zhi_ok, t0 + k + 1)
                    nc.vector.scalar_tensor_tensor(out=z_lo[:, t0 + k, :], in0=acc[banks[k]],
                                                   scalar=dinvz[:, t0 + k:t0 + k + 1], in1=z_hi[:, t0 + k, :],
                                                   op0=ALU.mult, op1=ALU.subtract).then_inc(zlo_ok, 1)

            def ternary(chunk, b, src, first=False):
                q, kind, c = chunk
                base, n = WOPS * q, 0
                dve.wait_ge(abs_ok, 2 * q + 2)
                if kind == 1:
                    k, width, scale, total = 2, D, s1[:, ds(2 * c, 2)], asum[:, b, 0:2]
                else:
                    k, width, scale, total = 1, F, s2[:, ds(c, 1)], thr[:, b, 0, 1:2]
                    nc.vector.tensor_scalar(total, asum[:, b, 0:1], asum[:, b, 1:2], None, ALU.add).then_inc(w_seq, 1)
                    n += 1
                    dve.wait_ge(w_seq, base + n)
                nc.vector.tensor_scalar(scale, total, 1.0 / width, QMIN, ALU.mult, ALU.max)
                nc.vector.tensor_scalar(thr[:, b, 1, 0:k], total, -0.5 / width, -0.5 * QMIN, ALU.mult, ALU.min)
                nc.vector.tensor_scalar(thr[:, b, 0, 0:k], total, 0.5 / width, 0.5 * QMIN, ALU.mult,
                                        ALU.max).then_inc(w_seq, 1)
                n += 1
                dve.wait_ge(w_seq, base + n)
                if not first:
                    dve.wait_ge(tr_ok, q - 1)
                for a in range(k):
                    cols = slice(a * width, (a + 1) * width)
                    nc.vector.tensor_scalar(tern[:, b, cols], src[:, cols], thr[:, b, 1, a:a + 1], None,
                                            ALU.is_lt).then_inc(w_seq, 1)
                for a in range(k):
                    n += 1
                    dve.wait_ge(w_seq, base + n)
                    cols = slice(a * width, (a + 1) * width)
                    ins = nc.vector.scalar_tensor_tensor(out=tern[:, b, cols], in0=src[:, cols],
                                                         scalar=thr[:, b, 0, a:a + 1], in1=tern[:, b, cols],
                                                         op0=ALU.is_gt, op1=ALU.subtract)
                assert n == WOPS
                ins.then_inc(tern_ok, 1)

            def early_round(rnd):
                for s in range(early_count(rnd)):
                    q = early(rnd, s)[0]
                    ternary(early(rnd, s), q % 2, raw_early[q % 3], q < 2)

            z_low(0)
            early_round(0)
            early_round(1)
            z_low(1)
            early_round(2)
            early_round(3)

            def norm_parts(part, t):
                if isinstance(t, int) and t >= 12:
                    x1 = [xg_z[:, t - 12 + b, :] for b in range(2)]
                else:
                    x1 = [xg_r[:, ds(t + b, 1), :].rearrange("p a d -> p (a d)") for b in range(2)]
                n = 5 * t + (4 if part == 1 else 0)
                src = x1
                if part == 0:
                    dve.wait_ge(x1_ok, t + 2)
                if part:
                    src = [xb[:, b, :] for b in range(2)]
                    dve.wait_ge(ln_root, t + part)
                    for b in range(2):
                        nc.vector.tensor_scalar(src[b], x1[b] if part == 1 else src[b], mvb[:, b, 0:1], rb[:, b, 1:2],
                                                ALU.subtract, ALU.mult).then_inc(ln_seq if part == 1 else ln_normed, 1)
                if part == 2:
                    return
                for b in range(2):
                    if part == 1:
                        dve.wait_ge(ln_seq, n + 1 + b)
                    nc.vector.bn_stats(stb[:, b, :], src[b]).then_inc(ln_seq, 1)
                n += 2 if part == 1 else 0
                for b in range(2):
                    dve.wait_ge(ln_seq, n + 1 + b)
                    dve.sem_inc(dve_waits, 1)
                    nc.vector.bn_aggr(mvb[:, b, :], stb[:, b, :]).then_inc(ln_seq, 1)
                dve.wait_ge(ln_seq, n + 4)
                nc.vector.tensor_scalar(rb[:, :, 0], mvb[:, :, 1], EPS, None, ALU.add).then_inc(ln_var, 1)

            def low(g, J, b):
                nc_ = Y_GROUPS[g][1] * P
                dve.wait_ge(athi_ok, J + 1)
                nc.vector.scalar_tensor_tensor(out=hl[:, b, 1, 0:nc_], in0=at[:, b, 0:nc_], scalar=A_SCALE,
                                               in1=hl[:, b, 0, 0:nc_], op0=ALU.mult, op1=ALU.subtract).then_inc(atlo_ok, 1)

            NORM_STEPS = {0: (), 1: (0, 1, 2), 2: (0, 2, 3)}

            def macro(g, m, norm_t=None, x1_from=None):
                for s in range(STEPS):
                    b = s % 2
                    if not (isinstance(m, int) and m == 0 and s < 2) and (s != 1 or x1_from is None):
                        low(g, STEPS * m + s, b)
                    if s == 0 and x1_from is not None:
                        x1_of_group(g - 1, x1_from)
                        low(g, STEPS * m + 1, 1)
                    if not (isinstance(m, int) and m == IDLE):
                        ternary(later(g, m - (g == 2), s), b, raw[:, b, :])
                    if norm_t is not None and s in NORM_STEPS[g]:
                        norm_parts(NORM_STEPS[g].index(s), norm_t)

            def x1_of_group(g, xg):
                t0, count = Y_GROUPS[g]
                x_rows = xg if g < 2 else raw[:, :, :].rearrange("p b (t d) -> p (b t) d", d=D)
                if g < 2:
                    dve.wait_ge(xg_in, 16 * Y_GROUPS[2][0] // 3)
                dve.wait_ge(p2_step, NT * (g + 1))
                for k in range(count):
                    if g == 2 and k % 2 == 0:
                        dve.wait_ge(xz_in[k // 2], 16)
                    nc.vector.scalar_tensor_tensor(out=xg[:, k, :], in0=acc[k], scalar=1.0 / (A_SCALE * U_SCALE),
                                                   in1=x_rows[:, k, :], op0=ALU.mult, op1=ALU.add).then_inc(x1_ok, 1)

            low(0, 0, 0)
            z_low(2)
            low(0, 1, 1)
            macro(0, 0)
            with dve.Fori(1, 4) as m:
                macro(0, m)
            macro(1, 4, x1_from=xg_r[:, 0:6, :])
            with dve.Fori(5, 8) as m:
                macro(1, m, 2 * m - 10)
            macro(2, 8, 6, x1_from=xg_r[:, 6:12, :])
            with dve.Fori(9, MACROS - 1) as m:
                macro(2, m, 2 * m - 10)
            macro(2, MACROS - 1)
            x1_of_group(2, xg_z)

            r_n = [0]

            def rstep(ins):
                r_n[0] += 1
                chained(ins, r_seq, r_n[0])

            dve.wait_ge(small_in, 48)
            rstep(nc.vector.tensor_copy(r3[:, :, 0, :], rt[:, :, :]))
            rstep(nc.vector.tensor_tensor(rtr[:, :, :], rt[:, :, :], r3[:, :, 0, :], ALU.subtract))
            rstep(nc.vector.tensor_copy(r3[:, :, 1, :], rtr[:, :, :]))
            rstep(nc.vector.tensor_tensor(rtr[:, :, :], rtr[:, :, :], r3[:, :, 1, :], ALU.subtract))
            nc.vector.tensor_copy(r3[:, :, 2, :], rtr[:, :, :]).then_inc(r3_ok, 1)

            LO = 4

            def tile(n, b, shared, lead, u, between=()):
                for half in range(2):
                    dve.wait_ge(m1_ok, n + 1)
                    if lead >= 1:
                        dve.wait_ge(h1_ok, 2 * n + half - 1)
                    nc.vector.tensor_tensor(
                        pre[:, half * 512:(half + 1) * 512].rearrange("p (f t) -> p f t", f=4),
                        ps_h[b][half][:, :].rearrange("p (f t) -> p f t", f=4),
                        s1[:, ds(u * FB + half * 4, 4)].rearrange("p (f a) -> p f a", a=1).to_broadcast([P, 4, P]),
                        ALU.mult).then_inc(pre_ok, 1)
                for work_, *args in between:
                    work_(*args)
                for half in range(2):
                    dve.wait_ge(h1hi_ok, 2 * n + half + 1)
                    cols = slice(half * 512, half * 512 + 512)
                    nc.vector.scalar_tensor_tensor(out=h1hl[:, b, 1, cols], in0=h1[:, cols], scalar=U_SCALE,
                                                   in1=h1hl[:, b, 0, cols], op0=ALU.mult,
                                                   op1=ALU.subtract).then_inc(h1lo_ok, 1)

            def route(n):
                k = [0]

                def step(ins):
                    k[0] += 1
                    chained(ins, l_seq, LO * n + k[0])

                row = lambda v: v[:, ds(n, 1), :].rearrange("p a e -> p (a e)")
                dve.wait_ge(r_ok, n + 1)
                part = [ps_r[:, k * E:(k + 1) * E] for k in range(3)]
                step(nc.vector.tensor_copy(lg2[:, 0, :], part[2]))
                step(nc.vector.tensor_tensor(lg2[:, 1, :], part[1], lg2[:, 0, :], ALU.add))
                step(nc.vector.tensor_tensor(row(lg), part[0], lg2[:, 1, :], ALU.add))
                step(nc.vector.tensor_reduce(mx[:, ds(n, 1)], row(lg), AX_X, ALU.max))
                nc.vector.tensor_scalar(row(hot), row(lg), mx[:, ds(n, 1)], None, ALU.is_equal).then_inc(l_ok, 1)

            def output(n, b, shared, lead):
                dve.wait_ge(m2_ok, n + 1)
                dve.wait_ge(s2_in[b], slot_count(n, b) + 16)
                if shared:
                    dve.wait_ge(base_in[b], slot_count(n, b) + 16)
                else:
                    dve.wait_ge(base_got[b], slot_count(n - NT, b) + 16)
                    if lead >= 2:
                        dve.wait_ge(out_stored[b], slot_count(n - NT, b))
                chained(nc.vector.scalar_tensor_tensor(out=s2bc[:, b, :], in0=ps_y[b][:, :], scalar=1.0 / U_SCALE,
                                                       in1=s2bc[:, b, :], op0=ALU.mult, op1=ALU.mult), y_seq, n + 1)
                if shared:
                    nc.vector.tensor_tensor(base_t[:, b, 0:D], base_t[:, b, 0:D], s2bc[:, b, :],
                                            ALU.add).then_inc(y_ok, 1)
                else:
                    nc.vector.scalar_tensor_tensor(out=o_t[:, b, :], in0=s2bc[:, b, :], scalar=base_t[:, b, D:D + 1],
                                                   in1=base_t[:, b, 0:D], op0=ALU.mult, op1=ALU.add).then_inc(y_ok, 1)

            def shared_tile(n, r, routes=(), between=()):
                lead = min(n, 2) if isinstance(n, int) else 2
                tile(n, r % 2, True, lead, 0, between)
                if not (isinstance(n, int) and n == 0):
                    output(n - 1, (r + 1) % 2, True, lead)
                for t in routes:
                    route(t)

            norm_parts(0, 12)
            norm_parts(1, 12)
            shared_tile(0, 0, [], [(norm_parts, 2, 12), (norm_parts, 0, 14)])
            shared_tile(1, 1, [1], [(route, 0)])
            shared_tile(2, 2, [3], [(route, 2)])
            shared_tile(3, 3, [5, 6], [(route, 4)])
            norm_parts(1, 14)
            norm_parts(2, 14)
            with dve.Fori(1, NT // RING - 1) as i:
                for r in range(RING):
                    n = RING * i + r
                    shared_tile(n, r, [n + AHEAD])
            shared_tile(NT - 4, 0, [NT - 1])

            q = [0]

            def rs_(ins):
                q[0] += 1
                chained(ins, rt_seq, q[0])

            dve.wait_ge(l_ok, NT)
            rs_(nc.vector.memset(rank[:, :, 0:1], 0.0))
            for e in range(1, E):
                rs_(nc.vector.tensor_tensor(rank[:, :, e:e + 1], rank[:, :, e - 1:e], hot[:, :, e - 1:e], ALU.max))
            rs_(nc.vector.tensor_tensor(seen[:, :, :], hot[:, :, :], rank[:, :, :], ALU.is_gt))
            rs_(nc.vector.memset(hot16[:, NT:NT + 1, :], 0.0))
            nc.vector.tensor_copy(hot16[:, 0:NT, :], seen[:, :, :]).then_inc(hot_ok, 1)
            nc.vector.tensor_tensor(lg[:, :, :], lg[:, :, :],
                                    mx.rearrange("p (t a) -> p t a", a=1).to_broadcast([P, NT, E]),
                                    ALU.subtract).then_inc(l_ok, 1)
            shared_tile(NT - 3, 1)

            dve.wait_ge(cnt_ok, 1)
            rs_(nc.vector.tensor_scalar(til[:, 0, :], ps_cnt[:, NT, :], float(P - 1), None, ALU.add))
            rs_(nc.vector.tensor_copy(tili[:, 0, :], til[:, 0, :]))
            rs_(nc.vector.tensor_scalar(tili[:, 1, :], tili[:, 0, :], 7, None, ALU.logical_shift_right))
            rs_(nc.vector.tensor_copy(til[:, 1, :], tili[:, 1, :]))
            rs_(nc.vector.memset(til[:, 2, 0:1], 0.0))
            for e in range(1, E):
                rs_(nc.vector.tensor_tensor(til[:, 2, e:e + 1], til[:, 2, e - 1:e], til[:, 1, e - 1:e], ALU.add))
            rs_(nc.vector.tensor_scalar(til[:, 0, :], til[:, 2, :], float(P), None, ALU.mult))
            rs_(nc.vector.tensor_tensor(sel[:, :, :], ps_cnt[:, 0:NT, :], til[:, 0:1, :].to_broadcast([P, NT, E]),
                                        ALU.add))
            rs_(nc.vector.tensor_tensor(sel[:, :, :], sel[:, :, :], seen[:, :, :], ALU.mult))
            rs_(nc.vector.tensor_reduce(rr[:, 0, :], sel[:, :, :], AX_X, ALU.add))
            rs_(nc.vector.tensor_copy(ri[:, 0, :], rr[:, 0, :]))
            rs_(nc.vector.tensor_scalar(ri[:, 1, :], ri[:, 0, :], P - 1, None, ALU.bitwise_and))
            rs_(nc.vector.tensor_scalar(ri[:, 2, :], ri[:, 0, :], 7, None, ALU.logical_shift_right))
            rs_(nc.vector.tensor_copy(rr[:, 1:3, :], ri[:, 1:3, :]))
            col = lambda k, width: rr[:, k, :].rearrange("p (t a) -> p t a", a=1).to_broadcast([P, NT, width])
            every = lambda v, width: v.rearrange("p (a l) -> p a l", a=1).to_broadcast([P, NT, width])
            dve.wait_ge(route_consts, 3)
            nc.vector.tensor_tensor(lane_hot, every(lane_no, P), col(1, P), ALU.is_equal).then_inc(slots_ok, 1)
            rs_(nc.vector.tensor_tensor(tile_tok, every(tile_no, ROUTED_TILES), col(2, ROUTED_TILES), ALU.is_equal))
            nc.vector.tensor_tensor(tile_tok, tile_tok,
                                    tok_pad.rearrange("p (t a) -> p t a", a=1).to_broadcast([P, NT, ROUTED_TILES]),
                                    ALU.mult).then_inc(slots_ok, 1)
            shared_tile(NT - 2, 2)

            dve.wait_ge(list_ok, 1)
            nc.vector.tensor_scalar(lst, ps_list, float(PAD), None, ALU.add).then_inc(lst_ok, 1)
            shared_tile(NT - 1, 3)
            dve.wait_ge(e_ok, 1)
            rs_(nc.vector.tensor_reduce(se, ex[:, :, :], AX_X, ALU.add))
            nc.vector.reciprocal(gate, se).then_inc(gate_ok, 1)
            rs_(nc.vector.memset(tacc, 0.0))
            for e in range(E):
                rs_(nc.vector.scalar_tensor_tensor(out=tacc, in0=tile_no[0:1, :], scalar=til[0:1, 2, e:e + 1],
                                                   in1=tacc, op0=ALU.is_ge, op1=ALU.add))
            nc.vector.tensor_copy(unit[:, NT:TILES], tacc).then_inc(unit_ok, 1)
            output(NT - 1, 1, True, 2)
            dve.wait_ge(unit_ok, 1)

            def load_unit(n):
                return dve.value_load(unit[0:1, ds(n, 1)], min_val=0, max_val=UNITS - 1)

            tile(NT, 0, False, 2, load_unit(NT))
            tile(NT + 1, 1, False, 2, load_unit(NT + 1))
            output(NT, 0, False, 0)
            tile(NT + 2, 0, False, 2, load_unit(NT + 2))
            output(NT + 1, 1, False, 1)
            with dve.Fori(NT // 2 + 1, TILES // 2 - 1) as i:
                tile(2 * i + 1, 1, False, 2, load_unit(2 * i + 1))
                output(2 * i, 0, False, 2)
                tile(2 * i + 2, 0, False, 2, load_unit(2 * i + 2))
                output(2 * i + 1, 1, False, 2)
            tile(TILES - 2, 1, False, 2, load_unit(TILES - 2))
            output(TILES - 3, 0, False, 2)
            tile(TILES - 1, 0, False, 2, load_unit(TILES - 1))
            output(TILES - 2, 1, False, 2)
            output(TILES - 1, 0, False, 2)

        @block.tensor
        def _(pe):
            def parts(dst, a_hi, a_lo, b_hi, b_lo, start):
                nc.tensor.matmul(dst, a_hi, b_hi, start=start, stop=False, skip_group_check=True)
                nc.tensor.matmul(dst, a_hi, b_lo, start=False, stop=False, skip_group_check=True)
                return nc.tensor.matmul(dst, a_lo, b_hi, start=False, stop=False, skip_group_check=True)

            def block_j(j, s, start):
                pe.wait_ge(u_ok, 2 * j + 2)
                for k in range(Z_GROUPS[0][1]):
                    c = slice(k * P, (k + 1) * P)
                    last = parts(acc[k], hl_z[:, s % 2, 0, c], hl_z[:, s % 2, 1, c], u_hi[:, ds(j * D, D)],
                                 u_lo[:, ds(j * D, D)], start)
                last.then_inc(p1_step, 1)

            pe.wait_ge(consts, 5)
            def add_identity(g, u, start, tiles=None, left=()):
                t0, count, banks = Z_GROUPS[g]
                for k in tiles or range(count):
                    t = t0 + k
                    if k < len(left):
                        pe.wait_ge(zlo_ok, left[k])
                    last = nc.tensor.matmul(acc[banks[k]], ident2[:, :], u[:, t * D:(t + 1) * D], start=start,
                                            stop=False, skip_group_check=True)
                return last

            def turn_w(chunk, b, first):
                q, kind, c = chunk
                pe.wait_ge(tern_ok, q + 1)
                if not first:
                    pe.wait_ge(wt_ok, q - 1)
                for k in range(8):
                    dst = (k % 4) * 2 + k // 4 if kind == 1 else k
                    last = nc.tensor.transpose(pst[b][:, dst * P:(dst + 1) * P], tern[:, b, k * P:(k + 1) * P], ident[:, :])
                last.then_inc(tr_ok, 1)

            assert Z_GROUPS[0][1] <= 2 * UNROLL
            for j in range(2 * UNROLL):
                block_j(j, j % UNROLL, j == 0)
            add_identity(0, u_hi, False)
            add_identity(0, u_lo, False, range(Z_GROUPS[0][1] - 1))
            with pe.Fori(2, NT // UNROLL) as i:
                for s in range(UNROLL):
                    block_j(UNROLL * i + s, s, False)
            add_identity(0, u_lo, False, (Z_GROUPS[0][1] - 1,)).then_inc(z_acc, 1)

            def early_round(g, rnd, first):
                t0, count, banks = Z_GROUPS[g]
                for k8 in range(ROUND_STEPS):
                    j = ROUND_STEPS * (rnd - 2 * (g - 1)) + k8
                    for k in range(count):
                        s_jk = [kept[:, g - 1, h, ds(j, 1), k * P:(k + 1) * P].rearrange("p j n -> p (j n)")
                                for h in range(2)]
                        parts(acc[banks[k]], *s_jk, u_hi[:, ds(j * D, D)], u_lo[:, ds(j * D, D)], False)
                    if k8 < (EARLY if g == 1 else EARLY + EARLY_W1) and not (first and k8 == 0):
                        if k8:
                            chunk = early(rnd, k8 - 1)
                        elif g == 1:
                            chunk = early(0, EARLY - 1)
                        else:
                            chunk = (2 * EARLY + (EARLY + EARLY_W1) * (rnd - 2) - 1, 2, None)
                        turn_w(chunk, (k8 - 1) % 2, first and k8 <= 2)

            add_identity(1, u_hi, True, left=(1, 2, 3, 4))
            early_round(1, 0, True)
            early_round(1, 1, False)
            add_identity(1, u_lo, False).then_inc(z_acc, 1)
            add_identity(2, u_hi, True, left=(9, 10))
            with pe.Fori(2, 4) as rnd:
                early_round(2, rnd, False)
            add_identity(2, u_lo, False).then_inc(z_acc, 1)

            def macro(g, m, first):
                t0, count = Y_GROUPS[g]
                for s in range(STEPS):
                    b = s % 2
                    late_turn = first and g == 1 and s == 1
                    idle = isinstance(m, int) and m == IDLE
                    if s and not (late_turn or idle):
                        turn_w(later(g, m - (g == 2), s - 1), (s - 1) % 2, False)
                    elif s == 0 and isinstance(m, int) and m == 0:
                        turn_w(early(ROUNDS - 1, early_count(ROUNDS - 1) - 1), 1, False)
                    elif s == 0 and not (isinstance(m, int) and m == IDLE + 1):
                        turn_w(later(g, m - 1 - (g == 2 and not idle), STEPS - 1), 1, False)
                    pe.wait_ge(atlo_ok, STEPS * m + s + 1)
                    j = STEPS * (m - g * NT // STEPS) + s
                    zj_hi = z_hi[:, ds(j, 1), :].rearrange("p a d -> p (a d)")
                    zj_lo = z_lo[:, ds(j, 1), :].rearrange("p a d -> p (a d)")
                    for k in range(count):
                        if first and s == 0 and g == 0 and k in Z_GROUPS[2][2]:
                            pe.wait_ge(zlo_ok, 13 + Z_GROUPS[2][2].index(k))
                        if first and s == 0 and g:
                            pe.wait_ge(x1_ok, Y_GROUPS[g - 1][0] + k + 1)
                        c = slice(k * P, (k + 1) * P)
                        last = parts(acc[k], hl[:, b, 0, c], hl[:, b, 1, c], zj_hi, zj_lo, first and s == 0)
                    last.then_inc(p2_step, 1)
                    if late_turn:
                        turn_w(later(g, m, 0), 0, False)

            for g in range(3):
                m0 = g * NT // STEPS
                macro(g, m0, True)
                if g == 2:
                    macro(g, IDLE + 1, False)
                with pe.Fori(m0 + 1 + (g == 2), m0 + NT // STEPS) as m:
                    macro(g, m, False)
            turn_w(later(2, MACROS - 2, STEPS - 1), 1, False)

            def rows_to_columns(n, b, shared):
                if shared:
                    pe.wait_ge(hrow_in[b], slot_count(n, b) + 16)
                else:
                    pe.wait_ge(hrow_got[b], slot_count(n - NT, b) + 16)
                if not (isinstance(n, int) and n == 0):
                    pe.wait_ge(ht_ok, n)
                for k in range(2 * DB):
                    last = nc.tensor.transpose(ps_ht[:, k * P:(k + 1) * P], hrow[:, b, k * P:(k + 1) * P], ident[:, :])
                last.then_inc(tr2_ok, 1)

            def first_product(n, r, lead, u):
                b = r % 2
                pe.wait_ge(ht_ok, n + 1)
                if lead >= 2:
                    pe.wait_ge(pre_ok, 2 * n - 2)
                for f in range(FB):
                    for d in range(DB):
                        w = w1t[:, ds(u * (4 * CHUNK) + (f // 2) * CHUNK + d * 2 * P + (f % 2) * P, P)]
                        for h in range(2):
                            c = (h * DB + d) * P
                            last = nc.tensor.matmul(ps_h[b][f // 4][:, (f % 4) * P:(f % 4 + 1) * P], w,
                                                    ht[r][:, c:c + P], start=(f % 4 == 0 and d == 0 and h == 0),
                                                    stop=False, skip_group_check=True)
                last.then_inc(m1_ok, 1)

            def logits(n, r):
                pe.wait_ge(ht_ok, n + 1)
                if not (isinstance(n, int) and n == 0):
                    pe.wait_ge(l_ok, n)
                for d in range(DB):
                    for h in range(2):
                        c = (h * DB + d) * P
                        last = nc.tensor.matmul(ps_r[:, 0:3 * E], ht[r][:, c:c + P],
                                                r3[:, d, :, :].rearrange("p a e -> p (a e)"),
                                                start=(d == 0 and h == 0), stop=False, skip_group_check=True)
                last.then_inc(r_ok, 1)

            def second_product(n, b, lead, u):
                pe.wait_ge(h1lo_ok, 2 * n + 2)
                if lead >= 2:
                    pe.wait_ge(y_ok, n - 1)
                for f in range(FB):
                    w = w2t[:, ds(u * (4 * CHUNK), 4 * CHUNK)].rearrange("p (d f c) -> p f d c", d=DB, f=FB)[:, f, :, :]
                    for h in range(2):
                        last = nc.tensor.matmul(ps_y[b][:, :].rearrange("p (d c) -> p d c", d=DB),
                                                h1hl[:, b, h, f * P:(f + 1) * P], w,
                                                start=(f == 0 and h == 0), stop=False, skip_group_check=True)
                last.then_inc(m2_ok, 1)

            pe.wait_ge(wt_ok, 2 * CHUNKS)

            def shared_first(n, r):
                first_product(n, r, min(n, 2) if isinstance(n, int) else 2, 0)

            def shared_second(n, r):
                second_product(n, r % 2, min(n, 2) if isinstance(n, int) else 2, 0)

            rows_to_columns(0, 0, True)
            pe.wait_ge(x1_ok, NT - 2)
            shared_first(0, 0)
            pe.wait_ge(r3_ok, 1)
            pe.wait_ge(x1_ok, NT)
            rows_to_columns(1, 1, True)
            for n in range(1, RING):
                shared_first(n, n)
                logits(2 * n - 2, (2 * n - 2) % RING)
                rows_to_columns(2 * n, 0, True)
                shared_second(n - 1, n - 1)
                logits(2 * n - 1, (2 * n - 1) % RING)
                if n < AHEAD:
                    rows_to_columns(2 * n + 1, 1, True)
            logits(2 * AHEAD, 2 * AHEAD % RING)
            with pe.Fori(1, NT // RING - 1) as i:
                for r in range(RING):
                    n = RING * i + r
                    shared_first(n, r)
                    rows_to_columns(n + AHEAD, (r + AHEAD) % 2, True)
                    shared_second(n - 1, (r + 3) % RING)
                    logits(n + AHEAD, (r + AHEAD) % RING)
            shared_first(NT - 4, 0)
            rows_to_columns(NT - 1, 1, True)
            shared_second(NT - 5, 3)
            logits(NT - 1, 3)

            shared_first(NT - 3, 1)
            pe.wait_ge(hot_ok, 1)
            hot_all = hot16.rearrange("p t e -> p (t e)")
            nc.tensor.matmul(ps_r[:, CNT0:CNT0 + (NT + 1) * E], tri[:, :], hot_all, start=True, stop=False,
                             skip_group_check=True)
            for t in range(1, NT + 1):
                last = nc.tensor.matmul(ps_r[:, CNT0 + t * E:CNT0 + (NT + 1) * E], ones[:, :],
                                        hot_all[:, 0:(NT + 1 - t) * E], start=False, stop=t == NT, skip_group_check=True)
            last.then_inc(cnt_ok, 1)
            shared_second(NT - 4, 0)

            shared_first(NT - 2, 2)
            shared_second(NT - 3, 1)
            pe.wait_ge(slots_ok, 2)
            for t in range(NT):
                last = nc.tensor.matmul(ps_list, lane_hot[:, t, :], tile_tok[:, t, :], start=t == 0, stop=t == NT - 1,
                                        skip_group_check=True)
            last.then_inc(list_ok, 1)
            shared_first(NT - 1, 3)
            shared_second(NT - 2, 2)
            rows_to_columns(NT, 0, False)
            shared_second(NT - 1, 3)
            pe.wait_ge(unit_ok, 1)

            def load_unit(n):
                return pe.value_load(unit[0:1, ds(n, 1)], min_val=0, max_val=UNITS - 1)

            def routed_turn(n, b):
                first_product(n, b, 2, load_unit(n))
                rows_to_columns(n + 1, 1 - b, False)
                second_product(n - 1, 1 - b, 2, load_unit(n - 1))

            first_product(NT, 0, 2, load_unit(NT))
            rows_to_columns(NT + 1, 1, False)
            routed_turn(NT + 1, 1)
            with pe.Fori(NT // 2 + 1, TILES // 2) as i:
                for b in range(2):
                    routed_turn(2 * i + b, b)
            first_product(TILES - 1, 0, 2, load_unit(TILES - 1))
            second_product(TILES - 2, 1, 2, load_unit(TILES - 2))
            second_product(TILES - 1, 0, 2, load_unit(TILES - 1))


def kernel(x, adj, L0_ffn_shared_w1, L0_ffn_shared_w2, L0_ffn_expert_w1, L0_ffn_expert_w2, L0_ffn_router_w,
           L0_ffn_ln_gamma, L0_ffn_ln_beta):
    import numpy as np
    import concourse.bacc as bacc
    from concourse.bass_utils import run_bass_kernel_spmd

    arrays = {
        "x": np.ascontiguousarray(x),
        "adj": np.ascontiguousarray(adj),
        "adj_t": np.ascontiguousarray(np.asarray(adj).T),
        "w1": np.concatenate([np.asarray(L0_ffn_shared_w1)[None], np.asarray(L0_ffn_expert_w1)]),
        "w2": np.concatenate([np.asarray(L0_ffn_shared_w2)[None], np.asarray(L0_ffn_expert_w2)]),
        "router_t": np.ascontiguousarray(np.asarray(L0_ffn_router_w).T),
        "gamma": np.ascontiguousarray(L0_ffn_ln_gamma),
        "beta": np.ascontiguousarray(L0_ffn_ln_beta),
    }
    nc = bacc.Bacc("TRN2", target_bir_lowering=False, num_devices=1, dynamic_dma_scratch_size=8192)
    args = [nc.dram_tensor(f"in_{k}", v.shape, mybir.dt.from_np(v.dtype), kind="ExternalInput").ap()
            for k, v in arrays.items()]
    out = nc.dram_tensor("out", (N, D), F32, kind="ExternalOutput").ap()
    build(nc, *args, out)
    r = run_bass_kernel_spmd(nc, [{f"in_{k}": v for k, v in arrays.items()}], core_ids=[0])
    return r.results[0]["out"]
```
